# Optimizing a Trainium2 kernel written in Bass

```python
import numpy as np
import jax
import jax.numpy as jnp

def _softmax(x, axis=-1):
    return jax.nn.softmax(x, axis=axis)

def _gelu(x):
    return jax.nn.gelu(x, approximate=True)

def _silu(x):
    return jax.nn.silu(x)

def _sigmoid(x):
    return jax.nn.sigmoid(x)

def _layernorm(x, axis=-1, eps=1e-05):
    m = jnp.mean(x, axis=axis, keepdims=True)
    v = jnp.var(x, axis=axis, keepdims=True)
    return (x - m) / jnp.sqrt(v + eps)

def _scatter_add(tgt, idx, src, axis=0):
    return tgt.at[idx].add(src)

def _segment_sum(src, seg, n):
    return jax.ops.segment_sum(src, seg, n)
kernel_name = 'mk_decoder_preln_d1_seqx_r4_d61a82'

def setup_inputs(seed: int=0):
    np.random.seed(seed)
    _w = jnp.asarray

    def _rec_inputs():
        import jax
        import jax.numpy as jnp
        _rk = jax.random.key(seed)
        x = -7.109e-05 + 0.9999 * jax.random.normal(jax.random.fold_in(_rk, 1), (8, 100, 256), jnp.float32)
        _lenS = 100 - jax.random.randint(jax.random.fold_in(_rk, 7), (8,), 0, max(1, 100 // 4) + 1, jnp.int32)
        _lenS2 = 361 - jax.random.randint(jax.random.fold_in(_rk, 8), (8,), 0, max(1, 361 // 4) + 1, jnp.int32)
        _ctx_768P = jax.random.normal(jax.random.fold_in(_rk, 11), (8, 16, 192), jnp.float32)
        _ctx_768c = jax.random.dirichlet(jax.random.fold_in(_rk, 511), 0.3 * jnp.ones((16,), jnp.float32), (8, 361))
        _ctx_768t = jnp.einsum('bsk,bkd->bsd', _ctx_768c, _ctx_768P)
        _ctx_768t = _ctx_768t * jax.lax.rsqrt(jnp.mean(jnp.square(_ctx_768t)) + 1e-12) * 0.953939
        ctx_768 = 0.000486113 + 1.00014 * (_ctx_768t + 0.3 * jax.random.normal(jax.random.fold_in(_rk, 611), (8, 361, 192), jnp.float32))
        return (x, ctx_768)
    x, ctx_768 = _rec_inputs()

    def _L0_attn_setup():
        import jax, jax.numpy as jnp
        import numpy as np
        B, S, D_IN, D_HID, D_OUT, PE_DIM = (4, 1024, 256, 256, 256, 16)
        R_MIN, R_MAX = (0.9, 0.999)

        def _pos_emb(batch_size, seq_len, dim):
            positions = jnp.arange(seq_len)[:, None]
            div_term = jnp.exp(jnp.arange(0, dim, 2) * (-jnp.log(10000.0) / dim))
            pe = jnp.zeros((seq_len, dim))
            pe = pe.at[:, 0::2].set(jnp.sin(positions * div_term))
            pe = pe.at[:, 1::2].set(jnp.cos(positions * div_term))
            return jnp.broadcast_to(pe, (batch_size, seq_len, dim)) / 10
        key = jax.random.key(seed)
        ks = jax.random.split(key, 12)
        d_feat = D_IN + PE_DIM
        x = jax.random.normal(ks[0], (B, S, D_IN), dtype=jnp.float32)
        u = jax.random.uniform(ks[1], (D_HID,), minval=R_MIN, maxval=R_MAX)
        a_logit = jnp.log(u) - jnp.log1p(-u)
        sc = 0.02
        W_dx = jax.random.normal(ks[2], (d_feat, D_OUT), dtype=jnp.float32) * sc
        b_dx = jnp.zeros((D_OUT,), dtype=jnp.float32)
        W_x = jax.random.normal(ks[3], (d_feat, D_HID), dtype=jnp.float32) * sc
        b_x = jnp.zeros((D_HID,), dtype=jnp.float32)
        W_gx = jax.random.normal(ks[4], (D_HID, D_HID), dtype=jnp.float32) * sc
        b_gx = jnp.zeros((D_HID,), dtype=jnp.float32)
        W_ga = jax.random.normal(ks[5], (D_HID, D_HID), dtype=jnp.float32) * sc
        b_ga = jnp.zeros((D_HID,), dtype=jnp.float32)
        W_o = jax.random.normal(ks[6], (D_HID, D_OUT), dtype=jnp.float32) * sc
        b_o = jnp.zeros((D_OUT,), dtype=jnp.float32)
        return {'x': x, 'a_logit': a_logit, 'W_dx': W_dx, 'b_dx': b_dx, 'W_x': W_x, 'b_x': b_x, 'W_gx': W_gx, 'b_gx': b_gx, 'W_ga': W_ga, 'b_ga': b_ga, 'W_o': W_o, 'b_o': b_o}
    _L0_attn_all = _L0_attn_setup()
    _L0_attn_in = {k: v for k, v in _L0_attn_all.items() if k in ('a_logit', 'W_dx', 'b_dx', 'W_x', 'b_x', 'W_gx', 'b_gx', 'W_ga', 'b_ga', 'W_o', 'b_o')}
    del _L0_attn_all

    def _L0_xattn_setup():
        import jax, jax.numpy as jnp
        import numpy as np
        N_HEADS = 8
        D_EMBED = 256
        D_CROSS = 192
        D_HEAD = D_EMBED // N_HEADS
        key = jax.random.key(seed)
        ks = jax.random.split(key, 10)
        B, Lq, Lkv = (16, 1024, 77)
        s_e = 1.0 / np.sqrt(D_EMBED)
        s_c = 1.0 / np.sqrt(D_CROSS)
        return {'x': jax.random.normal(ks[0], (B, Lq, D_EMBED), jnp.float32), 'y': jax.random.normal(ks[1], (B, Lkv, D_CROSS), jnp.float32), 'Wq': jax.random.normal(ks[2], (D_EMBED, D_EMBED), jnp.float32) * s_e, 'bq': jnp.zeros((D_EMBED,), jnp.float32), 'Wk': jax.random.normal(ks[3], (D_CROSS, D_EMBED), jnp.float32) * s_c, 'bk': jnp.zeros((D_EMBED,), jnp.float32), 'Wv': jax.random.normal(ks[4], (D_CROSS, D_EMBED), jnp.float32) * s_c, 'bv': jnp.zeros((D_EMBED,), jnp.float32), 'Wo': jax.random.normal(ks[5], (D_EMBED, D_EMBED), jnp.float32) * s_e, 'bo': jnp.zeros((D_EMBED,), jnp.float32)}
    _L0_xattn_all = _L0_xattn_setup()
    _L0_xattn_in = {k: v for k, v in _L0_xattn_all.items() if k in ('Wq', 'bq', 'Wk', 'bk', 'Wv', 'bv', 'Wo', 'bo')}
    del _L0_xattn_all

    def _L0_ffn_setup():
        import jax, jax.numpy as jnp
        import numpy as np
        E = 8
        K = 2
        CF = 1.2
        D = 256
        F = 1024
        B, S = (4, 256)
        key = jax.random.key(seed)
        ks = jax.random.split(key, 4)

        def init(k, shape, fan_in):
            return jax.random.normal(k, shape, jnp.float32) * (1.0 / np.sqrt(fan_in))
        return {'x': jax.random.normal(ks[0], (B, S, D), jnp.float32), 'Wg': init(ks[1], (D, E), D), 'bg': jnp.zeros((E,), jnp.float32), 'W1': init(ks[2], (E, D, F), D), 'b1': jnp.zeros((E, F), jnp.float32), 'W2': init(ks[3], (E, F, D), F), 'b2': jnp.zeros((E, D), jnp.float32)}
    _L0_ffn_all = _L0_ffn_setup()
    _L0_ffn_in = {k: v for k, v in _L0_ffn_all.items() if k in ('Wg', 'bg', 'W1', 'b1', 'W2', 'b2')}
    del _L0_ffn_all
    return {'x': x, 'ctx_768': ctx_768, 'L0_attn_a_logit': _L0_attn_in['a_logit'], 'L0_attn_W_dx': _L0_attn_in['W_dx'], 'L0_attn_b_dx': _L0_attn_in['b_dx'], 'L0_attn_W_x': _L0_attn_in['W_x'], 'L0_attn_b_x': _L0_attn_in['b_x'], 'L0_attn_W_gx': _L0_attn_in['W_gx'], 'L0_attn_b_gx': _L0_attn_in['b_gx'], 'L0_attn_W_ga': _L0_attn_in['W_ga'], 'L0_attn_b_ga': _L0_attn_in['b_ga'], 'L0_attn_W_o': _L0_attn_in['W_o'], 'L0_attn_b_o': _L0_attn_in['b_o'], 'L0_xattn_Wq': _L0_xattn_in['Wq'], 'L0_xattn_bq': _L0_xattn_in['bq'], 'L0_xattn_Wk': _L0_xattn_in['Wk'], 'L0_xattn_bk': _L0_xattn_in['bk'], 'L0_xattn_Wv': _L0_xattn_in['Wv'], 'L0_xattn_bv': _L0_xattn_in['bv'], 'L0_xattn_Wo': _L0_xattn_in['Wo'], 'L0_xattn_bo': _L0_xattn_in['bo'], 'L0_ffn_Wg': _L0_ffn_in['Wg'], 'L0_ffn_bg': _L0_ffn_in['bg'], 'L0_ffn_W1': _L0_ffn_in['W1'], 'L0_ffn_b1': _L0_ffn_in['b1'], 'L0_ffn_W2': _L0_ffn_in['W2'], 'L0_ffn_b2': _L0_ffn_in['b2']}

def reference(x, ctx_768, L0_attn_a_logit, L0_attn_W_dx, L0_attn_b_dx, L0_attn_W_x, L0_attn_b_x, L0_attn_W_gx, L0_attn_b_gx, L0_attn_W_ga, L0_attn_b_ga, L0_attn_W_o, L0_attn_b_o, L0_xattn_Wq, L0_xattn_bq, L0_xattn_Wk, L0_xattn_bk, L0_xattn_Wv, L0_xattn_bv, L0_xattn_Wo, L0_xattn_bo, L0_ffn_Wg, L0_ffn_bg, L0_ffn_W1, L0_ffn_b1, L0_ffn_W2, L0_ffn_b2):
    import jax
    import jax.numpy as jnp

    def _L0_attn_ref(x, a_logit, W_dx, b_dx, W_x, b_x, W_gx, b_gx, W_ga, b_ga, W_o, b_o):
        import jax, jax.numpy as jnp
        import numpy as np
        B, S, D_IN, D_HID, D_OUT, PE_DIM = (4, 1024, 256, 256, 256, 16)
        R_MIN, R_MAX = (0.9, 0.999)

        def _pos_emb(batch_size, seq_len, dim):
            positions = jnp.arange(seq_len)[:, None]
            div_term = jnp.exp(jnp.arange(0, dim, 2) * (-jnp.log(10000.0) / dim))
            pe = jnp.zeros((seq_len, dim))
            pe = pe.at[:, 0::2].set(jnp.sin(positions * div_term))
            pe = pe.at[:, 1::2].set(jnp.cos(positions * div_term))
            return jnp.broadcast_to(pe, (batch_size, seq_len, dim)) / 10
        batch_size, seq_len, _ = x.shape
        a_expit = jax.nn.sigmoid(a_logit)
        pe = _pos_emb(batch_size, seq_len, PE_DIM) / 10
        x = jnp.concatenate([x, pe], axis=-1)
        dx = x @ W_dx + b_dx
        xh = x @ W_x + b_x
        xh = jnp.sqrt(1 - a_expit ** 2) * xh
        gate_x = jax.nn.sigmoid(xh @ W_gx + b_gx)
        gate_a = jax.nn.sigmoid(xh @ W_ga + b_ga)
        a = gate_a * a_expit
        a_sq = a ** 2
        xg = gate_x * xh

        def step(h, inp):
            xi, ai, ai_sq = inp
            h = ai * h + jnp.sqrt(1 - ai_sq) * xi
            return (h, h)
        init = jnp.zeros((batch_size, xg.shape[-1]), dtype=xg.dtype)
        xs = (jnp.swapaxes(xg, 0, 1), jnp.swapaxes(a, 0, 1), jnp.swapaxes(a_sq, 0, 1))
        _, h = jax.lax.scan(step, init, xs)
        h = jnp.swapaxes(h, 0, 1)
        return (dx + h @ W_o + b_o) / 2

    def _L0_xattn_ref(x, y, Wq, bq, Wk, bk, Wv, bv, Wo, bo):
        import jax, jax.numpy as jnp
        import numpy as np
        N_HEADS = 8
        D_EMBED = 256
        D_CROSS = 192
        D_HEAD = D_EMBED // N_HEADS
        q = jnp.einsum('bqd,de->bqe', x, Wq) + bq
        k = jnp.einsum('bkc,ce->bke', y, Wk) + bk
        v = jnp.einsum('bkc,ce->bke', y, Wv) + bv
        scale = 1.0 / np.sqrt(D_HEAD)
        scores = jnp.einsum('bqe,bke->bqk', q, k) * scale
        attn = jax.nn.softmax(scores, axis=-1)
        out = jnp.einsum('bqk,bke->bqe', attn, v)
        return jnp.einsum('bqe,ef->bqf', out, Wo) + bo

    def _L0_ffn_ref(x, Wg, bg, W1, b1, W2, b2):
        import jax, jax.numpy as jnp
        import numpy as np
        E = 8
        K = 2
        CF = 1.2
        D = 256
        F = 1024
        B, S = (4, 256)
        Bx, Sx, Dx = x.shape
        T = Bx * Sx
        xt = x.reshape(T, Dx)
        logits = xt @ Wg + bg
        probs = jax.nn.softmax(logits, axis=-1)
        gate_vals, exp_idx = jax.lax.top_k(probs, K)
        gate_vals = gate_vals / jnp.sum(gate_vals, axis=-1, keepdims=True)
        capacity = int(np.ceil(CF * T * K / E))
        eidx = exp_idx.T.reshape(-1)
        gv = gate_vals.T.reshape(-1)
        oh = jax.nn.one_hot(eidx, E, dtype=jnp.int32)
        pos = jnp.sum((jnp.cumsum(oh, axis=0) - oh) * oh, axis=-1)
        keep = pos < capacity
        pos_c = jnp.where(keep, pos, capacity)
        xk = jnp.tile(xt, (K, 1))
        buf = jnp.zeros((E, capacity + 1, Dx), x.dtype)
        buf = buf.at[eidx, pos_c].add(jnp.where(keep[:, None], xk, 0.0))
        buf = buf[:, :capacity]
        h = jax.nn.gelu(jnp.einsum('ecd,edf->ecf', buf, W1) + b1[:, None, :], approximate=True)
        ye = jnp.einsum('ecf,efd->ecd', h, W2) + b2[:, None, :]
        ye = jnp.concatenate([ye, jnp.zeros((E, 1, Dx), ye.dtype)], axis=1)
        gathered = ye[eidx, pos_c] * (gv * keep.astype(gv.dtype))[:, None]
        out = jnp.sum(gathered.reshape(K, T, Dx), axis=0)
        return out.reshape(Bx, Sx, Dx)
    x = x + _L0_attn_ref(_layernorm(x, axis=-1), L0_attn_a_logit, L0_attn_W_dx, L0_attn_b_dx, L0_attn_W_x, L0_attn_b_x, L0_attn_W_gx, L0_attn_b_gx, L0_attn_W_ga, L0_attn_b_ga, L0_attn_W_o, L0_attn_b_o)
    x = x + _L0_xattn_ref(_layernorm(x, axis=-1), ctx_768, L0_xattn_Wq, L0_xattn_bq, L0_xattn_Wk, L0_xattn_bk, L0_xattn_Wv, L0_xattn_bv, L0_xattn_Wo, L0_xattn_bo)
    x = x + _L0_ffn_ref(_layernorm(x, axis=-1), L0_ffn_Wg, L0_ffn_bg, L0_ffn_W1, L0_ffn_b1, L0_ffn_W2, L0_ffn_b2)
    return x

_drawn_inputs = setup_inputs


def setup_inputs(seed=0):
    import zlib

    import numpy as np

    out = dict(_drawn_inputs(seed))
    spreads = {'L0_attn_b_dx': (0.0, 0.1),
     'L0_attn_b_x': (0.0, 2.0),
     'L0_attn_b_gx': (0.0, 2.0),
     'L0_attn_b_ga': (0.0, 2.0),
     'L0_attn_b_o': (0.0, 0.1),
     'L0_xattn_bq': (0.0, 0.1),
     'L0_xattn_bk': (0.0, 2.0),
     'L0_xattn_bv': (0.0, 0.1),
     'L0_xattn_bo': (0.0, 0.1),
     'L0_ffn_bg': (0.0, 0.1),
     'L0_ffn_b1': (0.0, 0.1),
     'L0_ffn_b2': (0.0, 0.1)}
    factors = {'L0_attn_a_logit': 30.312,
     'L0_attn_W_gx': 64.0,
     'L0_attn_W_ga': 64.0,
     'L0_attn_W_x': 8.0,
     'L0_attn_W_o': 8.0}
    for name, (base, spread) in spreads.items():
        noise = np.random.default_rng([zlib.crc32(name.encode()), seed]).standard_normal(out[name].shape)
        drawn = base * np.exp(spread * noise) if base else spread * noise
        out[name] = jnp.asarray(drawn.astype(out[name].dtype))
    for name, factor in factors.items():
        out[name] = (out[name] * factor).astype(out[name].dtype)
    return out
```

```python
from contextlib import ExitStack

import concourse.bass as bass
import numpy as np
from concourse import mybir

F32 = mybir.dt.float32
F32R = mybir.dt.float32r
U32 = mybir.dt.uint32
ALU = mybir.AluOpType
ACT = mybir.ActivationFunctionType
AX = mybir.AxisListType

B, S, D = 8, 100, 256
C, DC = 361, 192
E, F, TOPK = 8, 1024, 2
PE_DIM = 16
CAP = -(-12 * B * S * TOPK // (10 * E))
HD = 32
EPS = 1e-5
P = 128
KD, KF = D // P, F // P
T = B * S
NG, GB = 2, B // 2
GT = GB * S
NC = 3
CR = -(-C // NC)
CP = NC * CR
CE = C + 1
DA = DC + 1
DB = DA - P
HR = CAP // 2
NH = 2 * E
KB = TOPK * B
OUT_ROWS = T + CAP
RAW = 4
SCALE = 1.0 / float(np.sqrt(HD))

C_ID = 0
C_LM = C_ID + P
C_ONE = C_LM + S
C_MASK = C_ONE + P
C_EXP = C_MASK + P
C_TOK = C_EXP + P
C_ROW = C_TOK + KB
C_SPARE = C_ROW + HR
C_ALL = C_SPARE + NH

V_LOGIT, V_BGX, V_BGA, V_BQ, V_BV, V_B1 = 0, 2, 4, 6, 8, 10
V_ALL = V_B1 + E * KF

R_PE, R_WX, R_WDX, R_BO = 0, S, S + D, S + 2 * D
R_ALL = S + 3 * D

L_X, L_DX, L_GX, L_GA, L_O = range(5)
A_WQ, A_WK, A_WV, A_WO = 0, D, D + DA, D + DA + DC
A_ALL = A_WO + D


def layer_kernel(nc, x, consts, vectors, rows, w_lru, w_att, y_turned, y_rows, wg, bg, w1, w2, b2,
                 xn_dram, out):
    with ExitStack() as ctx, ExitStack() as front:
        def sb(name, shape, dt=F32, where=ctx):
            return where.enter_context(nc.sbuf_tensor(name, shape, dt))

        def sem(name):
            return ctx.enter_context(nc.semaphore(name))

        bank = [ctx.enter_context(nc.psum_tensor(f"bank{i}", [P, 512], F32)) for i in range(8)]

        cst = sb("cst", [P, C_ALL])
        vec = sb("vec", [P, V_ALL])
        x_sb = sb("x_sb", [S, B, D])
        xn_sb = sb("xn_sb", [S, B, D])
        xnT = sb("xnT", [P, KD, T])
        stats = sb("stats", [S, B, 6])
        mv = sb("mv", [S, B, 2])
        veps = sb("veps", [S, B])
        rstd = sb("rstd", [S, B])
        pw = sb("pw", [P, B])
        b2_sb = sb("b2_sb", [HR, E, D])
        bg_sb = sb("bg_sb", [S, E])
        raw = [sb(f"raw{i}", [P, KF * D]) for i in range(RAW)]
        w1_hi, w1_lo, w2_hi, w2_lo = ([None, None] for _ in range(4))

        def split_slot(i):
            w1_hi[i] = sb(f"w1_hi{i}", [P, KD, F], F32R)
            w1_lo[i] = sb(f"w1_lo{i}", [P, KD, F], F32R)
            w2_hi[i] = sb(f"w2_hi{i}", [P, KF, D], F32R)
            w2_lo[i] = sb(f"w2_lo{i}", [P, KF, D], F32R)

        split_slot(0)

        def fb(name, shape, dt=F32):
            return sb(name, shape, dt, front)

        rows_sb = fb("rows_sb", [PE_DIM + 2, R_ALL])
        wl = fb("wl", [P, 5, KD, D])
        wa = fb("wa", [P, KD, A_ALL])
        wg_sb = fb("wg_sb", [P, KD, E])
        yT = fb("yT", [P, 2, B * CE])
        yr = fb("yr", [CR, B * NC, DC])
        nlog = fb("nlog", [P, 2])
        ae = fb("ae", [P, 2])
        s_in = fb("s_in", [P, 2])
        half = fb("half", [P, 2])
        xtab = fb("xtab", [P, 2, S])
        dxtab = fb("dxtab", [S, D])
        xh = fb("xh", [P, 2, T])
        gx = fb("gx", [P, 2, T])
        ga = fb("ga", [P, 2, T])
        rt = fb("rt", [P, 2, T])
        bvb = fb("bvb", [P, KD, S])
        m_sb = fb("m_sb", [P, KD, DA])
        qb = fb("qb", [P, 2])
        qbs = fb("qbs", [P, 2])
        wvo = fb("wvo", [P, 2, D])
        brow = fb("brow", [S, D])
        qT = fb("qT", [P, 2, T])
        probs = fb("probs", [S, 2, CP])
        pT = fb("pT", [CR, 2, NC * S])
        zT = fb("zT", [P, 2, 2, S])
        nmax = fb("nmax", [S, B])
        psums = fb("psums", [S, B])
        rsum = fb("rsum", [S, B])
        front.close()

        split_slot(1)
        lg = sb("lg", [S, B, E])
        top = sb("top", [S, B, 8])
        topi = sb("topi", [S, B, 8], U32)
        dlog = sb("dlog", [S, B])
        e2 = sb("e2", [S, B])
        den = sb("den", [S, B])
        gate = sb("gate", [S, TOPK, B])
        chosen = sb("chosen", [S, KB])
        hot = sb("hot", [S, E, KB])
        cum = sb("cum", [S, E * KB])
        pos = sb("pos", [S, E * KB])
        kept = sb("kept", [S, E, KB])
        posk = sb("posk", [S, E, KB])
        own = sb("own", [S, KB])
        low = sb("low", [S, KB])
        ishi = sb("ishi", [S, KB])
        hoth = sb("hoth", [S, KB, E, 2])
        tokv = sb("tokv", [S, KB])
        rhs = sb("rhs", [S, KB, 2, NH])
        hotl = sb("hotl", [S, KB, HR])
        slot_gate = sb("slot_gate", [HR, NH])
        slot_tok = sb("slot_tok", [HR, NH])
        put_idx = sb("put_idx", [HR, NH], U32)
        get_idx = sb("get_idx", [HR, NH], U32)
        xe = sb("xe", [HR, 2, 2, D])
        xeT_hi = [sb(f"xeT_hi{i}", [P, KD, CAP], F32R) for i in range(2)]
        xeT_lo = [sb(f"xeT_lo{i}", [P, KD, CAP], F32R) for i in range(2)]
        hid = sb("hid", [P, KF, CAP])
        hid_hi = [sb(f"hid_hi{i}", [P, KF, CAP], F32R) for i in range(2)]
        hid_lo = [sb(f"hid_lo{i}", [P, KF, CAP], F32R) for i in range(2)]
        y_sb = sb("y_sb", [HR, 2, 2, D])

        ident = cst[:, C_ID:C_ID + P]
        ones = cst[:, C_ONE:C_ONE + P]

        ld_x = [sem(f"ld_x{g}") for g in range(NG)]
        ld_small, ld_rows, ld_lru, ld_att, ld_yT, ld_yr, ld_moe = (
            sem(n) for n in ("ld_small", "ld_rows", "ld_lru", "ld_att", "ld_yT", "ld_yr", "ld_moe"))
        ld_raw = [sem(f"ld_raw{i}") for i in range(RAW)]
        st_xn, st_out = sem("st_xn"), sem("st_out")
        v_chain, a_chain, p_chain = sem("v_chain"), sem("a_chain"), sem("p_chain")
        var_ready, rstd_ready, xn_ready = sem("var_ready"), sem("rstd_ready"), sem("xn_ready")
        nlog_ready, elog_ready, ae_ready, sin_ready = (
            sem(n) for n in ("nlog_ready", "elog_ready", "ae_ready", "sin_ready"))
        pe_tabs, tabs_ready, xt_ready = sem("pe_tabs"), sem("tabs_ready"), sem("xt_ready")
        bvb_ready = sem("bvb_ready")
        pe_turn, turn0_ready, turn1_ready = sem("pe_turn"), sem("turn0_ready"), sem("turn1_ready")
        pe_xh, xh_ready = sem("pe_xh"), sem("xh_ready")
        pe_setup, setup_ready = sem("pe_setup"), sem("setup_ready")
        pe_gate, gate_ready, sq_ready, rt_ready = (
            sem(n) for n in ("pe_gate", "gate_ready", "sq_ready", "rt_ready"))
        gxh_ready, h_ready = sem("gxh_ready"), sem("h_ready")
        pe_x2, x2_ready, xb_ready = sem("pe_x2"), sem("x2_ready"), sem("xb_ready")
        pe_q, q0_ready, q1_ready = sem("pe_q"), sem("q0_ready"), sem("q1_ready")
        pad_ready = sem("pad_ready")
        pe_score, nmax_ready, probs_ready = sem("pe_score"), sem("nmax_ready"), sem("probs_ready")
        pe_pT, pT_ready, pe_z, z_ready = sem("pe_pT"), sem("pT_ready"), sem("pe_z"), sem("z_ready")
        pe_x3, x3_ready = sem("pe_x3"), sem("x3_ready")
        pe_logits, dlog_ready, e2_ready = sem("pe_logits"), sem("dlog_ready"), sem("e2_ready")
        hot_ready, pe_count, map_ready, pe_map = (
            sem(n) for n in ("hot_ready", "pe_count", "map_ready", "pe_map"))
        idx_ready = sem("idx_ready")
        w_hi, w_lo = sem("w_hi"), sem("w_lo")
        got = [sem(f"got{i}") for i in range(2)]
        put = sem("put")
        pe_xeT, xe_hi, xe_lo = sem("pe_xeT"), sem("xe_hi"), sem("xe_lo")
        pe_hid, hid_ready, hid_hi_ready, hid_lo_ready = (
            sem(n) for n in ("pe_hid", "hid_ready", "hid_hi_ready", "hid_lo_ready"))
        pe_y, y_ready = sem("pe_y"), sem("y_ready")

        block = ctx.enter_context(nc.Block())

        def tok(g):
            return slice(g * GT, (g + 1) * GT)

        def row_tok(b):
            return slice(b * S, (b + 1) * S)

        def raw_load(eng, u):
            if u >= RAW:
                eng.wait_ge(w_hi, u - RAW + 1)
                eng.wait_ge(w_lo, u - RAW + 1)
            src = (w1 if u % 2 == 0 else w2)[u // 2]
            eng.dma_start(raw[u % RAW][:, :], src).then_inc(ld_raw[u % RAW], 16)

        def split_of(u):
            hi, lo = ((w1_hi, w1_lo), (w2_hi, w2_lo))[u % 2]
            s = (u // 2) % 2
            flat = "p a b -> p (a b)"
            return hi[s][:, :, :].rearrange(flat), lo[s][:, :, :].rearrange(flat)

        @block.sync
        def _(sp):
            sp.dma_start(x_sb[:, 0:GB, :], x[:, 0:GB, :]).then_inc(ld_x[0], 16)
            sp.dma_start(cst[:, :], consts).then_inc(ld_small, 16)
            sp.dma_start(x_sb[:, GB:B, :], x[:, GB:B, :]).then_inc(ld_x[1], 16)
            sp.dma_start(wl[:, L_GX:, :, :], w_lru[:, L_GX:, :, :]).then_inc(ld_lru, 16)
            sp.dma_start(wa[:, :, :], w_att).then_inc(ld_att, 16)
            sp.dma_start(yT[:, :, :], y_turned).then_inc(ld_yT, 16)
            sp.dma_start(yr[:, :, :], y_rows).then_inc(ld_yr, 16)
            sp.dma_start(wg_sb[:, :, :], wg).then_inc(ld_moe, 16)
            sp.dma_start(bg_sb[:, :], bg.to_broadcast([S, E])).then_inc(ld_moe, 16)
            sp.dma_start(b2_sb[:, :, :], b2.unsqueeze(0).to_broadcast([HR, E, D])).then_inc(ld_moe, 16)
            for u in range(RAW):
                raw_load(sp, u)
            sp.wait_ge(ld_moe, 48)
            sp.dma_start(out[T:OUT_ROWS, :].rearrange("(a p) d -> p a d", p=HR),
                         b2_sb[:, 0:2, :]).then_inc(st_out, 16)
            raw_load(sp, RAW)
            raw_load(sp, RAW + 1)
            for g in range(NG):
                bs = slice(g * GB, (g + 1) * GB)
                sp.wait_ge(x3_ready, (g + 1) * GB)
                sp.dma_start(out[tok(g), :].rearrange("(b t) d -> t b d", t=S),
                             x_sb[:, bs, :]).then_inc(st_out, 16)
                sp.wait_ge(xn_ready, 2 * B + (g + 1) * GB)
                sp.dma_start(xn_dram[tok(g), :].rearrange("(b t) d -> t b d", t=S),
                             xn_sb[:, bs, :]).then_inc(st_xn, 16)
            for u in range(RAW + 2, 2 * E):
                raw_load(sp, u)
            sp.wait_ge(st_out, 48)
            sp.wait_ge(st_xn, 32)

        @block.gpsimd
        def _(pool):
            links = [0]

            def link(ins):
                links[0] += 1
                ins.then_inc(p_chain, 1)
                pool.wait_ge(p_chain, links[0])

            def rstd_pair(n):
                pr = slice(2 * (n % 4), 2 * (n % 4) + 2)
                pool.wait_ge(var_ready, n + 1)
                link(pool.tensor_scalar(veps[:, pr], mv[:, pr, 1], EPS, None, ALU.add))
                pool.tensor_tensor(rstd[:, pr], veps[:, pr], pw[0:S, 0:2], ALU.pow).then_inc(rstd_ready, 1)

            pool.memset(probs[:, :, C:CP], 0.0).then_inc(pad_ready, 1)
            link(pool.memset(half[:, :], 0.5))
            link(pool.memset(pw[:, :], -0.5))
            for n in range(4):
                rstd_pair(n)
            pool.wait_ge(ld_small, 32)
            pool.tensor_scalar(nlog[:, :], vec[:, V_LOGIT:V_LOGIT + 2], -1.0, 80.0,
                               ALU.mult, ALU.min).then_inc(nlog_ready, 1)
            pool.wait_ge(ae_ready, 1)
            link(pool.tensor_tensor(s_in[:, :], ae[:, :], ae[:, :], ALU.mult))
            link(pool.tensor_scalar(s_in[:, :], s_in[:, :], -1.0, 1.0, ALU.mult, ALU.add))
            pool.tensor_tensor(s_in[:, :], s_in[:, :], half[:, :], ALU.pow).then_inc(sin_ready, 1)
            pool.wait_ge(tabs_ready, 3)
            for g in range(NG):
                bs = slice(g * GB, (g + 1) * GB)
                pool.wait_ge(xn_ready, (g + 1) * GB)
                pool.tensor_tensor(x_sb[:, bs, :], x_sb[:, bs, :],
                                   dxtab[:, :].unsqueeze(1).to_broadcast([S, GB, D]),
                                   ALU.add).then_inc(xt_ready, 1)
            for g in range(NG):
                for m in range(2):
                    pool.wait_ge(gate_ready, 4 * g + 2 * m + 2)
                    pool.wait_ge(xh_ready, 2 * g + m + 1)
                    pool.tensor_tensor(gx[:, m, tok(g)], gx[:, m, tok(g)], xh[:, m, tok(g)],
                                       ALU.mult).then_inc(gxh_ready, 1)
            for g in range(NG):
                for n in range(2):
                    rstd_pair(4 + 2 * g + n)
                bs = slice(g * GB, (g + 1) * GB)
                pool.wait_ge(xn_ready, B + (g + 1) * GB)
                pool.wait_ge(setup_ready, 5)
                pool.tensor_tensor(x_sb[:, bs, :], x_sb[:, bs, :],
                                   brow[:, :].unsqueeze(1).to_broadcast([S, GB, D]),
                                   ALU.add).then_inc(xb_ready, 1)
            for n in range(4):
                rstd_pair(8 + n)

            def gather(e):
                if e >= 2:
                    pool.wait_ge(pe_xeT, e - 1)
                for j in range(2):
                    h = 2 * e + j
                    pool.indirect_dma_start(
                        xe[:, e % 2, j, :], None, xn_dram,
                        bass.IndirectOffsetOnAxis(ap=get_idx[:, h:h + 1], axis=0),
                        bounds_check=T - 1, oob_is_err=False).then_inc(got[e % 2], 16)

            def scatter_add(e):
                pool.wait_ge(put, 32 * e) if e else pool.wait_ge(st_out, 48)
                for j in range(2):
                    h = 2 * e + j
                    pool.wait_ge(y_ready, h + 1)
                    pool.indirect_dma_start(
                        out, bass.IndirectOffsetOnAxis(ap=put_idx[:, h:h + 1], axis=0),
                        y_sb[:, e % 2, j, :], None,
                        bounds_check=OUT_ROWS - 1, oob_is_err=True,
                        compute_op=ALU.add).then_inc(put, 16)

            pool.wait_ge(idx_ready, 2)
            pool.wait_ge(st_xn, 32)
            gather(0)
            gather(1)
            gather(2)
            for e in range(E):
                if e + 3 < E:
                    gather(e + 3)
                scatter_add(e)
            pool.wait_ge(put, 32 * E)

        @block.scalar
        def _(act):
            links = [0]

            def link(ins):
                links[0] += 1
                ins.then_inc(a_chain, 1)
                act.wait_ge(a_chain, links[0])

            def turn_evac(n, src):
                act.wait_ge(pe_turn, 2 * n + 2)
                act.activation(xnT[:, 1, tok(n % 2)], src[:, 0:GT], ACT.Copy).then_inc(turn1_ready, 1)

            def w_high(u):
                act.wait_ge(ld_raw[u % RAW], 16 * (u // RAW + 1))
                if u >= 4:
                    act.wait_ge(pe_hid if u % 2 == 0 else pe_y,
                                (4 if u % 2 == 0 else 2) * (u // 2 - 1))
                act.activation(split_of(u)[0], raw[u % RAW][:, :], ACT.Copy).then_inc(w_hi, 1)

            act.dma_start(rows_sb[:, :], rows).then_inc(ld_rows, 16)
            act.dma_start(vec[:, :], vectors).then_inc(ld_small, 16)
            act.dma_start(wl[:, 0:L_GX, :, :], w_lru[:, 0:L_GX, :, :]).then_inc(ld_lru, 16)
            act.wait_ge(nlog_ready, 1)
            act.activation(nlog[:, :], nlog[:, :], ACT.Exp).then_inc(elog_ready, 1)
            turn_evac(0, bank[1])
            turn_evac(1, bank[1])
            act.wait_ge(pe_setup, 1)
            act.activation(m_sb[:, :, :], bank[6][:, 0:KD * DA], ACT.Copy)
            act.activation(qb[:, 0:1], bank[6][:, 400:401], ACT.Copy)
            act.activation(qb[0:DB, 1:2], bank[6][0:DB, 401:402], ACT.Copy)
            act.activation(qbs[:, 0:1], bank[6][:, 400:401], ACT.Copy, scale=SCALE)
            act.activation(qbs[0:DB, 1:2], bank[6][0:DB, 401:402], ACT.Copy, scale=SCALE).then_inc(setup_ready, 1)
            act.wait_ge(pe_setup, 2)
            act.activation(wvo[:, 0, :], bank[7][:, 0:D], ACT.Copy).then_inc(setup_ready, 1)
            act.activation(wvo[0:DC - P, 1, :], bank[7][0:DC - P, D:2 * D], ACT.Copy).then_inc(setup_ready, 1)
            act.wait_ge(pe_setup, 3)
            act.activation(brow[:, :], bank[0][0:S, 0:D], ACT.Copy).then_inc(setup_ready, 2)

            for g in range(NG):
                for m in range(2):
                    j = 4 * g + 2 * m
                    act.wait_ge(pe_gate, j + 1)
                    act.activation(ga[:, m, tok(g)], bank[j % 4][:, 0:GT], ACT.Sigmoid,
                                   bias=vec[:, V_BGA + m:V_BGA + m + 1]).then_inc(gate_ready, 1)
                    act.wait_ge(pe_gate, j + 2)
                    act.activation(gx[:, m, tok(g)], bank[(j + 1) % 4][:, 0:GT], ACT.Sigmoid,
                                   bias=vec[:, V_BGX + m:V_BGX + m + 1]).then_inc(gate_ready, 1)
                    act.wait_ge(gate_ready, j + 1)
                    act.activation(rt[:, m, tok(g)], ga[:, m, tok(g)], ACT.Square,
                                   scale=ae[:, m:m + 1]).then_inc(sq_ready, 1)
            for n in range(4):
                act.wait_ge(sq_ready, n + 1)
                act.activation(rt[:, n % 2, tok(n // 2)], rt[:, n % 2, tok(n // 2)], ACT.Sqrt,
                               bias=1.0, scale=-1.0).then_inc(rt_ready, 1)
            w_high(0)
            w_high(1)
            for g in range(NG):
                turn_evac(2 + g, bank[1])
                act.wait_ge(pe_q, 2 * g + 2)
                act.activation(qT[0:DB, 1, tok(g)], bank[3][0:DB, 0:GT], ACT.Identity,
                               bias=qbs[0:DB, 1:2], scale=SCALE).then_inc(q1_ready, 1)
            act.wait_ge(pad_ready, 1)
            for b in range(B):
                act.wait_ge(nmax_ready, b + 1)
                if b >= 2:
                    act.wait_ge(pe_pT, b - 1)
                act.activation(probs[:, b % 2, 0:C], bank[4 + b % 2][0:S, 0:C], ACT.Exp,
                               bias=nmax[:, b:b + 1], accum_out=psums[:, b:b + 1]).then_inc(probs_ready, 1)
                act.wait_ge(pe_pT, b + 1)
                if b >= 2:
                    act.wait_ge(pe_z, b - 1)
                act.activation(pT[:, b % 2, :], bank[6][0:CR, 0:NC * S], ACT.Copy).then_inc(pT_ready, 1)
                act.wait_ge(pe_z, b + 1)
                if b >= 2:
                    act.wait_ge(pe_x3, b - 1)
                act.activation(zT[:, b % 2, 0, :], bank[7][:, 0:S], ACT.Copy)
                act.activation(zT[0:DC - P, b % 2, 1, :], bank[7][0:DC - P, S:2 * S],
                               ACT.Copy).then_inc(z_ready, 1)
            for g in range(NG):
                turn_evac(4 + g, bank[3])
            act.wait_ge(dlog_ready, 1)
            act.activation(e2[:, :], dlog[:, :], ACT.Exp).then_inc(e2_ready, 1)
            w_high(2)
            w_high(3)

            def xe_high(e):
                act.wait_ge(pe_xeT, e + 1)
                if e >= 2:
                    act.wait_ge(pe_hid, 4 * (e - 1))
                act.activation(xeT_hi[e % 2][:, :, :], bank[6 + e % 2][:, 0:KD * CAP],
                               ACT.Copy).then_inc(xe_hi, 1)

            def hidden(e):
                for f in range(KF):
                    act.wait_ge(pe_hid, 4 * e + f // 2 + 1)
                    if e >= 1:
                        act.wait_ge(hid_lo_ready, 2 * (e - 1) + f // 4 + 1)
                    act.activation(hid[:, f, :], bank[f // 2][:, (f % 2) * CAP:(f % 2 + 1) * CAP],
                                   ACT.Gelu_apprx_tanh,
                                   bias=vec[:, V_B1 + e * KF + f:V_B1 + e * KF + f + 1]).then_inc(hid_ready, 1)
                    if f % 4 == 3:
                        act.wait_ge(hid_ready, KF * e + f + 1)
                        if e >= 2:
                            act.wait_ge(pe_y, 2 * (e - 1))
                        act.activation(hid_hi[e % 2][:, f - 3:f + 1, :], hid[:, f - 3:f + 1, :],
                                       ACT.Copy).then_inc(hid_hi_ready, 1)

            xe_high(0)
            xe_high(1)
            hidden(0)
            for e in range(E):
                if e + 2 < E:
                    xe_high(e + 2)
                    w_high(2 * (e + 2))
                if e + 1 < E:
                    hidden(e + 1)
                if e + 2 < E:
                    w_high(2 * (e + 2) + 1)

        @block.tensor
        def _(pe):
            def turn(n, banks):
                g = n % 2
                for b in range(GB):
                    pe.wait_ge(xn_ready, B * (n // 2) + g * GB + b + 1)
                    for k in range(KD):
                        mm = pe.transpose(banks[k][:, row_tok(b)], xn_sb[:, g * GB + b, k * P:(k + 1) * P],
                                          ident[0:S, 0:S])
                        if b == GB - 1:
                            mm.then_inc(pe_turn, 1)

            def lru_mm(dst, w, m, rhs_of):
                for k in range(KD):
                    mm = pe.matmul(dst, wl[:, w, k, m * P:(m + 1) * P], rhs_of(k), start=k == 0, stop=k == KD - 1)
                return mm

            pe.wait_ge(ld_rows, 16)
            for m in range(2):
                pe.matmul(bank[7][:, m * S:(m + 1) * S], rows_sb[0:PE_DIM + 1, R_WX + m * P:R_WX + (m + 1) * P],
                          rows_sb[0:PE_DIM + 1, R_PE:R_PE + S], start=True, stop=True)
            pe.matmul(bank[7][0:S, D:2 * D], rows_sb[:, R_PE:R_PE + S], rows_sb[:, R_WDX:R_WDX + D],
                      start=True, stop=True).then_inc(pe_tabs, 1)
            pe.wait_ge(ld_small, 32)
            turn(0, bank[0:2])
            pe.wait_ge(ld_lru, 32)

            def xh_products(g):
                pe.wait_ge(turn0_ready, g + 1)
                pe.wait_ge(turn1_ready, g + 1)
                for m in range(2):
                    lru_mm(bank[2 + 2 * g + m][:, 0:GT], L_X, m, lambda k: xnT[:, k, tok(g)]).then_inc(pe_xh, 1)

            xh_products(0)
            turn(1, bank[0:2])
            xh_products(1)

            pe.wait_ge(ld_att, 16)
            for m in range(KD):
                for k in range(KD):
                    pe.matmul(bank[6][:, m * DA:(m + 1) * DA], wa[:, k, A_WQ + m * P:A_WQ + (m + 1) * P],
                              wa[:, k, A_WK:A_WK + DA], start=k == 0, stop=k == KD - 1)
            for m, n in ((0, P), (1, DB)):
                for k in range(KD):
                    mm = pe.matmul(bank[6][0:n, 400 + m:401 + m], wa[:, k, A_WK + m * P:A_WK + m * P + n],
                                   vec[:, V_BQ + k:V_BQ + k + 1], start=k == 0, stop=k == KD - 1)
            mm.then_inc(pe_setup, 1)
            pe.wait_ge(tabs_ready, 3)
            for m, n in ((0, P), (1, DC - P)):
                for k in range(KD):
                    mm = pe.matmul(bank[7][0:n, m * D:(m + 1) * D], wa[:, k, A_WV + m * P:A_WV + m * P + n],
                                   wa[:, k, A_WO:A_WO + D], start=k == 0, stop=k == KD - 1)
            mm.then_inc(pe_setup, 1)
            pe.wait_ge(bvb_ready, 1)
            for k in range(KD):
                pe.matmul(bank[0][0:S, 0:D], bvb[:, k, :], wa[:, k, A_WO:A_WO + D], start=k == 0, stop=False)
            pe.matmul(bank[0][0:S, 0:D], ones[0:1, 0:S], rows_sb[0:1, R_BO:R_BO + D],
                      start=False, stop=True).then_inc(pe_setup, 1)

            for g in range(NG):
                pe.wait_ge(xh_ready, 2 * g + 2)
                for i, (w, m) in enumerate(((L_GA, 0), (L_GX, 0), (L_GA, 1), (L_GX, 1))):
                    j = 4 * g + i
                    if j == 0:
                        pe.wait_ge(setup_ready, 5)
                    if j >= 4:
                        pe.wait_ge(gate_ready, j - 3)
                    lru_mm(bank[i][:, 0:GT], w, m, lambda k: xh[:, k, tok(g)]).then_inc(pe_gate, 1)
            for pair in range(4):
                for i in range(2):
                    for k in range(KD):
                        pe.matmul(bank[4 + pair][0:S, i * D:(i + 1) * D], xnT[:, k, row_tok(2 * pair + i)],
                                  wl[:, L_DX, k, :], start=(i == 0 and k == 0), stop=False,
                                  skip_group_check=True)
            for pair in range(4):
                pe.wait_ge(h_ready, 2 * (pair // 2) + 2)
                for i in range(2):
                    for k in range(KD):
                        mm = pe.matmul(bank[4 + pair][0:S, i * D:(i + 1) * D], xh[:, k, row_tok(2 * pair + i)],
                                       wl[:, L_O, k, :], start=False, stop=(i == 1 and k == KD - 1),
                                       skip_group_check=True)
                mm.then_inc(pe_x2, 1)

            def q_products(g):
                pe.wait_ge(turn0_ready, 3 + g)
                pe.wait_ge(turn1_ready, 3 + g)
                if g == 1:
                    pe.wait_ge(q0_ready, 1)
                    pe.wait_ge(q1_ready, 1)
                for m, n in ((0, P), (1, DB)):
                    for k in range(KD):
                        mm = pe.matmul(bank[2 + m][0:n, 0:GT], m_sb[:, k, m * P:m * P + n], xnT[:, k, tok(g)],
                                       start=k == 0, stop=k == KD - 1)
                    mm.then_inc(pe_q, 1)

            def scores(b):
                if b >= 2:
                    pe.wait_ge(probs_ready, b - 1)
                else:
                    pe.wait_ge(x2_ready, 4)
                pe.wait_ge(q0_ready, b // GB + 1)
                pe.wait_ge(q1_ready, b // GB + 1)
                for m, n in ((0, P), (1, DB)):
                    mm = pe.matmul(bank[4 + b % 2][0:S, 0:CE], qT[0:n, m, row_tok(b)],
                                   yT[0:n, m, b * CE:(b + 1) * CE], start=m == 0, stop=m == 1)
                mm.then_inc(pe_score, 1)

            def turn_probs(b):
                pe.wait_ge(probs_ready, b + 1)
                if b >= 1:
                    pe.wait_ge(pT_ready, b)
                for c in range(NC):
                    mm = pe.transpose(bank[6][0:CR, c * S:(c + 1) * S], probs[:, b % 2, c * CR:(c + 1) * CR],
                                      ident[0:S, 0:S])
                mm.then_inc(pe_pT, 1)

            def mix(b):
                pe.wait_ge(pT_ready, b + 1)
                if b >= 1:
                    pe.wait_ge(z_ready, b)
                for m, n in ((0, P), (1, DC - P)):
                    for c in range(NC):
                        mm = pe.matmul(bank[7][0:n, m * S:(m + 1) * S], yr[:, b * NC + c, m * P:m * P + n],
                                       pT[:, b % 2, c * S:(c + 1) * S], start=c == 0, stop=c == NC - 1)
                mm.then_inc(pe_z, 1)

            def project(b):
                pe.wait_ge(z_ready, b + 1)
                if b >= 2:
                    pe.wait_ge(x3_ready, b - 1)
                for m, n in ((0, P), (1, DC - P)):
                    mm = pe.matmul(bank[b % 2][0:S, 0:D], zT[0:n, b % 2, m, :], wvo[0:n, m, :],
                                   start=m == 0, stop=m == 1)
                mm.then_inc(pe_x3, 1)

            pe.wait_ge(gate_ready, 8)
            turn(2, bank[0:2])
            q_products(0)
            pe.wait_ge(ld_yT, 16)
            scores(0)
            scores(1)
            turn(3, bank[0:2])
            q_products(1)
            pe.wait_ge(ld_yr, 16)
            for b in range(B):
                turn_probs(b)
                if b + 2 < B:
                    scores(b + 2)
                mix(b)
                if b >= 1:
                    project(b - 1)
                if b == 6:
                    pe.wait_ge(q0_ready, 2)
                    pe.wait_ge(q1_ready, 2)
                    turn(4, bank[2:4])
            project(B - 1)
            pe.wait_ge(turn0_ready, 5)
            pe.wait_ge(turn1_ready, 5)
            turn(5, bank[2:4])
            pe.wait_ge(ld_moe, 48)
            pe.wait_ge(turn0_ready, 6)
            pe.wait_ge(turn1_ready, 6)
            for b in range(B):
                for k in range(KD):
                    mm = pe.matmul(bank[4][0:S, b * E:(b + 1) * E], xnT[:, k, row_tok(b)], wg_sb[:, k, :],
                                   start=k == 0, stop=k == KD - 1)
            mm.then_inc(pe_logits, 1)
            pe.wait_ge(hot_ready, 1)
            hots = hot[:, :, :].rearrange("p e k -> p (e k)")
            pe.matmul(bank[5][0:S, 0:P], cst[0:S, C_LM:C_LM + S], hots, start=True, stop=True)
            pe.matmul(bank[5][0:S, P:2 * P], ones[0:S, 0:S], hots, start=True, stop=True).then_inc(pe_count, 1)
            pe.wait_ge(map_ready, 1)
            for n in range(KB):
                mm = pe.matmul(bank[4][0:HR, 0:2 * NH], hotl[:, n, :],
                               rhs[:, n, :, :].rearrange("p q h -> p (q h)"), start=n == 0, stop=n == KB - 1)
            mm.then_inc(pe_map, 1)

            def split_mm(dst, a, b, first, last):
                pe.matmul(dst, a[0], b[0], start=first, stop=False)
                pe.matmul(dst, a[0], b[1], start=False, stop=False)
                return pe.matmul(dst, a[1], b[0], start=False, stop=last)

            def turn_rows(e):
                pe.wait_ge(got[e % 2], 32 * (e // 2 + 1))
                if e >= 2:
                    pe.wait_ge(xe_lo, e - 1)
                for k in range(KD):
                    for j in range(2):
                        mm = pe.transpose(bank[6 + e % 2][:, k * CAP + j * HR:k * CAP + (j + 1) * HR],
                                          xe[:, e % 2, j, k * P:(k + 1) * P], ident[0:HR, 0:HR])
                mm.then_inc(pe_xeT, 1)

            def up(e):
                pe.wait_ge(xe_lo, e + 1)
                pe.wait_ge(w_lo, 2 * e + 1)
                s = e % 2
                for f in range(KF):
                    if e >= 1 and f % 2 == 0:
                        pe.wait_ge(hid_ready, KF * (e - 1) + f + 2)
                    for k in range(KD):
                        fs = slice(f * P, (f + 1) * P)
                        mm = split_mm(bank[f // 2][:, (f % 2) * CAP:(f % 2 + 1) * CAP],
                                      (w1_hi[s][:, k, fs], w1_lo[s][:, k, fs]),
                                      (xeT_hi[s][:, k, :], xeT_lo[s][:, k, :]), k == 0, k == KD - 1)
                    if f % 2 == 1:
                        mm.then_inc(pe_hid, 1)

            def down(e):
                pe.wait_ge(w_lo, 2 * e + 2)
                s = e % 2
                for j in range(2):
                    if e >= 1:
                        pe.wait_ge(y_ready, 2 * (e - 1) + j + 1)
                    hs = slice(j * HR, (j + 1) * HR)
                    for f in range(KF):
                        if j == 0 and f % 4 == 0:
                            pe.wait_ge(hid_lo_ready, 2 * e + f // 4 + 1)
                        mm = split_mm(bank[4 + j][0:HR, 0:D], (hid_hi[s][:, f, hs], hid_lo[s][:, f, hs]),
                                      (w2_hi[s][:, f, :], w2_lo[s][:, f, :]), f == 0, f == KF - 1)
                    mm.then_inc(pe_y, 1)

            turn_rows(0)
            turn_rows(1)
            up(0)
            for e in range(E):
                if e + 2 < E:
                    turn_rows(e + 2)
                if e + 1 < E:
                    up(e + 1)
                down(e)

        @block.vector
        def _(dve):
            links = [0]

            def link(ins):
                links[0] += 1
                ins.then_inc(v_chain, 1)
                dve.wait_ge(v_chain, links[0])

            def ln_stats(layer, pair):
                for b in (2 * pair, 2 * pair + 1):
                    link(dve.bn_stats(stats[:, b, :], x_sb[:, b, :]))
                    ins = dve.bn_aggr(mv[:, b, :], stats[:, b, :])
                ins.then_inc(var_ready, 1)
                dve.wait_ge(var_ready, 4 * layer + pair + 1)

            def ln_scale(layer, pair):
                dve.wait_ge(rstd_ready, 4 * layer + pair + 1)
                for b in (2 * pair, 2 * pair + 1):
                    dve.tensor_scalar(xn_sb[:, b, :], x_sb[:, b, :], mv[:, b, 0:1], rstd[:, b:b + 1],
                                      ALU.subtract, ALU.mult).then_inc(xn_ready, 1)

            def turn_evac(n, src):
                dve.wait_ge(pe_turn, 2 * n + 1)
                dve.tensor_copy(xnT[:, 0, tok(n % 2)], src[:, 0:GT]).then_inc(turn0_ready, 1)

            def w_low(u, parts=1, part=0):
                n = KF * D // parts
                cols = slice(part * n, (part + 1) * n)
                dve.wait_ge(w_hi, u + 1)
                hi, lo = split_of(u)
                ins = dve.tensor_tensor(lo[:, cols], raw[u % RAW][:, cols], hi[:, cols].bitcast(F32), ALU.subtract)
                if part == parts - 1:
                    ins.then_inc(w_lo, 1)

            for pair in range(4):
                if pair % 2 == 0:
                    dve.wait_ge(ld_x[pair // 2], 16)
                ln_stats(0, pair)
                if pair >= 1:
                    ln_scale(0, pair - 1)
            ln_scale(0, 3)
            turn_evac(0, bank[0])
            dve.wait_ge(elog_ready, 1)
            link(dve.tensor_scalar(nlog[:, :], nlog[:, :], 1.0, None, ALU.add))
            dve.reciprocal(ae[:, :], nlog[:, :]).then_inc(ae_ready, 1)
            dve.wait_ge(pe_tabs, 1)
            dve.tensor_scalar(dxtab[:, :], bank[7][0:S, D:2 * D], 0.5, None, ALU.mult).then_inc(tabs_ready, 1)
            for k in range(KD):
                ins = dve.tensor_copy(bvb[:, k, :], vec[:, V_BV + k:V_BV + k + 1].to_broadcast([P, S]))
            ins.then_inc(bvb_ready, 1)
            dve.wait_ge(sin_ready, 1)
            for m in range(2):
                dve.tensor_scalar(xtab[:, m, :], bank[7][:, m * S:(m + 1) * S], s_in[:, m:m + 1], None,
                                  ALU.mult).then_inc(tabs_ready, 1)
            dve.wait_ge(tabs_ready, 3)
            for g in range(NG):
                if g == 1:
                    turn_evac(1, bank[0])
                for m in range(2):
                    dve.wait_ge(pe_xh, 2 * g + m + 1)
                    dve.scalar_tensor_tensor(
                        xh[:, m, tok(g)].rearrange("p (b t) -> p b t", t=S),
                        bank[2 + 2 * g + m][:, 0:GT].rearrange("p (b t) -> p b t", t=S),
                        s_in[:, m:m + 1], xtab[:, m, :].unsqueeze(1).to_broadcast([P, GB, S]),
                        ALU.mult, ALU.add).then_inc(xh_ready, 1)
            for g in range(NG):
                for m in range(2):
                    n = 2 * g + m
                    a = ga[:, m, tok(g)]
                    dve.wait_ge(sq_ready, n + 1)
                    link(dve.tensor_scalar(a, a, ae[:, m:m + 1], None, ALU.mult))
                    dve.memset(a[:, 0:GT:S], 0.0)
                    dve.wait_ge(gxh_ready, n + 1)
                    dve.wait_ge(rt_ready, n + 1)
                    link(dve.tensor_tensor(gx[:, m, tok(g)], gx[:, m, tok(g)], rt[:, m, tok(g)], ALU.mult))
                    dve.wait_ge(pe_gate, 4 * g + 4)
                    dve.tensor_tensor_scan(xh[:, m, tok(g)], a, gx[:, m, tok(g)], 0.0,
                                           ALU.mult, ALU.add).then_inc(h_ready, 1)
            for pair in range(4):
                dve.wait_ge(pe_x2, pair + 1)
                dve.wait_ge(xt_ready, pair // 2 + 1)
                xp = x_sb[:, 2 * pair:2 * pair + 2, :].rearrange("p b d -> p (b d)")
                dve.scalar_tensor_tensor(xp, bank[4 + pair][0:S, :], 0.5, xp,
                                         ALU.mult, ALU.add).then_inc(x2_ready, 1)
                dve.wait_ge(x2_ready, pair + 1)
                ln_stats(1, pair)
                if pair >= 1:
                    ln_scale(1, pair - 1)
            ln_scale(1, 3)
            for g in range(NG):
                turn_evac(2 + g, bank[0])
                dve.wait_ge(pe_q, 2 * g + 1)
                dve.wait_ge(setup_ready, 1)
                dve.tensor_scalar(qT[:, 0, tok(g)], bank[2][:, 0:GT], qb[:, 0:1], SCALE,
                                  ALU.add, ALU.mult).then_inc(q0_ready, 1)

            def row_max(b):
                dve.wait_ge(pe_score, b + 1)
                dve.tensor_reduce(nmax[:, b:b + 1], bank[4 + b % 2][0:S, 0:C], AX.X, ALU.max,
                                  negate=True).then_inc(nmax_ready, 1)

            def x3_evac(b):
                dve.wait_ge(pe_x3, b + 1)
                dve.wait_ge(xb_ready, b // GB + 1)
                link(dve.reciprocal(rsum[:, b:b + 1], psums[:, b:b + 1]))
                dve.scalar_tensor_tensor(x_sb[:, b, :], bank[b % 2][0:S, 0:D], rsum[:, b:b + 1], x_sb[:, b, :],
                                         ALU.mult, ALU.add).then_inc(x3_ready, 1)
                dve.wait_ge(x3_ready, b + 1)
                if b % 2 == 1:
                    ln_stats(2, b // 2)

            row_max(0)
            row_max(1)
            for b in range(B):
                w_low(b // 4, 4, b % 4)
                if b + 2 < B:
                    row_max(b + 2)
                if b >= 1:
                    x3_evac(b - 1)
                    if b % 2 == 0:
                        pass
                    elif b >= 3:
                        ln_scale(2, (b - 3) // 2)
                if b == 7:
                    turn_evac(4, bank[2])
            x3_evac(B - 1)
            ln_scale(2, 3)
            turn_evac(5, bank[2])

            dve.wait_ge(pe_logits, 1)
            link(dve.tensor_tensor(lg[:, :, :], bank[4][0:S, 0:B * E].rearrange("p (b e) -> p b e", e=E),
                                   bg_sb[:, :].unsqueeze(1).to_broadcast([S, B, E]), ALU.add))
            for b in range(B):
                ins = dve.max(top[:, b, :], lg[:, b, :])
            link(ins)
            for b in range(B):
                dve.max_index(topi[:, b, :], top[:, b, :], lg[:, b, :])
            dve.tensor_tensor(dlog[:, :], top[:, :, 1], top[:, :, 0], ALU.subtract).then_inc(dlog_ready, 1)
            dve.wait_ge(dlog_ready, 1)
            link(dve.tensor_copy(chosen[:, :].rearrange("p (k b) -> p k b", k=TOPK),
                                 topi[:, :, 0:TOPK].rearrange("p b k -> p k b")))
            dve.tensor_tensor(hot[:, :, :], chosen[:, :].unsqueeze(1).to_broadcast([S, E, KB]),
                              cst[0:S, C_EXP:C_EXP + E * KB].rearrange("p (e k) -> p e k", e=E),
                              ALU.is_equal).then_inc(hot_ready, 1)
            dve.wait_ge(e2_ready, 1)
            link(dve.tensor_scalar(den[:, :], e2[:, :], 1.0, None, ALU.add))
            link(dve.reciprocal(gate[:, 0, :], den[:, :]))
            link(dve.tensor_tensor(gate[:, 1, :], gate[:, 0, :], e2[:, :], ALU.mult))
            dve.wait_ge(pe_count, 1)
            link(dve.tensor_tensor_scan(cum[:, :], cst[0:S, C_MASK:C_MASK + E * KB], bank[5][0:S, P:2 * P], 0.0,
                                        ALU.mult, ALU.add))
            link(dve.tensor_tensor(pos[:, :], bank[5][0:S, 0:P], cum[:, :], ALU.add))
            flat = "p e k -> p (e k)"
            link(dve.scalar_tensor_tensor(kept[:, :, :].rearrange(flat), pos[:, :], float(CAP),
                                          hot[:, :, :].rearrange(flat), ALU.is_lt, ALU.mult))
            link(dve.tensor_tensor(posk[:, :, :].rearrange(flat), pos[:, :], kept[:, :, :].rearrange(flat), ALU.mult))
            link(dve.tensor_reduce(own[:, :], posk[:, :, :].rearrange("p e k -> p k e"), AX.X, ALU.add))
            link(dve.tensor_scalar(ishi[:, :], own[:, :], float(HR), None, ALU.is_ge))
            link(dve.scalar_tensor_tensor(low[:, :], ishi[:, :], -float(HR), own[:, :], ALU.mult, ALU.add))
            dve.tensor_tensor(hotl[:, :, :], low[:, :].unsqueeze(2).to_broadcast([S, KB, HR]),
                              cst[0:S, C_ROW:C_ROW + HR].unsqueeze(1).to_broadcast([S, KB, HR]), ALU.is_equal)
            keptk = kept[:, :, :].rearrange("p e k -> p k e")
            link(dve.tensor_tensor(hoth[:, :, :, 1], keptk, ishi[:, :].unsqueeze(2).to_broadcast([S, KB, E]), ALU.mult))
            dve.tensor_tensor(hoth[:, :, :, 0], keptk, hoth[:, :, :, 1], ALU.subtract)
            link(dve.tensor_tensor(tokv[:, :], cst[0:S, C_TOK:C_TOK + KB], own[:, :], ALU.subtract))
            hoths = hoth[:, :, :, :].rearrange("p k e j -> p k (e j)")
            dve.tensor_tensor(rhs[:, :, 0, :], hoths, tokv[:, :].unsqueeze(2).to_broadcast([S, KB, NH]), ALU.mult)
            dve.tensor_tensor(rhs[:, :, 1, :], hoths,
                              gate[:, :, :].rearrange("p k b -> p (k b)").unsqueeze(2).to_broadcast([S, KB, NH]),
                              ALU.mult).then_inc(map_ready, 1)
            dve.wait_ge(pe_map, 1)
            link(dve.tensor_tensor(slot_tok[:, :], bank[4][0:HR, 0:NH], cst[0:HR, C_SPARE:C_SPARE + NH], ALU.add))
            dve.tensor_scalar(get_idx[:, :], slot_tok[:, :], float(T - 1), None, ALU.min).then_inc(idx_ready, 1)
            dve.tensor_copy(put_idx[:, :], slot_tok[:, :]).then_inc(idx_ready, 1)
            dve.tensor_copy(slot_gate[:, :], bank[4][0:HR, NH:2 * NH])

            def xe_low(e):
                dve.wait_ge(xe_hi, e + 1)
                dve.tensor_tensor(xeT_lo[e % 2][:, :, :], bank[6 + e % 2][:, 0:KD * CAP].rearrange(
                    "p (k r) -> p k r", k=KD), xeT_hi[e % 2][:, :, :].bitcast(F32), ALU.subtract).then_inc(xe_lo, 1)

            def hidden_low(e):
                for n in range(2):
                    fs = slice(4 * n, 4 * n + 4)
                    dve.wait_ge(hid_hi_ready, 2 * e + n + 1)
                    dve.tensor_tensor(hid_lo[e % 2][:, fs, :], hid[:, fs, :], hid_hi[e % 2][:, fs, :].bitcast(F32),
                                      ALU.subtract).then_inc(hid_lo_ready, 1)

            def y_rows_out(e):
                for j in range(2):
                    h = 2 * e + j
                    dve.wait_ge(pe_y, h + 1)
                    if e >= 2 and j == 0:
                        dve.wait_ge(put, 32 * (e - 1))
                    yo = y_sb[:, e % 2, j, :]
                    link(dve.tensor_tensor(yo, bank[4 + j][0:HR, 0:D], b2_sb[:, e, :], ALU.add))
                    dve.tensor_scalar(yo, yo, slot_gate[:, h:h + 1], None, ALU.mult).then_inc(y_ready, 1)

            w_low(2)
            xe_low(0)
            xe_low(1)
            hidden_low(0)
            w_low(3)
            for e in range(E):
                if e + 2 < E:
                    xe_low(e + 2)
                    w_low(2 * (e + 2))
                if e + 1 < E:
                    hidden_low(e + 1)
                if e + 2 < E:
                    w_low(2 * (e + 2) + 1)
                y_rows_out(e)


def position_features():
    at = np.arange(S, dtype=np.float32)[:, None]
    div = np.exp(np.arange(0, PE_DIM, 2, dtype=np.float32) * np.float32(-np.log(10000.0) / PE_DIM))
    pe = np.zeros((S, PE_DIM), np.float32)
    pe[:, 0::2] = np.sin(at * div)
    pe[:, 1::2] = np.cos(at * div)
    return (pe / np.float32(10) / np.float32(10)).T


def constants():
    c = np.zeros((P, C_ALL), np.float32)
    row = np.arange(P)
    c[:, C_ID:C_ID + P] = np.eye(P)
    c[:, C_LM:C_LM + S] = (row[:, None] < np.arange(S)[None]) - 1.0
    c[:, C_ONE:C_ONE + P] = 1.0
    c[:, C_MASK:C_MASK + P] = np.arange(P) % KB != 0
    c[:, C_EXP:C_EXP + P] = np.arange(P) // KB
    c[:, C_TOK:C_TOK + KB] = (np.arange(KB) % B)[None] * S + row[:, None] - T
    c[:, C_ROW:C_ROW + HR] = np.arange(HR)
    c[:, C_SPARE:C_SPARE + NH] = T + row[:, None] + HR * (np.arange(NH) % 2)[None]
    return c


def kernel(**inputs):
    import numpy as _np
    import concourse.bacc as _bacc
    from concourse import mybir as _mybir
    from concourse.bass_utils import run_bass_kernel_spmd as _run

    v = {k: _np.asarray(a) for k, a in inputs.items()}

    def blocks(w):
        return w.reshape(-1, P, w.shape[-1]).transpose(1, 0, 2)

    def cols(w):
        return w.reshape(-1, P).T

    cat, f32 = _np.concatenate, _np.float32
    w_x, w_dx = v["L0_attn_W_x"], v["L0_attn_W_dx"]
    ctx = v["ctx_768"]
    rows = _np.zeros((PE_DIM + 2, R_ALL), f32)
    rows[:, R_PE:R_PE + S] = cat([position_features(), _np.ones((2, S), f32)])
    rows[:PE_DIM, R_WX:R_WX + D] = w_x[D:]
    rows[PE_DIM, R_WX:R_WX + D] = v["L0_attn_b_x"]
    rows[:PE_DIM, R_WDX:R_WDX + D] = w_dx[D:]
    rows[PE_DIM, R_WDX:R_WDX + D] = v["L0_attn_b_dx"]
    rows[PE_DIM + 1, R_WDX:R_WDX + D] = v["L0_attn_b_o"]
    rows[0, R_BO:R_BO + D] = v["L0_xattn_bo"]
    y_turned = _np.zeros((2 * P, B, CE), f32)
    y_turned[:DC, :, :C] = ctx.transpose(2, 0, 1)
    y_turned[DC] = 1.0
    y_rows = _np.zeros((B, CP, DC), f32)
    y_rows[:, :C] = ctx
    arrays = {
        "x": v["x"].transpose(1, 0, 2),
        "consts": constants(),
        "vectors": cat([cols(v[n]) for n in ("L0_attn_a_logit", "L0_attn_b_gx", "L0_attn_b_ga", "L0_xattn_bq",
                                             "L0_xattn_bv", "L0_ffn_b1")], 1),
        "rows": rows,
        "w_lru": _np.stack([blocks(w) for w in (w_x[:D], w_dx[:D], v["L0_attn_W_gx"], v["L0_attn_W_ga"],
                                                v["L0_attn_W_o"])], 1),
        "w_att": cat([blocks(v["L0_xattn_Wq"].T), blocks(v["L0_xattn_Wk"].T), blocks(v["L0_xattn_bk"][:, None]),
                      blocks(v["L0_xattn_Wv"].T), blocks(v["L0_xattn_Wo"])], 2),
        "y_turned": y_turned.reshape(2, P, B * CE).transpose(1, 0, 2),
        "y_rows": y_rows.reshape(B * NC, CR, DC).transpose(1, 0, 2),
        "wg": blocks(v["L0_ffn_Wg"]),
        "bg": v["L0_ffn_bg"][None],
        "w1": v["L0_ffn_W1"].reshape(E, KD, P, F).transpose(0, 2, 1, 3).reshape(E, P, KD * F),
        "w2": v["L0_ffn_W2"].reshape(E, KF, P, D).transpose(0, 2, 1, 3).reshape(E, P, KF * D),
        "b2": v["L0_ffn_b2"],
    }
    arrays = {f"in_{k}_dram": _np.ascontiguousarray(a) for k, a in arrays.items()}
    nc = _bacc.Bacc("TRN2", target_bir_lowering=False, num_devices=1)
    args = [nc.dram_tensor(n, a.shape, _mybir.dt.from_np(a.dtype), kind="ExternalInput").ap()
            for n, a in arrays.items()]
    xn_dram = nc.dram_tensor("xn_dram", (T, D), _mybir.dt.float32, kind="Internal").ap()
    out = nc.dram_tensor("out_0_dram", (OUT_ROWS, D), _mybir.dt.float32, kind="ExternalOutput").ap()
    layer_kernel(nc, *args, xn_dram, out)
    r = _run(nc, [arrays], core_ids=[0])
    return r.results[0]["out_0_dram"][:T].reshape(B, S, D)
```

```python
from contextlib import ExitStack

import concourse.bass as bass
import numpy as np
from concourse import mybir

F32 = mybir.dt.float32
F32R = mybir.dt.float32r
BF16 = mybir.dt.bfloat16
U32 = mybir.dt.uint32
ALU = mybir.AluOpType
ACT = mybir.ActivationFunctionType
AX = mybir.AxisListType

B, S, D = 8, 100, 256
C, DC = 361, 192
E, F, TOPK = 8, 1024, 2
PE_DIM = 16
CAP = -(-12 * B * S * TOPK // (10 * E))
HD = 32
EPS = 1e-5
P = 128
KD, KF = D // P, F // P
T = B * S
NG, GB = 2, B // 2
GT = GB * S
NC = 3
CR = -(-C // NC)
CP = NC * CR
CE = C + 1
DA = DC + 1
DB = DA - P
HR = CAP // 2
NH = 2 * E
KB = TOPK * B
OUT_ROWS = T + CAP
NQ = 5
RAW = 4
SCALE = 1.0 / float(np.sqrt(HD))

C_ID = 0
C_LM = C_ID + P
C_ONE = C_LM + S
C_MASK = C_ONE + P
C_EXP = C_MASK + P
C_TOKH = C_EXP + P
C_TOKL = C_TOKH + KB
C_ROW = C_TOKL + KB
C_SPARE = C_ROW + HR
C_ALL = C_SPARE + NH

V_LOGIT, V_BGX, V_BGA, V_BQ, V_BV, V_B1 = 0, 2, 4, 6, 8, 10
V_ALL = V_B1 + E * KF

R_PE, R_WX, R_WDX, R_BO = 0, S, S + D, S + 2 * D
R_ALL = S + 3 * D

L_X, L_DX, L_GX, L_GA, L_O = range(5)
A_WQ, A_WK, A_WV, A_WO = 0, D, D + DA, D + DA + DC
A_ALL = A_WO + D


def layer_kernel(nc, x, consts, vectors, rows, w_lru, w_att, y_turned, y_rows, wg, bg, w1, w2, b2,
                 xn_dram, out):
    with ExitStack() as ctx, ExitStack() as front:
        def sb(name, shape, dt=F32, where=ctx):
            return where.enter_context(nc.sbuf_tensor(name, shape, dt))

        def sem(name):
            return ctx.enter_context(nc.semaphore(name))

        bank = [ctx.enter_context(nc.psum_tensor(f"bank{i}", [P, 512], F32)) for i in range(8)]

        cst = sb("cst", [P, C_ALL])
        vec = sb("vec", [P, V_ALL])
        x_sb = sb("x_sb", [S, B, D])
        xn_sb = sb("xn_sb", [S, B, D])
        xnT = sb("xnT", [P, KD, T])
        stats = sb("stats", [S, B, 6])
        mv = sb("mv", [S, B, 2])
        veps = sb("veps", [S, B])
        rstd = sb("rstd", [S, B])
        pw = sb("pw", [P, B])
        b2_sb = sb("b2_sb", [HR, E, D])
        bg_sb = sb("bg_sb", [S, E])
        with ExitStack() as early:
            wl_hi = sb("wl_hi", [P, 4, KD, D], F32R, early)
            wl_lo = sb("wl_lo", [P, 4, KD, D], F32R, early)
        raw = [sb(f"raw{i}", [P, KF * D]) for i in (2, 3, 0, 1)]
        raw = raw[2:] + raw[:2]
        w1_hi, w1_lo, w2_hi, w2_lo = ([None, None] for _ in range(4))

        def split_slot(i):
            w1_hi[i] = sb(f"w1_hi{i}", [P, KD, F], F32R)
            w1_lo[i] = sb(f"w1_lo{i}", [P, KD, F], F32R)
            w2_hi[i] = sb(f"w2_hi{i}", [P, KF, D], F32R)
            w2_lo[i] = sb(f"w2_lo{i}", [P, KF, D], F32R)

        split_slot(0)

        def fb(name, shape, dt=F32):
            return sb(name, shape, dt, front)

        rows_sb = fb("rows_sb", [PE_DIM + 2, R_ALL])
        wl = fb("wl", [P, 5, KD, D])
        wa = fb("wa", [P, KD, A_ALL])
        wg_sb = fb("wg_sb", [P, KD, E])
        yT = fb("yT", [P, 2, B * CE])
        yr = fb("yr", [CR, B * NC, DC])
        nlog = fb("nlog", [P, 2])
        ae = fb("ae", [P, 2])
        s_in = fb("s_in", [P, 2])
        half = fb("half", [P, 2])
        xtab = fb("xtab", [P, 2, S])
        dxtab = fb("dxtab", [S, D])
        xh = fb("xh", [P, 2, T])
        gx = fb("gx", [P, 2, T])
        ga = fb("ga", [P, 2, T])
        rt = fb("rt", [P, 2, T])
        bvb = fb("bvb", [P, KD, S])
        m_sb = fb("m_sb", [P, KD, DA])
        qb = fb("qb", [P, 2])
        qbs = fb("qbs", [P, 2])
        wvo = fb("wvo", [P, 2, D])
        brow = fb("brow", [S, D])
        qT = fb("qT", [P, 2, T])
        probs = fb("probs", [S, 2, CP])
        pT = fb("pT", [CR, 2, NC * S])
        zT = fb("zT", [P, 2, 2, S])
        nmax = fb("nmax", [S, B])
        psums = fb("psums", [S, B])
        rsum = fb("rsum", [S, B])
        front.close()

        split_slot(1)
        lg = sb("lg", [S, B, E])
        top = sb("top", [S, B, 8])
        topi = sb("topi", [S, B, 8], U32)
        dlog = sb("dlog", [S, B])
        e2 = sb("e2", [S, B])
        den = sb("den", [S, B])
        gate = sb("gate", [S, KB])
        chosen = sb("chosen", [S, KB])
        hot = sb("hot", [S, E, KB], BF16)
        cum = sb("cum", [S, E * KB])
        pos = sb("pos", [S, E * KB])
        kept = sb("kept", [S, E, KB], BF16)
        posk = sb("posk", [S, E, KB])
        own = sb("own", [S, KB])
        low = sb("low", [S, KB], BF16)
        ishi = sb("ishi", [S, KB], BF16)
        hoth = sb("hoth", [S, E, 2, KB], BF16)
        tokq = sb("tokq", [S, NQ, KB], BF16)
        rhs = sb("rhs", [S, NQ, NH, KB], BF16)
        hotl = sb("hotl", [S, HR, KB], BF16)
        rows_b = sb("rows_b", [S, HR, KB], BF16)
        lm_b = sb("lm_b", [S, S], BF16)
        one_b = sb("one_b", [S, S], BF16)
        slot_gate = sb("slot_gate", [HR, NH])
        slot_tok = sb("slot_tok", [HR, NH])
        put_idx = sb("put_idx", [HR, NH], U32)
        get_idx = sb("get_idx", [HR, NH], U32)
        xe = sb("xe", [HR, 2, 2, D])
        xeT_hi = [sb(f"xeT_hi{i}", [P, KD, CAP], F32R) for i in range(2)]
        xeT_lo = [sb(f"xeT_lo{i}", [P, KD, CAP], F32R) for i in range(2)]
        hid = sb("hid", [P, KF, CAP])
        hid_hi = [sb(f"hid_hi{i}", [P, KF, CAP], F32R) for i in range(2)]
        hid_lo = [sb(f"hid_lo{i}", [P, KF, CAP], F32R) for i in range(2)]
        y_sb = sb("y_sb", [HR, 2, 2, D])

        xh_hi, xh_lo, xnT_hi, xnT_lo = (
            w[0][:, :, :].rearrange("p a b -> p (a b)")[:, 0:KD * T].rearrange("p (k t) -> p k t", k=KD)
            for w in (w2_hi, w2_lo, w1_hi, w1_lo))

        warm = sb("warm", [P, 4])
        ident = cst[:, C_ID:C_ID + P]
        ones = cst[:, C_ONE:C_ONE + P]

        ld_x = [sem(f"ld_x{g}") for g in range(NG)]
        ld_small, ld_rows, ld_lru, ld_att, ld_yT, ld_yr, ld_moe = (
            sem(n) for n in ("ld_small", "ld_rows", "ld_lru", "ld_att", "ld_yT", "ld_yr", "ld_moe"))
        ld_raw = [sem(f"ld_raw{i}") for i in range(RAW)]
        st_xn, st_out = sem("st_xn"), sem("st_out")
        v_chain, a_chain, p_chain = sem("v_chain"), sem("a_chain"), sem("p_chain")
        var_ready, rstd_ready, xn_ready = sem("var_ready"), sem("rstd_ready"), sem("xn_ready")
        nlog_ready, elog_ready, ae_ready, sin_ready = (
            sem(n) for n in ("nlog_ready", "elog_ready", "ae_ready", "sin_ready"))
        pe_tabs, tabs_ready, xt_ready = sem("pe_tabs"), sem("tabs_ready"), sem("xt_ready")
        bvb_ready = sem("bvb_ready")
        pe_turn, turn0_ready, turn1_ready = sem("pe_turn"), sem("turn0_ready"), sem("turn1_ready")
        pe_xh, xh_ready = sem("pe_xh"), sem("xh_ready")
        pe_setup, setup_ready = sem("pe_setup"), sem("setup_ready")
        pe_gate, gate_ready, sq_ready, rt_ready = (
            sem(n) for n in ("pe_gate", "gate_ready", "sq_ready", "rt_ready"))
        h_ready = sem("h_ready")
        wgate_hi, wgate_lo, xh_hi_ready, xh_lo_ready = (
            sem(n) for n in ("wgate_hi", "wgate_lo", "xh_hi_ready", "xh_lo_ready"))
        dx_split, h_hi_ready, h_lo_ready = sem("dx_split"), sem("h_hi_ready"), sem("h_lo_ready")
        pe_x2, x2_ready, xb_ready = sem("pe_x2"), sem("x2_ready"), sem("xb_ready")
        pe_q, q0_ready, q1_ready = sem("pe_q"), sem("q0_ready"), sem("q1_ready")
        pad_ready = sem("pad_ready")
        pe_score, nmax_ready, probs_ready = sem("pe_score"), sem("nmax_ready"), sem("probs_ready")
        pe_pT, pT_ready, pe_z, z_ready = sem("pe_pT"), sem("pT_ready"), sem("pe_z"), sem("z_ready")
        pe_x3, x3_ready = sem("pe_x3"), sem("x3_ready")
        pe_turn3, turn3_ready, pe_logits, lg_ready = (
            sem(n) for n in ("pe_turn3", "turn3_ready", "pe_logits", "lg_ready"))
        dlog_ready, e2_ready = sem("dlog_ready"), sem("e2_ready")
        hot_ready, pe_count, map_ready, pe_map = (
            sem(n) for n in ("hot_ready", "pe_count", "map_ready", "pe_map"))
        idx_ready = sem("idx_ready")
        w_hi, w_lo = sem("w_hi"), sem("w_lo")
        got = [sem(f"got{i}") for i in range(2)]
        put = sem("put")
        pe_xeT, xe_hi, xe_lo = sem("pe_xeT"), sem("xe_hi"), sem("xe_lo")
        pe_hid, hid_ready, hid_hi_ready, hid_lo_ready = (
            sem(n) for n in ("pe_hid", "hid_ready", "hid_hi_ready", "hid_lo_ready"))
        pe_y, y_ready = sem("pe_y"), sem("y_ready")

        block = ctx.enter_context(nc.Block())

        def tok(g):
            return slice(g * GT, (g + 1) * GT)

        def row_tok(b):
            return slice(b * S, (b + 1) * S)

        def raw_load(eng, u):
            if u >= RAW:
                eng.wait_ge(w_hi, u - RAW + 1)
                eng.wait_ge(w_lo, u - RAW + 1)
            src = (w1 if u % 2 == 0 else w2)[u // 2]
            eng.dma_start(raw[u % RAW][:, :], src).then_inc(ld_raw[u % RAW], 16)

        def split_of(u):
            hi, lo = ((w1_hi, w1_lo), (w2_hi, w2_lo))[u % 2]
            s = (u // 2) % 2
            flat = "p a b -> p (a b)"
            return hi[s][:, :, :].rearrange(flat), lo[s][:, :, :].rearrange(flat)

        @block.sync
        def _(sp):
            sp.dma_start(x_sb[:, 0:GB, :], x[:, 0:GB, :]).then_inc(ld_x[0], 16)
            sp.dma_start(cst[:, :], consts).then_inc(ld_small, 16)
            sp.dma_start(x_sb[:, GB:B, :], x[:, GB:B, :]).then_inc(ld_x[1], 16)
            sp.dma_start(wl[:, L_GX:, :, :], w_lru[:, L_GX:, :, :]).then_inc(ld_lru, 16)
            sp.dma_start(wa[:, :, :], w_att).then_inc(ld_att, 16)
            sp.dma_start(yT[:, :, :], y_turned).then_inc(ld_yT, 16)
            sp.dma_start(yr[:, :, :], y_rows).then_inc(ld_yr, 16)
            sp.dma_start(wg_sb[:, :, :], wg).then_inc(ld_moe, 16)
            sp.dma_start(bg_sb[:, :], bg.to_broadcast([S, E])).then_inc(ld_moe, 16)
            sp.dma_start(b2_sb[:, :, :], b2.unsqueeze(0).to_broadcast([HR, E, D])).then_inc(ld_moe, 16)
            raw_load(sp, 0)
            raw_load(sp, 1)
            sp.wait_ge(ld_moe, 48)
            sp.dma_start(out[T:OUT_ROWS, :].rearrange("(a p) d -> p a d", p=HR),
                         b2_sb[:, 0:2, :]).then_inc(st_out, 16)
            sp.wait_ge(pe_x2, 4)
            for u in range(2, RAW + 2):
                raw_load(sp, u)
            for g in range(NG):
                bs = slice(g * GB, (g + 1) * GB)
                sp.wait_ge(x3_ready, (g + 1) * GB)
                sp.dma_start(out[tok(g), :].rearrange("(b t) d -> t b d", t=S),
                             x_sb[:, bs, :]).then_inc(st_out, 16)
                sp.wait_ge(xn_ready, 2 * B + (g + 1) * GB)
                sp.dma_start(xn_dram[tok(g), :].rearrange("(b t) d -> t b d", t=S),
                             xn_sb[:, bs, :]).then_inc(st_xn, 16)
            for u in range(RAW + 2, 2 * E):
                raw_load(sp, u)
            sp.wait_ge(st_out, 48)
            sp.wait_ge(st_xn, 32)

        @block.gpsimd
        def _(pool):
            links = [0]

            def link(ins):
                links[0] += 1
                ins.then_inc(p_chain, 1)
                pool.wait_ge(p_chain, links[0])

            def rstd_of(layer, b):
                pool.wait_ge(var_ready, B * layer + b + 1)
                link(pool.tensor_scalar(veps[:, b:b + 1], mv[:, b, 1:2], EPS, None, ALU.add))
                pool.tensor_tensor(rstd[:, b:b + 1], veps[:, b:b + 1], pw[0:S, 0:1], ALU.pow).then_inc(rstd_ready, 1)

            link(pool.memset(pw[:, :], -0.5))
            link(pool.memset(half[:, :], 0.5))
            pool.wait_ge(ld_small, 32)
            pool.tensor_scalar(nlog[:, :], vec[:, V_LOGIT:V_LOGIT + 2], -1.0, 80.0,
                               ALU.mult, ALU.min).then_inc(nlog_ready, 1)
            for b in range(GB + 2):
                rstd_of(0, b)
            pool.wait_ge(ae_ready, 1)
            link(pool.tensor_tensor(s_in[:, :], ae[:, :], ae[:, :], ALU.mult))
            link(pool.tensor_scalar(s_in[:, :], s_in[:, :], -1.0, 1.0, ALU.mult, ALU.add))
            pool.tensor_tensor(s_in[:, :], s_in[:, :], half[:, :], ALU.pow).then_inc(sin_ready, 1)
            for b in range(GB + 2, B):
                rstd_of(0, b)
            pool.memset(probs[:, :, C:CP], 0.0).then_inc(pad_ready, 1)
            pool.wait_ge(wgate_hi, 1)
            pool.tensor_tensor(wl_lo[:, L_GX - 1:L_GA], wl[:, L_GX:L_O], wl_hi[:, L_GX - 1:L_GA].bitcast(F32),
                               ALU.subtract).then_inc(wgate_lo, 1)
            pool.wait_ge(tabs_ready, 3)
            for g in range(NG):
                bs = slice(g * GB, (g + 1) * GB)
                pool.wait_ge(xn_ready, (g + 1) * GB)
                pool.tensor_tensor(x_sb[:, bs, :], x_sb[:, bs, :],
                                   dxtab[:, :].unsqueeze(1).to_broadcast([S, GB, D]),
                                   ALU.add).then_inc(xt_ready, 1)
            for b in range(B):
                rstd_of(1, b)
            for g in range(NG):
                bs = slice(g * GB, (g + 1) * GB)
                pool.wait_ge(xn_ready, B + (g + 1) * GB)
                pool.wait_ge(setup_ready, 5)
                pool.tensor_tensor(x_sb[:, bs, :], x_sb[:, bs, :],
                                   brow[:, :].unsqueeze(1).to_broadcast([S, GB, D]),
                                   ALU.add).then_inc(xb_ready, 1)
            for b in range(B):
                rstd_of(2, b)

            def gather(e):
                if e >= 2:
                    pool.wait_ge(pe_xeT, e - 1)
                for j in range(2):
                    h = 2 * e + j
                    pool.indirect_dma_start(
                        xe[:, e % 2, j, :], None, xn_dram,
                        bass.IndirectOffsetOnAxis(ap=get_idx[:, h:h + 1], axis=0),
                        bounds_check=T - 1, oob_is_err=False).then_inc(got[e % 2], 16)

            def scatter_add(e):
                pool.wait_ge(put, 32 * e) if e else pool.wait_ge(st_out, 48)
                for j in range(2):
                    h = 2 * e + j
                    pool.wait_ge(y_ready, h + 1)
                    pool.indirect_dma_start(
                        out, bass.IndirectOffsetOnAxis(ap=put_idx[:, h:h + 1], axis=0),
                        y_sb[:, e % 2, j, :], None,
                        bounds_check=OUT_ROWS - 1, oob_is_err=True,
                        compute_op=ALU.add).then_inc(put, 16)

            pool.wait_ge(idx_ready, 2)
            pool.wait_ge(st_xn, 32)
            gather(0)
            gather(1)
            gather(2)
            for e in range(E):
                if e + 3 < E:
                    gather(e + 3)
                scatter_add(e)
            pool.wait_ge(put, 32 * E)

        @block.scalar
        def _(act):
            links = [0]

            def link(ins):
                links[0] += 1
                ins.then_inc(a_chain, 1)
                act.wait_ge(a_chain, links[0])

            def turn_evac(n, src):
                act.wait_ge(pe_turn, 2 * n + 2)
                act.activation(xnT[:, 1, tok(n % 2)], src[:, 0:GT], ACT.Copy).then_inc(turn1_ready, 1)

            def turn_pair_evac(p):
                act.wait_ge(pe_turn3, p + 1)
                act.activation(xnT[:, :, 2 * p * S:2 * (p + 1) * S],
                               bank[2 + p % 2][:, 0:2 * KD * S].rearrange("p (k t) -> p k t", k=KD),
                               ACT.Copy).then_inc(turn3_ready, 1)

            def w_high(u):
                act.wait_ge(ld_raw[u % RAW], 16 * (u // RAW + 1))
                if u >= 4:
                    act.wait_ge(pe_hid if u % 2 == 0 else pe_y,
                                (4 if u % 2 == 0 else 2) * (u // 2 - 1))
                act.activation(split_of(u)[0], raw[u % RAW][:, :], ACT.Copy).then_inc(w_hi, 1)

            def load_table(i, func):
                act.activation(warm[:, i:i + 1], ones[:, 0:1], func)

            act.dma_start(rows_sb[:, :], rows).then_inc(ld_rows, 16)
            act.dma_start(vec[:, :], vectors).then_inc(ld_small, 16)
            act.dma_start(wl[:, 0:L_GX, :, :], w_lru[:, 0:L_GX, :, :]).then_inc(ld_lru, 16)
            act.wait_ge(nlog_ready, 1)
            act.activation(nlog[:, :], nlog[:, :], ACT.Exp).then_inc(elog_ready, 1)
            load_table(0, ACT.Sigmoid)
            turn_evac(0, bank[1])
            act.wait_ge(ld_lru, 32)
            act.activation(wl_hi[:, L_GX - 1:L_GA], wl[:, L_GX:L_O], ACT.Copy).then_inc(wgate_hi, 1)

            def xh_high(g):
                act.wait_ge(xh_ready, 2 * g + 2)
                act.activation(xh_hi[:, :, tok(g)], xh[:, :, tok(g)], ACT.Copy).then_inc(xh_hi_ready, 1)

            turn_evac(1, bank[1])
            xh_high(0)
            xh_high(1)
            for n in range(2 * NG):
                g, m = n // 2, n % 2
                act.wait_ge(pe_gate, n + 1)
                act.activation(ga[:, m, tok(g)], bank[n][:, 0:GT], ACT.Sigmoid,
                               bias=vec[:, V_BGA + m:V_BGA + m + 1]).then_inc(gate_ready, 1)
                act.wait_ge(gate_ready, n + 1)
                act.activation(rt[:, m, tok(g)], ga[:, m, tok(g)], ACT.Square,
                               scale=ae[:, m:m + 1]).then_inc(sq_ready, 1)
            for n in range(2 * NG):
                act.wait_ge(sq_ready, n + 1)
                act.activation(rt[:, n % 2, tok(n // 2)], rt[:, n % 2, tok(n // 2)], ACT.Sqrt,
                               bias=1.0, scale=-1.0).then_inc(rt_ready, 1)
            load_table(1, ACT.Sigmoid)
            for n in range(2 * NG):
                g, m = n // 2, n % 2
                act.wait_ge(pe_gate, 2 * NG + n + 1)
                act.activation(gx[:, m, tok(g)], bank[n][:, 0:GT], ACT.Sigmoid,
                               bias=vec[:, V_BGX + m:V_BGX + m + 1]).then_inc(gate_ready, 1)

            def h_high(n):
                h = (slice(None), n % 2, tok(n // 2))
                act.wait_ge(h_ready, n + 1)
                act.activation(xh_hi[h], xh[h], ACT.Copy).then_inc(h_hi_ready, 1)

            h_high(0)
            h_high(1)
            act.wait_ge(pe_setup, 1)
            act.activation(m_sb[:, :, :], bank[6][:, 0:KD * DA], ACT.Copy)
            act.activation(qb[:, 0:1], bank[6][:, 400:401], ACT.Copy)
            act.activation(qb[0:DB, 1:2], bank[6][0:DB, 401:402], ACT.Copy)
            act.activation(qbs[:, 0:1], bank[6][:, 400:401], ACT.Copy, scale=SCALE)
            act.activation(qbs[0:DB, 1:2], bank[6][0:DB, 401:402], ACT.Copy, scale=SCALE).then_inc(setup_ready, 1)
            act.wait_ge(pe_setup, 2)
            act.activation(wvo[:, 0, :], bank[7][:, 0:D], ACT.Copy).then_inc(setup_ready, 1)
            act.activation(wvo[0:DC - P, 1, :], bank[7][0:DC - P, D:2 * D], ACT.Copy).then_inc(setup_ready, 1)
            h_high(2)
            h_high(3)
            act.wait_ge(pe_setup, 3)
            act.activation(brow[:, :], bank[0][0:S, 0:D], ACT.Copy).then_inc(setup_ready, 2)

            load_table(2, ACT.Exp)

            def q_evac(g):
                turn_evac(2 + g, bank[1])
                act.wait_ge(pe_q, 2 * g + 2)
                act.activation(qT[0:DB, 1, tok(g)], bank[3][0:DB, 0:GT], ACT.Identity,
                               bias=qbs[0:DB, 1:2], scale=SCALE).then_inc(q1_ready, 1)

            q_evac(0)
            act.wait_ge(pad_ready, 1)
            act.wait_ge(pe_x2, 4)
            w_high(0)
            for b in range(B):
                act.wait_ge(nmax_ready, b + 1)
                if b >= 2:
                    act.wait_ge(pe_pT, b - 1)
                act.activation(probs[:, b % 2, 0:C], bank[4 + b % 2][0:S, 0:C], ACT.Exp,
                               bias=nmax[:, b:b + 1], accum_out=psums[:, b:b + 1]).then_inc(probs_ready, 1)
                act.wait_ge(pe_pT, b + 1)
                if b >= 2:
                    act.wait_ge(pe_z, b - 1)
                act.activation(pT[:, b % 2, :], bank[6][0:CR, 0:NC * S], ACT.Copy).then_inc(pT_ready, 1)
                act.wait_ge(pe_z, b + 1)
                if b >= 2:
                    act.wait_ge(pe_x3, b - 1)
                act.activation(zT[:, b % 2, 0, :], bank[7][:, 0:S], ACT.Copy)
                act.activation(zT[0:DC - P, b % 2, 1, :], bank[7][0:DC - P, S:2 * S],
                               ACT.Copy).then_inc(z_ready, 1)
                if b == 0:
                    q_evac(1)
                if b == 1:
                    w_high(1)
                if b >= 4 and b % 2 == 0:
                    turn_pair_evac(b // 2 - 2)
            turn_pair_evac(2)
            turn_pair_evac(3)
            act.wait_ge(dlog_ready, 1)
            act.activation(e2[:, :], dlog[:, :], ACT.Exp).then_inc(e2_ready, 1)
            load_table(3, ACT.Gelu_apprx_tanh)
            act.wait_ge(pe_logits, 4)
            w_high(2)

            def xe_high(e):
                act.wait_ge(pe_xeT, e + 1)
                if e >= 2:
                    act.wait_ge(pe_hid, 4 * (e - 1))
                act.activation(xeT_hi[e % 2][:, :, :], bank[6 + e % 2][:, 0:KD * CAP],
                               ACT.Copy).then_inc(xe_hi, 1)

            def hidden(e, between=None):
                for f in range(KF):
                    if between is not None and f == KF // 2:
                        xe_high(between)
                    act.wait_ge(pe_hid, 4 * e + f // 2 + 1)
                    if e >= 1:
                        act.wait_ge(hid_lo_ready, 2 * (e - 1) + f // 4 + 1)
                    act.activation(hid[:, f, :], bank[f // 2][:, (f % 2) * CAP:(f % 2 + 1) * CAP],
                                   ACT.Gelu_apprx_tanh,
                                   bias=vec[:, V_B1 + e * KF + f:V_B1 + e * KF + f + 1]).then_inc(hid_ready, 1)
                    if f % 4 == 3:
                        act.wait_ge(hid_ready, KF * e + f + 1)
                        if e >= 2:
                            act.wait_ge(pe_y, 2 * (e - 1))
                        act.activation(hid_hi[e % 2][:, f - 3:f + 1, :], hid[:, f - 3:f + 1, :],
                                       ACT.Copy).then_inc(hid_hi_ready, 1)

            xe_high(0)
            hidden(0, between=1)
            for e in range(E):
                if e + 2 < E:
                    xe_high(e + 2)
                if e + 1 < E:
                    w_high(2 * (e + 1) + 1)
                if e + 2 < E:
                    w_high(2 * (e + 2))
                if e + 1 < E:
                    hidden(e + 1)

        @block.tensor
        def _(pe):
            def turn(n, banks):
                g = n % 2
                for b in range(GB):
                    pe.wait_ge(xn_ready, B * (n // 2) + g * GB + b + 1)
                    for k in range(KD):
                        mm = pe.transpose(banks[k][:, row_tok(b)], xn_sb[:, g * GB + b, k * P:(k + 1) * P],
                                          ident[0:S, 0:S])
                        if b == GB - 1:
                            mm.then_inc(pe_turn, 1)

            def split_mm(dst, a, b, first, last, **kw):
                pe.matmul(dst, a[0], b[0], start=first, stop=False, **kw)
                pe.matmul(dst, a[0], b[1], start=False, stop=False, **kw)
                return pe.matmul(dst, a[1], b[0], start=False, stop=last, **kw)

            def lru_mm(dst, w, m, rhs_of):
                for k in range(KD):
                    mm = pe.matmul(dst, wl[:, w, k, m * P:(m + 1) * P], rhs_of(k), start=k == 0, stop=k == KD - 1)
                return mm

            pe.wait_ge(ld_rows, 16)
            for m in range(2):
                pe.matmul(bank[7][:, m * S:(m + 1) * S], rows_sb[0:PE_DIM + 1, R_WX + m * P:R_WX + (m + 1) * P],
                          rows_sb[0:PE_DIM + 1, R_PE:R_PE + S], start=True, stop=True)
            pe.matmul(bank[7][0:S, D:2 * D], rows_sb[:, R_PE:R_PE + S], rows_sb[:, R_WDX:R_WDX + D],
                      start=True, stop=True).then_inc(pe_tabs, 1)
            pe.wait_ge(ld_small, 32)
            turn(0, bank[0:2])
            pe.wait_ge(ld_lru, 32)

            def xh_products(g):
                pe.wait_ge(turn0_ready, g + 1)
                pe.wait_ge(turn1_ready, g + 1)
                for m in range(2):
                    lru_mm(bank[2 + 2 * g + m][:, 0:GT], L_X, m, lambda k: xnT[:, k, tok(g)]).then_inc(pe_xh, 1)

            xh_products(0)
            turn(1, bank[0:2])
            xh_products(1)

            def gate_products(w, g):
                pe.wait_ge(xh_lo_ready, g + 1)
                pe.wait_ge(wgate_lo, 1)
                for m in range(2):
                    n = 2 * g + m
                    if w == L_GX:
                        pe.wait_ge(gate_ready, n + 1)
                    for k in range(KD):
                        ms = slice(m * P, (m + 1) * P)
                        mm = split_mm(bank[n][:, 0:GT], (wl_hi[:, w - 1, k, ms], wl_lo[:, w - 1, k, ms]),
                                      (xh_hi[:, k, tok(g)], xh_lo[:, k, tok(g)]), k == 0, k == KD - 1)
                    mm.then_inc(pe_gate, 1)

            def dx_products(pair):
                pe.wait_ge(dx_split, 1)
                if pair >= 2:
                    pe.wait_ge(setup_ready, 5)
                for i in range(2):
                    for k in range(KD):
                        rows_ = row_tok(2 * pair + i)
                        split_mm(bank[4 + pair][0:S, i * D:(i + 1) * D], (xnT_hi[:, k, rows_], xnT_lo[:, k, rows_]),
                                 (wl_hi[:, L_DX - 1, k, :], wl_lo[:, L_DX - 1, k, :]), i == 0 and k == 0, False,
                                 skip_group_check=True)

            def h_products(pair):
                pe.wait_ge(h_lo_ready, 2 * (pair // 2) + 2)
                for i in range(2):
                    for k in range(KD):
                        rows_ = row_tok(2 * pair + i)
                        mm = split_mm(bank[4 + pair][0:S, i * D:(i + 1) * D], (xh_hi[:, k, rows_], xh_lo[:, k, rows_]),
                                      (wl_hi[:, L_O - 1, k, :], wl_lo[:, L_O - 1, k, :]), False,
                                      i == 1 and k == KD - 1, skip_group_check=True)
                mm.then_inc(pe_x2, 1)

            for w in (L_GA, L_GX):
                for g in range(NG):
                    gate_products(w, g)

            pe.wait_ge(ld_att, 16)
            for m in range(KD):
                for k in range(KD):
                    pe.matmul(bank[6][:, m * DA:(m + 1) * DA], wa[:, k, A_WQ + m * P:A_WQ + (m + 1) * P],
                              wa[:, k, A_WK:A_WK + DA], start=k == 0, stop=k == KD - 1)
            for m, n in ((0, P), (1, DB)):
                for k in range(KD):
                    mm = pe.matmul(bank[6][0:n, 400 + m:401 + m], wa[:, k, A_WK + m * P:A_WK + m * P + n],
                                   vec[:, V_BQ + k:V_BQ + k + 1], start=k == 0, stop=k == KD - 1)
            mm.then_inc(pe_setup, 1)
            pe.wait_ge(tabs_ready, 3)
            for m, n in ((0, P), (1, DC - P)):
                for k in range(KD):
                    mm = pe.matmul(bank[7][0:n, m * D:(m + 1) * D], wa[:, k, A_WV + m * P:A_WV + m * P + n],
                                   wa[:, k, A_WO:A_WO + D], start=k == 0, stop=k == KD - 1)
            mm.then_inc(pe_setup, 1)
            pe.wait_ge(bvb_ready, 1)
            pe.wait_ge(gate_ready, 5)
            for k in range(KD):
                pe.matmul(bank[0][0:S, 0:D], bvb[:, k, :], wa[:, k, A_WO:A_WO + D], start=k == 0, stop=False)
            pe.matmul(bank[0][0:S, 0:D], ones[0:1, 0:S], rows_sb[0:1, R_BO:R_BO + D],
                      start=False, stop=True).then_inc(pe_setup, 1)

            for g in range(NG):
                dx_products(2 * g)
                dx_products(2 * g + 1)
                h_products(2 * g)
                h_products(2 * g + 1)

            def q_products(g):
                pe.wait_ge(turn0_ready, 3 + g)
                pe.wait_ge(turn1_ready, 3 + g)
                if g == 1:
                    pe.wait_ge(q0_ready, 1)
                    pe.wait_ge(q1_ready, 1)
                for m, n in ((0, P), (1, DB)):
                    for k in range(KD):
                        mm = pe.matmul(bank[2 + m][0:n, 0:GT], m_sb[:, k, m * P:m * P + n], xnT[:, k, tok(g)],
                                       start=k == 0, stop=k == KD - 1)
                    mm.then_inc(pe_q, 1)

            def scores(b):
                if b >= 2:
                    pe.wait_ge(probs_ready, b - 1)
                else:
                    pe.wait_ge(x2_ready, 4)
                pe.wait_ge(q0_ready, b // GB + 1)
                pe.wait_ge(q1_ready, b // GB + 1)
                for m, n in ((0, P), (1, DB)):
                    mm = pe.matmul(bank[4 + b % 2][0:S, 0:CE], qT[0:n, m, row_tok(b)],
                                   yT[0:n, m, b * CE:(b + 1) * CE], start=m == 0, stop=m == 1)
                mm.then_inc(pe_score, 1)

            def turn_probs(b):
                pe.wait_ge(probs_ready, b + 1)
                if b >= 1:
                    pe.wait_ge(pT_ready, b)
                for c in range(NC):
                    mm = pe.transpose(bank[6][0:CR, c * S:(c + 1) * S], probs[:, b % 2, c * CR:(c + 1) * CR],
                                      ident[0:S, 0:S])
                mm.then_inc(pe_pT, 1)

            def mix(b):
                pe.wait_ge(pT_ready, b + 1)
                if b >= 1:
                    pe.wait_ge(z_ready, b)
                for m, n in ((0, P), (1, DC - P)):
                    for c in range(NC):
                        mm = pe.matmul(bank[7][0:n, m * S:(m + 1) * S], yr[:, b * NC + c, m * P:m * P + n],
                                       pT[:, b % 2, c * S:(c + 1) * S], start=c == 0, stop=c == NC - 1)
                mm.then_inc(pe_z, 1)

            def project(b):
                pe.wait_ge(z_ready, b + 1)
                if b >= 2:
                    pe.wait_ge(x3_ready, b - 1)
                for m, n in ((0, P), (1, DC - P)):
                    mm = pe.matmul(bank[b % 2][0:S, 0:D], zT[0:n, b % 2, m, :], wvo[0:n, m, :],
                                   start=m == 0, stop=m == 1)
                mm.then_inc(pe_x3, 1)

            def turn3(p):
                if p < 2:
                    pe.wait_ge(q0_ready, 2)
                    pe.wait_ge(q1_ready, 2)
                else:
                    pe.wait_ge(lg_ready, p - 1)
                for i in range(2):
                    pe.wait_ge(xn_ready, 2 * B + 2 * p + i + 1)
                    for k in range(KD):
                        c = (k * 2 + i) * S
                        mm = pe.transpose(bank[2 + p % 2][:, c:c + S], xn_sb[:, 2 * p + i, k * P:(k + 1) * P],
                                          ident[0:S, 0:S])
                mm.then_inc(pe_turn3, 1)

            def logits(p):
                pe.wait_ge(ld_moe, 48)
                pe.wait_ge(turn3_ready, p + 1)
                for i in range(2):
                    for k in range(KD):
                        c = 2 * KD * S + i * E
                        mm = pe.matmul(bank[2 + p % 2][0:S, c:c + E], xnT[:, k, row_tok(2 * p + i)], wg_sb[:, k, :],
                                       start=k == 0, stop=k == KD - 1)
                mm.then_inc(pe_logits, 1)

            pe.wait_ge(gate_ready, 8)
            pe.wait_ge(setup_ready, 5)
            turn(2, bank[0:2])
            q_products(0)
            pe.wait_ge(ld_yT, 16)
            scores(0)
            scores(1)
            pe.wait_ge(ld_yr, 16)
            for b in range(B):
                turn_probs(b)
                if b + 2 < B:
                    scores(b + 2)
                mix(b)
                if b == 0:
                    turn(3, bank[0:2])
                    q_products(1)
                if b >= 1:
                    project(b - 1)
                if b >= 4 and b % 2 == 0:
                    turn3(b // 2 - 2)
                if b >= 5 and b % 2 == 1:
                    logits((b - 5) // 2)
            project(B - 1)
            turn3(2)
            logits(2)
            turn3(3)
            logits(3)
            pe.wait_ge(hot_ready, 1)
            hots = hot[:, :, :].rearrange("p e k -> p (e k)")
            pe.matmul(bank[5][0:S, 0:P], lm_b[:, :], hots, start=True, stop=True)
            pe.matmul(bank[5][0:S, P:2 * P], one_b[:, :], hots, start=True, stop=True).then_inc(pe_count, 1)
            pe.wait_ge(map_ready, 1)
            for n in range(KB):
                mm = pe.matmul(bank[4][0:HR, 0:NQ * NH], hotl[:, :, n],
                               rhs[:, :, :, n].rearrange("p q h -> p (q h)"), start=n == 0, stop=n == KB - 1)
            mm.then_inc(pe_map, 1)

            def turn_rows(e):
                pe.wait_ge(got[e % 2], 32 * (e // 2 + 1))
                if e >= 2:
                    pe.wait_ge(xe_lo, e - 1)
                for k in range(KD):
                    for j in range(2):
                        mm = pe.transpose(bank[6 + e % 2][:, k * CAP + j * HR:k * CAP + (j + 1) * HR],
                                          xe[:, e % 2, j, k * P:(k + 1) * P], ident[0:HR, 0:HR])
                mm.then_inc(pe_xeT, 1)

            def up(e, between=None):
                pe.wait_ge(xe_lo, e + 1)
                pe.wait_ge(w_lo, 2 * e + 1)
                s = e % 2
                for f in range(KF):
                    if between is not None and f == KF // 2:
                        turn_rows(between)
                    if e >= 1 and f % 2 == 0:
                        pe.wait_ge(hid_ready, KF * (e - 1) + f + 2)
                    for k in range(KD):
                        fs = slice(f * P, (f + 1) * P)
                        mm = split_mm(bank[f // 2][:, (f % 2) * CAP:(f % 2 + 1) * CAP],
                                      (w1_hi[s][:, k, fs], w1_lo[s][:, k, fs]),
                                      (xeT_hi[s][:, k, :], xeT_lo[s][:, k, :]), k == 0, k == KD - 1)
                    if f % 2 == 1:
                        mm.then_inc(pe_hid, 1)

            def down(e):
                pe.wait_ge(w_lo, 2 * e + 2)
                s = e % 2
                for j in range(2):
                    if e >= 1:
                        pe.wait_ge(y_ready, 2 * (e - 1) + j + 1)
                    hs = slice(j * HR, (j + 1) * HR)
                    for f in range(KF):
                        if j == 0 and f % 4 == 0:
                            pe.wait_ge(hid_lo_ready, 2 * e + f // 4 + 1)
                        mm = split_mm(bank[4 + j][0:HR, 0:D], (hid_hi[s][:, f, hs], hid_lo[s][:, f, hs]),
                                      (w2_hi[s][:, f, :], w2_lo[s][:, f, :]), f == 0, f == KF - 1)
                    mm.then_inc(pe_y, 1)

            turn_rows(0)
            up(0, between=1)
            for e in range(E):
                if e + 2 < E:
                    turn_rows(e + 2)
                if e + 1 < E:
                    up(e + 1)
                down(e)

        @block.vector
        def _(dve):
            links = [0]

            def link(ins):
                links[0] += 1
                ins.then_inc(v_chain, 1)
                dve.wait_ge(v_chain, links[0])

            def ln_stats(layer, b):
                link(dve.bn_stats(stats[:, b, :], x_sb[:, b, :]))
                dve.bn_aggr(mv[:, b, :], stats[:, b, :]).then_inc(var_ready, 1)

            def ln_scale(layer, b):
                dve.wait_ge(rstd_ready, B * layer + b + 1)
                dve.tensor_scalar(xn_sb[:, b, :], x_sb[:, b, :], mv[:, b, 0:1], rstd[:, b:b + 1],
                                  ALU.subtract, ALU.mult).then_inc(xn_ready, 1)

            def turn_evac(n, src):
                dve.wait_ge(pe_turn, 2 * n + 1)
                dve.tensor_copy(xnT[:, 0, tok(n % 2)], src[:, 0:GT]).then_inc(turn0_ready, 1)

            def w_low(u, parts=1, part=0):
                n = KF * D // parts
                cols = slice(part * n, (part + 1) * n)
                dve.wait_ge(w_hi, u + 1)
                hi, lo = split_of(u)
                ins = dve.tensor_tensor(lo[:, cols], raw[u % RAW][:, cols], hi[:, cols].bitcast(F32), ALU.subtract)
                if part == parts - 1:
                    ins.then_inc(w_lo, 1)

            for b in range(B + 1):
                if b % GB == 0 and b < B:
                    dve.wait_ge(ld_x[b // GB], 16)
                if b < B:
                    ln_stats(0, b)
                if b >= 1:
                    ln_scale(0, b - 1)
                if b == GB + 1:
                    dve.wait_ge(elog_ready, 1)
                    link(dve.tensor_scalar(nlog[:, :], nlog[:, :], 1.0, None, ALU.add))
                    dve.reciprocal(ae[:, :], nlog[:, :]).then_inc(ae_ready, 1)
                    turn_evac(0, bank[0])
            dve.wait_ge(pe_tabs, 1)
            dve.tensor_scalar(dxtab[:, :], bank[7][0:S, D:2 * D], 0.5, None, ALU.mult).then_inc(tabs_ready, 1)
            for k in range(KD):
                ins = dve.tensor_copy(bvb[:, k, :], vec[:, V_BV + k:V_BV + k + 1].to_broadcast([P, S]))
            ins.then_inc(bvb_ready, 1)
            dve.wait_ge(sin_ready, 1)
            for m in range(2):
                dve.tensor_scalar(xtab[:, m, :], bank[7][:, m * S:(m + 1) * S], s_in[:, m:m + 1], None,
                                  ALU.mult).then_inc(tabs_ready, 1)
            dve.wait_ge(tabs_ready, 3)

            def xh_low(g):
                dve.wait_ge(xh_hi_ready, g + 1)
                dve.tensor_tensor(xh_lo[:, :, tok(g)], xh[:, :, tok(g)], xh_hi[:, :, tok(g)].bitcast(F32),
                                  ALU.subtract).then_inc(xh_lo_ready, 1)

            for g in range(NG):
                if g == 1:
                    turn_evac(1, bank[0])
                    xh_low(0)
                for m in range(2):
                    dve.wait_ge(pe_xh, 2 * g + m + 1)
                    dve.scalar_tensor_tensor(
                        xh[:, m, tok(g)].rearrange("p (b t) -> p b t", t=S),
                        bank[2 + 2 * g + m][:, 0:GT].rearrange("p (b t) -> p b t", t=S),
                        s_in[:, m:m + 1], xtab[:, m, :].unsqueeze(1).to_broadcast([P, GB, S]),
                        ALU.mult, ALU.add).then_inc(xh_ready, 1)
            xh_low(1)
            for w in (L_DX, L_O):
                link(dve.tensor_copy(wl_hi[:, w - 1], wl[:, w]))
                link(dve.tensor_tensor(wl_lo[:, w - 1], wl[:, w], wl_hi[:, w - 1].bitcast(F32), ALU.subtract))
            dve.wait_ge(turn1_ready, 2)
            link(dve.tensor_copy(xnT_hi, xnT[:, :, :]))
            dve.tensor_tensor(xnT_lo, xnT[:, :, :], xnT_hi.bitcast(F32), ALU.subtract).then_inc(dx_split, 1)
            for n in range(2 * NG):
                m, t = n % 2, tok(n // 2)
                dve.wait_ge(sq_ready, n + 1)
                link(dve.tensor_scalar(ga[:, m, t], ga[:, m, t], ae[:, m:m + 1], None, ALU.mult))
                dve.memset(ga[:, m, t][:, 0:GT:S], 0.0)
            for n in range(2 * NG):
                m, t = n % 2, tok(n // 2)
                dve.wait_ge(rt_ready, n + 1)
                link(dve.tensor_tensor(rt[:, m, t], rt[:, m, t], xh[:, m, t], ALU.mult))

            def h_low(n):
                h = (slice(None), n % 2, tok(n // 2))
                dve.wait_ge(h_hi_ready, n + 1)
                dve.tensor_tensor(xh_lo[h], xh[h], xh_hi[h].bitcast(F32), ALU.subtract).then_inc(h_lo_ready, 1)

            for n in range(2 * NG):
                m, t = n % 2, tok(n // 2)
                dve.wait_ge(gate_ready, 2 * NG + n + 1)
                link(dve.tensor_tensor(gx[:, m, t], gx[:, m, t], rt[:, m, t], ALU.mult))
                dve.tensor_tensor_scan(xh[:, m, t], ga[:, m, t], gx[:, m, t], 0.0,
                                       ALU.mult, ALU.add).then_inc(h_ready, 1)
                if n >= 1:
                    h_low(n - 1)
            h_low(2 * NG - 1)

            def x2_evac(pair):
                dve.wait_ge(pe_x2, pair + 1)
                dve.wait_ge(xt_ready, pair // 2 + 1)
                xp = x_sb[:, 2 * pair:2 * pair + 2, :].rearrange("p b d -> p (b d)")
                dve.scalar_tensor_tensor(xp, bank[4 + pair][0:S, :], 0.5, xp,
                                         ALU.mult, ALU.add).then_inc(x2_ready, 1)
                dve.wait_ge(x2_ready, pair + 1)

            def q_evac(g):
                dve.wait_ge(pe_q, 2 * g + 1)
                dve.wait_ge(setup_ready, 1)
                dve.tensor_scalar(qT[:, 0, tok(g)], bank[2][:, 0:GT], qb[:, 0:1], SCALE,
                                  ALU.add, ALU.mult).then_inc(q0_ready, 1)

            def row_max(b):
                dve.wait_ge(pe_score, b + 1)
                dve.tensor_reduce(nmax[:, b:b + 1], bank[4 + b % 2][0:S, 0:C], AX.X, ALU.max,
                                  negate=True).then_inc(nmax_ready, 1)

            def x3_evac(b):
                dve.wait_ge(pe_x3, b + 1)
                dve.wait_ge(xb_ready, b // GB + 1)
                link(dve.reciprocal(rsum[:, b:b + 1], psums[:, b:b + 1]))
                dve.scalar_tensor_tensor(x_sb[:, b, :], bank[b % 2][0:S, 0:D], rsum[:, b:b + 1], x_sb[:, b, :],
                                         ALU.mult, ALU.add).then_inc(x3_ready, 1)
                dve.wait_ge(x3_ready, b + 1)
                ln_stats(2, b)

            def best(p):
                pr = slice(2 * p, 2 * p + 2)
                dve.wait_ge(pe_logits, p + 1)
                c = 2 * KD * S
                dve.tensor_tensor(lg[:, pr, :], bank[2 + p % 2][0:S, c:c + 2 * E].rearrange("p (b e) -> p b e", e=E),
                                  bg_sb[:, :].unsqueeze(1).to_broadcast([S, 2, E]), ALU.add).then_inc(lg_ready, 1)
                dve.wait_ge(lg_ready, p + 1)
                dve.max(top[:, 2 * p, :], lg[:, 2 * p, :])
                link(dve.max(top[:, 2 * p + 1, :], lg[:, 2 * p + 1, :]))
                for b in (2 * p, 2 * p + 1):
                    dve.max_index(topi[:, b, :], top[:, b, :], lg[:, b, :])

            x2_evac(0)
            ln_stats(1, 0)
            ln_stats(1, 1)
            x2_evac(1)
            ln_scale(1, 0)
            ln_stats(1, 2)
            ln_scale(1, 1)
            ln_stats(1, 3)
            ln_scale(1, 2)
            ln_scale(1, 3)
            x2_evac(2)
            turn_evac(2, bank[0])
            ln_stats(1, 4)
            ln_stats(1, 5)
            x2_evac(3)
            q_evac(0)
            ln_scale(1, 4)
            ln_stats(1, 6)
            ln_scale(1, 5)
            ln_stats(1, 7)
            row_max(0)
            ln_scale(1, 6)
            ln_scale(1, 7)
            row_max(1)
            for b in range(B):
                if b == 1:
                    turn_evac(3, bank[0])
                    q_evac(1)
                if b + 2 < B:
                    row_max(b + 2)
                w_low(b // 4, 4, b % 4)
                if b >= 2:
                    ln_scale(2, b - 2)
                if b >= 1:
                    x3_evac(b - 1)
                if b >= 6 and b % 2 == 0:
                    best(b // 2 - 3)
            ln_scale(2, B - 2)
            x3_evac(B - 1)
            best(1)
            ln_scale(2, B - 1)
            best(2)
            dve.tensor_copy(lm_b[:, :], cst[0:S, C_LM:C_LM + S])
            dve.tensor_copy(one_b[:, :], cst[0:S, C_ONE:C_ONE + S])
            dve.tensor_copy(tokq[:, 0, :], cst[0:S, C_TOKH:C_TOKH + KB])
            dve.tensor_copy(rows_b[:, :, :], cst[0:S, C_ROW:C_ROW + HR].unsqueeze(2).to_broadcast([S, HR, KB]))
            best(3)

            dve.tensor_tensor(dlog[:, :], top[:, :, 1], top[:, :, 0], ALU.subtract).then_inc(dlog_ready, 1)
            dve.wait_ge(dlog_ready, 1)
            link(dve.tensor_copy(chosen[:, :].rearrange("p (k b) -> p k b", k=TOPK),
                                 topi[:, :, 0:TOPK].rearrange("p b k -> p k b")))
            dve.tensor_tensor(hot[:, :, :], chosen[:, :].unsqueeze(1).to_broadcast([S, E, KB]),
                              cst[0:S, C_EXP:C_EXP + E * KB].rearrange("p (e k) -> p e k", e=E),
                              ALU.is_equal).then_inc(hot_ready, 1)
            dve.wait_ge(e2_ready, 1)
            link(dve.tensor_scalar(den[:, :], e2[:, :], 1.0, None, ALU.add))
            link(dve.reciprocal(gate[:, 0:B], den[:, :]))
            link(dve.tensor_tensor(gate[:, B:2 * B], gate[:, 0:B], e2[:, :], ALU.mult))
            for n in range(3):
                link(dve.tensor_copy(tokq[:, 2 + n, :], gate[:, :]))
                if n < 2:
                    link(dve.tensor_tensor(gate[:, :], gate[:, :], tokq[:, 2 + n, :], ALU.subtract))
            dve.wait_ge(pe_count, 1)
            link(dve.tensor_tensor_scan(cum[:, :], cst[0:S, C_MASK:C_MASK + E * KB], bank[5][0:S, P:2 * P], 0.0,
                                        ALU.mult, ALU.add))
            link(dve.tensor_tensor(pos[:, :], bank[5][0:S, 0:P], cum[:, :], ALU.add))
            flat = "p e k -> p (e k)"
            dve.scalar_tensor_tensor(kept[:, :, :].rearrange(flat), pos[:, :], float(CAP),
                                     hot[:, :, :].rearrange(flat), ALU.is_lt, ALU.mult)
            link(dve.tensor_tensor(posk[:, :, :].rearrange(flat), pos[:, :], hot[:, :, :].rearrange(flat), ALU.mult))
            link(dve.tensor_reduce(own[:, :], posk[:, :, :].rearrange("p e k -> p k e"), AX.X, ALU.add))
            dve.tensor_tensor(tokq[:, 1, :], cst[0:S, C_TOKL:C_TOKL + KB], own[:, :], ALU.subtract)
            link(dve.tensor_scalar(ishi[:, :], own[:, :], float(HR), None, ALU.is_ge))
            link(dve.scalar_tensor_tensor(low[:, :], ishi[:, :], -float(HR), own[:, :], ALU.mult, ALU.add))
            dve.tensor_tensor(hotl[:, :, :], low[:, :].unsqueeze(1).to_broadcast([S, HR, KB]), rows_b[:, :, :],
                              ALU.is_equal)
            link(dve.tensor_tensor(hoth[:, :, 1, :], kept[:, :, :], ishi[:, :].unsqueeze(1).to_broadcast([S, E, KB]),
                                   ALU.mult))
            link(dve.tensor_tensor(hoth[:, :, 0, :], kept[:, :, :], hoth[:, :, 1, :], ALU.subtract))
            dve.tensor_tensor(rhs[:, :, :, :],
                              hoth[:, :, :, :].rearrange("p e j k -> p (e j) k").unsqueeze(1).to_broadcast([S, NQ, NH, KB]),
                              tokq[:, :, :].unsqueeze(2).to_broadcast([S, NQ, NH, KB]),
                              ALU.mult).then_inc(map_ready, 1)
            dve.wait_ge(pe_map, 1)
            qcol = [bank[4][0:HR, q * NH:(q + 1) * NH] for q in range(NQ)]
            link(dve.tensor_tensor(slot_tok[:, :], qcol[0], cst[0:HR, C_SPARE:C_SPARE + NH], ALU.add))
            link(dve.tensor_tensor(slot_tok[:, :], qcol[1], slot_tok[:, :], ALU.add))
            dve.tensor_scalar(get_idx[:, :], slot_tok[:, :], float(T - 1), None, ALU.min).then_inc(idx_ready, 1)
            dve.tensor_copy(put_idx[:, :], slot_tok[:, :]).then_inc(idx_ready, 1)
            link(dve.tensor_copy(slot_gate[:, :], qcol[2]))
            link(dve.tensor_tensor(slot_gate[:, :], qcol[3], slot_gate[:, :], ALU.add))
            dve.tensor_tensor(slot_gate[:, :], qcol[4], slot_gate[:, :], ALU.add)

            def xe_low(e):
                dve.wait_ge(xe_hi, e + 1)
                dve.tensor_tensor(xeT_lo[e % 2][:, :, :], bank[6 + e % 2][:, 0:KD * CAP].rearrange(
                    "p (k r) -> p k r", k=KD), xeT_hi[e % 2][:, :, :].bitcast(F32), ALU.subtract).then_inc(xe_lo, 1)

            def hidden_low(e, between=None):
                for n in range(2):
                    if between is not None and n == 1:
                        xe_low(between)
                    fs = slice(4 * n, 4 * n + 4)
                    dve.wait_ge(hid_hi_ready, 2 * e + n + 1)
                    dve.tensor_tensor(hid_lo[e % 2][:, fs, :], hid[:, fs, :], hid_hi[e % 2][:, fs, :].bitcast(F32),
                                      ALU.subtract).then_inc(hid_lo_ready, 1)

            def y_rows_out(e):
                for j in range(2):
                    h = 2 * e + j
                    dve.wait_ge(pe_y, h + 1)
                    if e >= 2 and j == 0:
                        dve.wait_ge(put, 32 * (e - 1))
                    yo = y_sb[:, e % 2, j, :]
                    link(dve.tensor_tensor(yo, bank[4 + j][0:HR, 0:D], b2_sb[:, e, :], ALU.add))
                    dve.tensor_scalar(yo, yo, slot_gate[:, h:h + 1], None, ALU.mult).then_inc(y_ready, 1)

            w_low(2)
            xe_low(0)
            hidden_low(0, between=1)
            for e in range(E):
                if e + 2 < E:
                    xe_low(e + 2)
                if e + 1 < E:
                    w_low(2 * (e + 1) + 1)
                if e + 2 < E:
                    w_low(2 * (e + 2))
                if e + 1 < E:
                    hidden_low(e + 1)
                y_rows_out(e)


def position_features():
    at = np.arange(S, dtype=np.float32)[:, None]
    div = np.exp(np.arange(0, PE_DIM, 2, dtype=np.float32) * np.float32(-np.log(10000.0) / PE_DIM))
    pe = np.zeros((S, PE_DIM), np.float32)
    pe[:, 0::2] = np.sin(at * div)
    pe[:, 1::2] = np.cos(at * div)
    return (pe / np.float32(10) / np.float32(10)).T


def constants():
    c = np.zeros((P, C_ALL), np.float32)
    row = np.arange(P)
    c[:, C_ID:C_ID + P] = np.eye(P)
    c[:, C_LM:C_LM + S] = (row[:, None] < np.arange(S)[None]) - 1.0
    c[:, C_ONE:C_ONE + P] = 1.0
    c[:, C_MASK:C_MASK + P] = np.arange(P) % KB != 0
    c[:, C_EXP:C_EXP + P] = np.arange(P) // KB
    token = (np.arange(KB) % B)[None] * S + row[:, None] - T
    c[:, C_TOKH:C_TOKH + KB] = token // 4 * 4
    c[:, C_TOKL:C_TOKL + KB] = token % 4
    c[:, C_ROW:C_ROW + HR] = np.arange(HR)
    c[:, C_SPARE:C_SPARE + NH] = T + row[:, None] + HR * (np.arange(NH) % 2)[None]
    return c


def kernel(**inputs):
    import numpy as _np
    import concourse.bacc as _bacc
    from concourse import mybir as _mybir
    from concourse.bass_utils import run_bass_kernel_spmd as _run

    v = {k: _np.asarray(a) for k, a in inputs.items()}

    def blocks(w):
        return w.reshape(-1, P, w.shape[-1]).transpose(1, 0, 2)

    def cols(w):
        return w.reshape(-1, P).T

    cat, f32 = _np.concatenate, _np.float32
    w_x, w_dx = v["L0_attn_W_x"], v["L0_attn_W_dx"]
    ctx = v["ctx_768"]
    rows = _np.zeros((PE_DIM + 2, R_ALL), f32)
    rows[:, R_PE:R_PE + S] = cat([position_features(), _np.ones((2, S), f32)])
    rows[:PE_DIM, R_WX:R_WX + D] = w_x[D:]
    rows[PE_DIM, R_WX:R_WX + D] = v["L0_attn_b_x"]
    rows[:PE_DIM, R_WDX:R_WDX + D] = w_dx[D:]
    rows[PE_DIM, R_WDX:R_WDX + D] = v["L0_attn_b_dx"]
    rows[PE_DIM + 1, R_WDX:R_WDX + D] = v["L0_attn_b_o"]
    rows[0, R_BO:R_BO + D] = v["L0_xattn_bo"]
    y_turned = _np.zeros((2 * P, B, CE), f32)
    y_turned[:DC, :, :C] = ctx.transpose(2, 0, 1)
    y_turned[DC] = 1.0
    y_rows = _np.zeros((B, CP, DC), f32)
    y_rows[:, :C] = ctx
    arrays = {
        "x": v["x"].transpose(1, 0, 2),
        "consts": constants(),
        "vectors": cat([cols(v[n]) for n in ("L0_attn_a_logit", "L0_attn_b_gx", "L0_attn_b_ga", "L0_xattn_bq",
                                             "L0_xattn_bv", "L0_ffn_b1")], 1),
        "rows": rows,
        "w_lru": _np.stack([blocks(w) for w in (w_x[:D], w_dx[:D], v["L0_attn_W_gx"], v["L0_attn_W_ga"],
                                                v["L0_attn_W_o"])], 1),
        "w_att": cat([blocks(v["L0_xattn_Wq"].T), blocks(v["L0_xattn_Wk"].T), blocks(v["L0_xattn_bk"][:, None]),
                      blocks(v["L0_xattn_Wv"].T), blocks(v["L0_xattn_Wo"])], 2),
        "y_turned": y_turned.reshape(2, P, B * CE).transpose(1, 0, 2),
        "y_rows": y_rows.reshape(B * NC, CR, DC).transpose(1, 0, 2),
        "wg": blocks(v["L0_ffn_Wg"]),
        "bg": v["L0_ffn_bg"][None],
        "w1": v["L0_ffn_W1"].reshape(E, KD, P, F).transpose(0, 2, 1, 3).reshape(E, P, KD * F),
        "w2": v["L0_ffn_W2"].reshape(E, KF, P, D).transpose(0, 2, 1, 3).reshape(E, P, KF * D),
        "b2": v["L0_ffn_b2"],
    }
    arrays = {f"in_{k}_dram": _np.ascontiguousarray(a) for k, a in arrays.items()}
    nc = _bacc.Bacc("TRN2", target_bir_lowering=False, num_devices=1)
    args = [nc.dram_tensor(n, a.shape, _mybir.dt.from_np(a.dtype), kind="ExternalInput").ap()
            for n, a in arrays.items()]
    xn_dram = nc.dram_tensor("xn_dram", (T, D), _mybir.dt.float32, kind="Internal").ap()
    out = nc.dram_tensor("out_0_dram", (OUT_ROWS, D), _mybir.dt.float32, kind="ExternalOutput").ap()
    layer_kernel(nc, *args, xn_dram, out)
    r = _run(nc, [arrays], core_ids=[0])
    return r.results[0]["out_0_dram"][:T].reshape(B, S, D)
```

```python
from contextlib import ExitStack

import concourse.bass as bass
import numpy as np
from concourse import mybir

F32 = mybir.dt.float32
F32R = mybir.dt.float32r
BF16 = mybir.dt.bfloat16
U32 = mybir.dt.uint32
ALU = mybir.AluOpType
ACT = mybir.ActivationFunctionType
AX = mybir.AxisListType

B, S, D = 8, 100, 256
C, DC = 361, 192
E, F, TOPK = 8, 1024, 2
PE_DIM = 16
CAP = -(-12 * B * S * TOPK // (10 * E))
HD = 32
EPS = 1e-5
P = 128
KD, KF = D // P, F // P
T = B * S
NG, GB = 2, B // 2
GT = GB * S
NC = 3
CR = -(-C // NC)
CP = NC * CR
CE = C + 1
DA = DC + 1
DB = DA - P
HR = CAP // 2
NH = 2 * E
KB = TOPK * B
OUT_ROWS = T + CAP
NQ = 5
GQ = 1
KW_START, KW_TURN, KW_TAIL = 45, (2, 0, 3, 1), (4, 6, 22, 6, 20, 20, 8)
RAW = 4
SCALE = 1.0 / float(np.sqrt(HD))

C_ID = 0
C_LM = C_ID + P
C_ONE = C_LM + S
C_MASK = C_ONE + P
C_EXP = C_MASK + P
C_TOKH = C_EXP + P
C_TOKL = C_TOKH + KB
C_ROW = C_TOKL + KB
C_SPARE = C_ROW + CAP
C_ALL = C_SPARE + NH

V_LOGIT, V_BGX, V_BGA, V_BQ, V_BV, V_B1 = 0, 2, 4, 6, 8, 10
V_ALL = V_B1 + E * KF

R_PE, R_WX, R_WDX, R_BO = 0, S, S + D, S + 2 * D
R_ALL = S + 3 * D

L_X, L_DX, L_GX, L_GA, L_O = range(5)
A_WQ, A_WK, A_WV, A_WO = 0, D, D + DA, D + DA + DC
A_ALL = A_WO + D


def layer_kernel(nc, x, consts, vectors, rows, w_lru, w_att, y_turned, y_rows, wg, bg, w1, w2, b2,
                 xn_dram, out):
    with ExitStack() as ctx, ExitStack() as front:
        def sb(name, shape, dt=F32, where=ctx):
            return where.enter_context(nc.sbuf_tensor(name, shape, dt))

        def sem(name):
            return ctx.enter_context(nc.semaphore(name))

        bank = [ctx.enter_context(nc.psum_tensor(f"bank{i}", [P, 512], F32)) for i in range(8)]

        cst = sb("cst", [P, C_ALL])
        vec = sb("vec", [P, V_ALL])
        x_sb = sb("x_sb", [S, B, D])
        xn_sb = sb("xn_sb", [S, B, D])
        xnT = sb("xnT", [P, KD, T])
        stats = sb("stats", [S, B, 6])
        mv = sb("mv", [S, B, 2])
        nmr = sb("nmr", [S, B])
        veps = sb("veps", [S, B])
        rstd = sb("rstd", [S, B])
        pw = sb("pw", [P, B])
        b2_sb = sb("b2_sb", [HR, E, D])
        bg_sb = sb("bg_sb", [S, E])
        busy = sb("busy", [P, P], BF16)
        warm = sb("warm", [P, 5])
        with ExitStack() as early:
            wl_hi = sb("wl_hi", [P, 4, KD, D], F32R, early)
            wl_lo = sb("wl_lo", [P, 4, KD, D], F32R, early)
            wx_hi = sb("wx_hi", [P, KD, D], F32R, early)
            wx_lo = sb("wx_lo", [P, KD, D], F32R, early)
        raw = [sb(f"raw{i}", [P, KF * D]) for i in (2, 3, 0, 1)]
        raw = raw[2:] + raw[:2]
        w1_hi, w1_lo, w2_hi, w2_lo = ([None, None] for _ in range(4))

        def split_slot(i):
            w1_hi[i] = sb(f"w1_hi{i}", [P, KD, F], F32R)
            w1_lo[i] = sb(f"w1_lo{i}", [P, KD, F], F32R)
            w2_hi[i] = sb(f"w2_hi{i}", [P, KF, D], F32R)
            w2_lo[i] = sb(f"w2_lo{i}", [P, KF, D], F32R)

        split_slot(0)

        def fb(name, shape, dt=F32):
            return sb(name, shape, dt, front)

        rows_sb = fb("rows_sb", [PE_DIM + 2, R_ALL])
        wl = fb("wl", [P, 5, KD, D])
        wa = fb("wa", [P, KD, A_ALL])
        wg_sb = fb("wg_sb", [P, KD, E])
        nlog = fb("nlog", [P, 2])
        ae = fb("ae", [P, 2])
        s_in = fb("s_in", [P, 2])
        half = fb("half", [P, 2])
        xtab = fb("xtab", [P, 2, S])
        dxtab = fb("dxtab", [S, D])
        xh = fb("xh", [P, 2, T])
        bvb = fb("bvb", [P, KD, S])
        m_hi = fb("m_hi", [P, KD, DA], F32R)
        m_lo = fb("m_lo", [P, KD, DA], F32R)
        qb = fb("qb", [P, 2])
        qbs = fb("qbs", [P, 2])
        wvo = fb("wvo", [P, 2, D])
        brow = fb("brow", [S, D])
        with ExitStack() as late:
            xn_hi = sb("xn_hi", [S, B, D], F32R, late)
            xn_lo = sb("xn_lo", [S, B, D], F32R, late)
        with ExitStack() as late:
            qn_hi = sb("qn_hi", [P, KD, T], F32R, late)
            qn_lo = sb("qn_lo", [P, KD, T], F32R, late)
        gx = fb("gx", [P, 2, T])
        ga = fb("ga", [P, 2, T])
        rt = fb("rt", [P, 2, T])
        yT = fb("yT", [P, 2, B * CE])
        yr = fb("yr", [CR, B * NC, DC])
        qT = fb("qT", [P, 2, T])
        probs = fb("probs", [S, 2, CP])
        pT = fb("pT", [CR, 2, NC * S])
        zT = fb("zT", [P, 2, 2, S])
        nmax = fb("nmax", [S, B])
        psums = fb("psums", [S, B])
        rsum = fb("rsum", [S, B])
        front.close()

        split_slot(1)
        hid_hi, hid_lo, xeT_hi, xeT_lo = ([None, None] for _ in range(4))

        def row_slot(i):
            hid_hi[i] = sb(f"hid_hi{i}", [P, KF, CAP], F32R)
            hid_lo[i] = sb(f"hid_lo{i}", [P, KF, CAP], F32R)
            xeT_hi[i] = sb(f"xeT_hi{i}", [P, KD, CAP], F32R)
            xeT_lo[i] = sb(f"xeT_lo{i}", [P, KD, CAP], F32R)

        row_slot(1)
        y_sb = sb("y_sb", [HR, 2, 2, D])
        lg = sb("lg", [S, B, E])
        top = sb("top", [S, B, 8])
        topi = sb("topi", [S, B, 8], U32)
        dlog = sb("dlog", [S, B])
        e2 = sb("e2", [S, B])
        den = sb("den", [S, B])
        gate = sb("gate", [S, KB])
        chosen = sb("chosen", [S, KB])
        hot = sb("hot", [S, E, KB], BF16)
        cum = sb("cum", [S, E * KB])
        pos = sb("pos", [S, E * KB])
        kept = sb("kept", [S, E, KB], BF16)
        posk = sb("posk", [S, E, KB])
        own = sb("own", [S, KB])
        low = sb("low", [S, KB], BF16)
        ishi = sb("ishi", [S, KB], BF16)
        hoth = sb("hoth", [S, E, 2, KB], BF16)
        tokq = sb("tokq", [S, NQ, KB], BF16)
        rhs = sb("rhs", [S, NQ, NH, KB], BF16)
        hotl = sb("hotl", [S, HR, KB], BF16)
        rows_b = sb("rows_b", [S, HR, KB], BF16)
        lm_b = sb("lm_b", [S, S], BF16)
        one_b = sb("one_b", [S, S], BF16)
        slot_gate = sb("slot_gate", [HR, NH])
        slot_tok = sb("slot_tok", [HR, NH])
        put_idx = sb("put_idx", [HR, NH], U32)
        get_idx = sb("get_idx", [HR, NH], U32)
        xe = sb("xe", [HR, 2, 2, D])
        hid = sb("hid", [P, KF, CAP])
        row_slot(0)
        own1 = sb("own1", [S, KB])
        row0 = sb("row0", [S, B])
        hot0 = hid_hi[0]

        xh_hi, xh_lo, xnT_hi, xnT_lo = (
            w[0][:, :, :].rearrange("p a b -> p (a b)")[:, 0:KD * T].rearrange("p (k t) -> p k t", k=KD)
            for w in (w2_hi, w2_lo, w1_hi, w1_lo))

        ident = cst[:, C_ID:C_ID + P]
        ones = cst[:, C_ONE:C_ONE + P]

        ld_x = [sem(f"ld_x{b}") for b in (0, 2, 4)]
        ld_ident, ld_vec, ld_cst, ld_wx, ld_gates, ld_dx, ld_rows, ld_att, ld_yT, ld_yr, ld_moe = (
            sem(n) for n in ("ld_ident", "ld_vec", "ld_cst", "ld_wx", "ld_gates", "ld_dx", "ld_rows", "ld_att", "ld_yT", "ld_yr", "ld_moe"))
        ld_raw = [sem(f"ld_raw{i}") for i in range(RAW)]
        st_xn, st_out = sem("st_xn"), sem("st_out")
        v_chain, a_chain, p_chain = sem("v_chain"), sem("a_chain"), sem("p_chain")
        busy_ready = sem("busy_ready")
        nmr_ready = sem("nmr_ready")
        var_ready, rstd_ready, xn_ready = sem("var_ready"), sem("rstd_ready"), sem("xn_ready")
        nlog_ready, elog_ready, ae_ready, sin_ready = (
            sem(n) for n in ("nlog_ready", "elog_ready", "ae_ready", "sin_ready"))
        pe_tabs, tabs_ready, xt_ready = sem("pe_tabs"), sem("tabs_ready"), sem("xt_ready")
        bvb_ready = sem("bvb_ready")
        turn_hi, turn_lo = sem("turn_hi"), sem("turn_lo")
        m_hi_ready, m_lo_ready = sem("m_hi_ready"), sem("m_lo_ready")
        wx_hi_ready, wx_lo_ready = sem("wx_hi_ready"), sem("wx_lo_ready")
        pe_turn = sem("pe_turn")
        pe_xh, xh_ready = sem("pe_xh"), sem("xh_ready")
        pe_setup, setup_ready = sem("pe_setup"), sem("setup_ready")
        pe_gate, gate_ready, sq_ready, rt_ready = (
            sem(n) for n in ("pe_gate", "gate_ready", "sq_ready", "rt_ready"))
        h_ready = sem("h_ready")
        wgate_hi, wgate_lo, xh_hi_ready, xh_lo_ready = (
            sem(n) for n in ("wgate_hi", "wgate_lo", "xh_hi_ready", "xh_lo_ready"))
        dx_split, h_hi_ready, h_lo_ready = sem("dx_split"), sem("h_hi_ready"), sem("h_lo_ready")
        pe_x2, x2_ready, xb_ready = sem("pe_x2"), sem("x2_ready"), sem("xb_ready")
        pe_q, q0_ready, q1_ready = sem("pe_q"), sem("q0_ready"), sem("q1_ready")
        pad_ready = sem("pad_ready")
        pe_score, nmax_ready, probs_ready = sem("pe_score"), sem("nmax_ready"), sem("probs_ready")
        pe_pT, pT_ready, pe_z, z_ready = sem("pe_pT"), sem("pT_ready"), sem("pe_z"), sem("z_ready")
        pe_x3, x3_ready = sem("pe_x3"), sem("x3_ready")
        pe_turn3, turn3_ready, pe_logits, lg_ready = (
            sem(n) for n in ("pe_turn3", "turn3_ready", "pe_logits", "lg_ready"))
        dlog_ready, e2_ready = sem("dlog_ready"), sem("e2_ready")
        hot_ready, pe_count, map_ready, pe_map = (
            sem(n) for n in ("hot_ready", "pe_count", "map_ready", "pe_map"))
        xn_hi_ready, xn_split, hot0_ready, map_read = (
            sem(n) for n in ("xn_hi_ready", "xn_split", "hot0_ready", "map_read"))
        rows_b_ready = sem("rows_b_ready")
        gate0_ready, gate_parts, hoth_ready = sem("gate0_ready"), sem("gate_parts"), sem("hoth_ready")
        idx_ready = sem("idx_ready")
        w_hi, w_lo = sem("w_hi"), sem("w_lo")
        got = [sem(f"got{i}") for i in range(2)]
        put = sem("put")
        pe_xeT, xe_hi, xe_lo = sem("pe_xeT"), sem("xe_hi"), sem("xe_lo")
        pe_hid, hid_ready, hid_hi_ready, hid_lo_ready = (
            sem(n) for n in ("pe_hid", "hid_ready", "hid_hi_ready", "hid_lo_ready"))
        pe_y, y_ready = sem("pe_y"), sem("y_ready")

        block = ctx.enter_context(nc.Block())

        def tok(g):
            return slice(g * GT, (g + 1) * GT)

        def row_tok(b):
            return slice(b * S, (b + 1) * S)

        def raw_load(eng, u):
            if u >= RAW:
                eng.wait_ge(w_hi, u - RAW + 1)
                eng.wait_ge(w_lo, u - RAW + 1)
            src = (w1 if u % 2 == 0 else w2)[u // 2]
            eng.dma_start(raw[u % RAW][:, :], src).then_inc(ld_raw[u % RAW], 16)

        def split_of(u):
            hi, lo = ((w1_hi, w1_lo), (w2_hi, w2_lo))[u % 2]
            s = (u // 2) % 2
            flat = "p a b -> p (a b)"
            return hi[s][:, :, :].rearrange(flat), lo[s][:, :, :].rearrange(flat)

        def map_rhs(eng, q0, q1):
            shape = [S, q1 - q0, NH, KB]
            return eng.tensor_tensor(
                rhs[:, q0:q1, :, :],
                hoth[:, :, :, :].rearrange("p e j k -> p (e j) k").unsqueeze(1).to_broadcast(shape),
                tokq[:, q0:q1, :].unsqueeze(2).to_broadcast(shape), ALU.mult)

        @block.sync
        def _(sp):
            sp.dma_start(x_sb[:, 0:2, :], x[:, 0:2, :]).then_inc(ld_x[0], 16)
            sp.dma_start(x_sb[:, 2:4, :], x[:, 2:4, :]).then_inc(ld_x[1], 16)
            sp.dma_start(x_sb[:, 4:B, :], x[:, 4:B, :]).then_inc(ld_x[2], 16)
            sp.dma_start(wl[:, L_X, :, :], w_lru[:, L_X, :, :]).then_inc(ld_wx, 16)
            sp.dma_start(wl[:, L_GX:L_O, :, :], w_lru[:, L_GX:L_O, :, :]).then_inc(ld_gates, 16)
            sp.dma_start(wl[:, L_DX, :, :], w_lru[:, L_DX, :, :]).then_inc(ld_dx, 16)
            sp.dma_start(wl[:, L_O, :, :], w_lru[:, L_O, :, :]).then_inc(ld_dx, 16)
            sp.dma_start(cst[:, P:], consts[:, P:]).then_inc(ld_cst, 16)
            sp.dma_start(wa[:, :, :], w_att).then_inc(ld_att, 16)
            sp.dma_start(yT[:, :, :], y_turned).then_inc(ld_yT, 16)
            sp.dma_start(yr[:, :, :], y_rows).then_inc(ld_yr, 16)
            sp.dma_start(wg_sb[:, :, :], wg).then_inc(ld_moe, 16)
            sp.dma_start(bg_sb[:, :], bg.to_broadcast([S, E])).then_inc(ld_moe, 16)
            sp.dma_start(b2_sb[:, :, :], b2.unsqueeze(0).to_broadcast([HR, E, D])).then_inc(ld_moe, 16)
            sp.wait_ge(pe_xh, 4)
            raw_load(sp, 0)
            raw_load(sp, 1)
            sp.wait_ge(ld_moe, 48)
            sp.dma_start(out[T:OUT_ROWS, :].rearrange("(a p) d -> p a d", p=HR),
                         b2_sb[:, 0:2, :]).then_inc(st_out, 16)
            sp.wait_ge(pe_x2, 4)
            for u in range(2, RAW + 1):
                raw_load(sp, u)
            for g in range(NG):
                bs = slice(g * GB, (g + 1) * GB)
                sp.wait_ge(x3_ready, (g + 1) * GB)
                sp.dma_start(out[tok(g), :].rearrange("(b t) d -> t b d", t=S),
                             x_sb[:, bs, :]).then_inc(st_out, 16)
                sp.wait_ge(xn_ready, 2 * B + (g + 1) * GB)
                sp.dma_start(xn_dram[tok(g), :].rearrange("(b t) d -> t b d", t=S),
                             xn_sb[:, bs, :]).then_inc(st_xn, 16)
            for u in range(RAW + 1, 2 * E):
                raw_load(sp, u)
            sp.wait_ge(st_out, 48)
            sp.wait_ge(st_xn, 32)

        @block.gpsimd
        def _(pool):
            links = [0]

            def link(ins):
                links[0] += 1
                ins.then_inc(p_chain, 1)
                pool.wait_ge(p_chain, links[0])

            def rstd_of(layer, b):
                pool.wait_ge(var_ready, B * layer + b + 1)
                link(pool.tensor_scalar(veps[:, b:b + 1], mv[:, b, 1:2], EPS, None, ALU.add))
                pool.tensor_tensor(rstd[:, b:b + 1], veps[:, b:b + 1], pw[0:S, 0:1], ALU.pow).then_inc(rstd_ready, 1)

            pool.memset(busy[:, :], 1.0).then_inc(busy_ready, 1)
            link(pool.memset(pw[:, :], -0.5))
            link(pool.memset(half[:, :], 0.5))

            def rstd_pair(p):
                pool.wait_ge(var_ready, 2 * p + 2)
                pr = slice(2 * p, 2 * p + 2)
                link(pool.tensor_scalar(veps[:, pr], mv[:, pr, 1], EPS, None, ALU.add))
                pool.tensor_tensor(rstd[:, pr], veps[:, pr], pw[0:S, 0:2], ALU.pow).then_inc(rstd_ready, 2)

            rstd_pair(0)
            pool.wait_ge(ld_vec, 16)
            pool.tensor_scalar(nlog[:, :], vec[:, V_LOGIT:V_LOGIT + 2], -1.0, 80.0,
                               ALU.mult, ALU.min).then_inc(nlog_ready, 1)
            for p in range(1, B // 2):
                rstd_pair(p)
            pool.wait_ge(ae_ready, 1)
            link(pool.tensor_tensor(s_in[:, :], ae[:, :], ae[:, :], ALU.mult))
            link(pool.tensor_scalar(s_in[:, :], s_in[:, :], -1.0, 1.0, ALU.mult, ALU.add))
            pool.tensor_tensor(s_in[:, :], s_in[:, :], half[:, :], ALU.pow).then_inc(sin_ready, 1)
            pool.memset(probs[:, :, C:CP], 0.0).then_inc(pad_ready, 1)
            for i, w in enumerate((L_GA, L_GX)):
                pool.wait_ge(wgate_hi, i + 1)
                pool.tensor_tensor(wl_lo[:, w - 1], wl[:, w], wl_hi[:, w - 1].bitcast(F32),
                                   ALU.subtract).then_inc(wgate_lo, 1)
            pool.wait_ge(tabs_ready, 3)
            for g in range(NG):
                bs = slice(g * GB, (g + 1) * GB)
                pool.wait_ge(xn_ready, (g + 1) * GB)
                pool.tensor_tensor(x_sb[:, bs, :], x_sb[:, bs, :],
                                   dxtab[:, :].unsqueeze(1).to_broadcast([S, GB, D]),
                                   ALU.add).then_inc(xt_ready, 1)
            for b in range(B):
                rstd_of(1, b)
            for g in range(NG):
                bs = slice(g * GB, (g + 1) * GB)
                pool.wait_ge(xn_ready, B + (g + 1) * GB)
                pool.wait_ge(setup_ready, 5)
                pool.tensor_tensor(x_sb[:, bs, :], x_sb[:, bs, :],
                                   brow[:, :].unsqueeze(1).to_broadcast([S, GB, D]),
                                   ALU.add).then_inc(xb_ready, 1)
            def split_rows(b):
                pool.wait_ge(xn_ready, 2 * B + b + 1)
                pool.tensor_copy(xn_hi[:, b, :], xn_sb[:, b, :]).then_inc(xn_hi_ready, 1)
                pool.wait_ge(xn_hi_ready, b + 1)
                pool.tensor_tensor(xn_lo[:, b, :], xn_sb[:, b, :], xn_hi[:, b, :].bitcast(F32),
                                   ALU.subtract).then_inc(xn_split, 1)

            for b in range(B):
                rstd_of(2, b)
                if b >= 2:
                    split_rows(b - 2)
            split_rows(B - 2)
            split_rows(B - 1)

            pool.wait_ge(gate0_ready, 1)
            link(pool.tensor_tensor(gate[:, B:2 * B], gate[:, 0:B], e2[:, :], ALU.mult))
            for n in range(3):
                ins = pool.tensor_copy(tokq[:, 2 + n, :], gate[:, :])
                if n < 2:
                    link(ins)
                    link(pool.tensor_tensor(gate[:, :], gate[:, :], tokq[:, 2 + n, :], ALU.subtract))
            ins.then_inc(gate_parts, 1)
            pool.wait_ge(gate_parts, 1)
            pool.wait_ge(hoth_ready, 1)
            map_rhs(pool, NQ - GQ, NQ).then_inc(map_ready, 1)

            def gather(e):
                if e >= 3:
                    pool.wait_ge(pe_xeT, e - 1)
                for j in range(2):
                    h = 2 * e + j
                    pool.indirect_dma_start(
                        xe[:, e % 2, j, :], None, xn_dram,
                        bass.IndirectOffsetOnAxis(ap=get_idx[:, h:h + 1], axis=0),
                        bounds_check=T - 1, oob_is_err=False).then_inc(got[e % 2], 16)

            def scatter_add(e):
                pool.wait_ge(put, 32 * e) if e else pool.wait_ge(st_out, 48)
                for j in range(2):
                    h = 2 * e + j
                    pool.wait_ge(y_ready, h + 1)
                    pool.indirect_dma_start(
                        out, bass.IndirectOffsetOnAxis(ap=put_idx[:, h:h + 1], axis=0),
                        y_sb[:, e % 2, j, :], None,
                        bounds_check=OUT_ROWS - 1, oob_is_err=True,
                        compute_op=ALU.add).then_inc(put, 16)

            pool.wait_ge(idx_ready, 2)
            pool.wait_ge(st_xn, 32)
            gather(1)
            gather(2)
            for e in range(E):
                if e + 3 < E:
                    gather(e + 3)
                scatter_add(e)
            pool.wait_ge(put, 32 * E)

        @block.scalar
        def _(act):
            links = [0]

            def link(ins):
                links[0] += 1
                ins.then_inc(a_chain, 1)
                act.wait_ge(a_chain, links[0])

            def turn_high(n):
                dst = xnT_hi if n < 2 else qn_hi
                for k in range(KD):
                    act.wait_ge(pe_turn, 2 * n + k + 1)
                    act.activation(dst[:, k, tok(n % 2)], bank[k][:, 0:GT], ACT.Copy).then_inc(turn_hi, 1)

            def turn3_evac(b):
                act.wait_ge(pe_turn3, b + 1)
                act.activation(xnT[:, :, row_tok(b)],
                               bank[2 + b % 2][:, 0:KD * S].rearrange("p (k t) -> p k t", k=KD),
                               ACT.Copy).then_inc(turn3_ready, 1)

            def w_high(u, parts=1, part=0):
                n = KF * D // parts
                cols = slice(part * n, (part + 1) * n)
                act.wait_ge(ld_raw[u % RAW], 16 * (u // RAW + 1))
                if u >= 4:
                    act.wait_ge(pe_hid if u % 2 == 0 else pe_y,
                                (4 if u % 2 == 0 else 2) * (u // 2 - 1))
                ins = act.activation(split_of(u)[0][:, cols], raw[u % RAW][:, cols], ACT.Copy)
                if part == parts - 1:
                    ins.then_inc(w_hi, 1)

            def load_table(i, func):
                act.activation(warm[:, i:i + 1], busy[:, 0:1], func)

            act.dma_start(cst[:, 0:P], consts[:, 0:P]).then_inc(ld_ident, 16)
            act.dma_start(vec[:, :], vectors).then_inc(ld_vec, 16)
            act.dma_start(rows_sb[:, :], rows).then_inc(ld_rows, 16)
            act.wait_ge(busy_ready, 1)
            load_table(0, ACT.Exp)

            def ln_scale(b):
                act.wait_ge(nmr_ready, b // 2 + 1)
                act.activation(xn_sb[:, b, :], x_sb[:, b, :], ACT.Identity, bias=nmr[:, b:b + 1],
                               scale=rstd[:, b:b + 1]).then_inc(xn_ready, 1)

            ln_scale(0)
            ln_scale(1)
            act.wait_ge(nlog_ready, 1)
            act.activation(nlog[:, :], nlog[:, :], ACT.Exp).then_inc(elog_ready, 1)
            ln_scale(2)
            ln_scale(3)
            act.wait_ge(ld_wx, 16)
            act.activation(wx_hi[:, :, :], wl[:, L_X, :, :], ACT.Copy).then_inc(wx_hi_ready, 1)
            turn_high(0)
            for b in range(GB, B):
                ln_scale(b)
            def gate_high(w):
                act.activation(wl_hi[:, w - 1], wl[:, w], ACT.Copy).then_inc(wgate_hi, 1)

            act.wait_ge(ld_gates, 16)
            gate_high(L_GA)
            turn_high(1)
            gate_high(L_GX)

            def xh_high(n):
                act.wait_ge(xh_ready, n + 1)
                act.activation(xh_hi[:, n % 2, tok(n // 2)], xh[:, n % 2, tok(n // 2)], ACT.Copy).then_inc(xh_hi_ready, 1)

            xh_high(0)
            xh_high(1)
            load_table(1, ACT.Sigmoid)
            xh_high(2)
            xh_high(3)
            for n in range(2 * NG):
                g, m = n // 2, n % 2
                act.wait_ge(pe_gate, n + 1)
                act.activation(ga[:, m, tok(g)], bank[n][:, 0:GT], ACT.Sigmoid,
                               bias=vec[:, V_BGA + m:V_BGA + m + 1]).then_inc(gate_ready, 1)
                act.wait_ge(gate_ready, n + 1)
                act.activation(rt[:, m, tok(g)], ga[:, m, tok(g)], ACT.Square,
                               scale=ae[:, m:m + 1]).then_inc(sq_ready, 1)
            for n in range(2 * NG):
                act.wait_ge(sq_ready, n + 1)
                act.activation(rt[:, n % 2, tok(n // 2)], rt[:, n % 2, tok(n // 2)], ACT.Sqrt,
                               bias=1.0, scale=-1.0).then_inc(rt_ready, 1)
            load_table(2, ACT.Sigmoid)
            for n in range(2 * NG):
                g, m = n // 2, n % 2
                act.wait_ge(pe_gate, 2 * NG + n + 1)
                act.activation(gx[:, m, tok(g)], bank[n][:, 0:GT], ACT.Sigmoid,
                               bias=vec[:, V_BGX + m:V_BGX + m + 1]).then_inc(gate_ready, 1)

            def h_high(n):
                h = (slice(None), n % 2, tok(n // 2))
                act.wait_ge(h_ready, n + 1)
                act.activation(xh_hi[h], xh[h], ACT.Copy).then_inc(h_hi_ready, 1)

            h_high(0)
            h_high(1)
            act.wait_ge(pe_setup, 1)
            act.activation(m_hi[:, :, :], bank[6][:, 0:KD * DA], ACT.Copy).then_inc(m_hi_ready, 1)
            act.activation(qb[:, 0:1], bank[6][:, 400:401], ACT.Copy)
            act.activation(qb[0:DB, 1:2], bank[6][0:DB, 401:402], ACT.Copy)
            act.activation(qbs[:, 0:1], bank[6][:, 400:401], ACT.Copy, scale=SCALE)
            act.activation(qbs[0:DB, 1:2], bank[6][0:DB, 401:402], ACT.Copy, scale=SCALE).then_inc(setup_ready, 1)
            act.wait_ge(pe_setup, 2)
            act.activation(wvo[:, 0, :], bank[7][:, 0:D], ACT.Copy).then_inc(setup_ready, 1)
            act.activation(wvo[0:DC - P, 1, :], bank[7][0:DC - P, D:2 * D], ACT.Copy).then_inc(setup_ready, 1)
            h_high(2)
            h_high(3)
            act.wait_ge(pe_setup, 3)
            act.activation(brow[:, :], bank[0][0:S, 0:D], ACT.Copy).then_inc(setup_ready, 2)

            load_table(3, ACT.Exp)

            def q_evac(g):
                act.wait_ge(pe_q, 2 * g + 2)
                act.activation(qT[0:DB, 1, tok(g)], bank[3][0:DB, 0:GT], ACT.Identity,
                               bias=qbs[0:DB, 1:2], scale=SCALE).then_inc(q1_ready, 1)

            def exp_of(b):
                act.wait_ge(nmax_ready, b + 1)
                if b >= 2:
                    act.wait_ge(pe_pT, b - 1)
                act.activation(probs[:, b % 2, 0:C], bank[4 + b % 2][0:S, 0:C], ACT.Exp,
                               bias=nmax[:, b:b + 1], accum_out=psums[:, b:b + 1]).then_inc(probs_ready, 1)

            turn_high(2)
            q_evac(0)
            act.wait_ge(pad_ready, 1)
            act.wait_ge(pe_x2, 4)
            w_high(0)
            exp_of(0)
            turn_high(3)
            for b in range(B):
                act.wait_ge(pe_pT, b + 1)
                if b >= 2:
                    act.wait_ge(pe_z, b - 1)
                act.activation(pT[:, b % 2, :], bank[6][0:CR, 0:NC * S], ACT.Copy).then_inc(pT_ready, 1)
                if b + 1 < B:
                    exp_of(b + 1)
                if 1 <= b <= 4:
                    w_high(1, 4, b - 1)
                if b >= 5:
                    w_high(2, 4, b - 5)
                act.wait_ge(pe_z, b + 1)
                if b >= 2:
                    act.wait_ge(pe_x3, b - 1)
                act.activation(zT[:, b % 2, 0, :], bank[7][:, 0:S], ACT.Copy)
                act.activation(zT[0:DC - P, b % 2, 1, :], bank[7][0:DC - P, S:2 * S],
                               ACT.Copy).then_inc(z_ready, 1)
                if b == 0:
                    q_evac(1)
                if b >= 2:
                    turn3_evac(b - 2)
            turn3_evac(B - 2)
            act.wait_ge(ld_cst, 16)
            act.wait_ge(pe_x3, B)
            act.activation(rows_b[:, :, :], cst[0:S, C_ROW:C_ROW + HR].unsqueeze(2).to_broadcast([S, HR, KB]),
                           ACT.Copy).then_inc(rows_b_ready, 1)
            turn3_evac(B - 1)
            w_high(2, 4, 3)
            act.wait_ge(dlog_ready, 1)
            act.activation(e2[:, :], dlog[:, :], ACT.Exp).then_inc(e2_ready, 1)
            load_table(4, ACT.Gelu_apprx_tanh)
            def xe_high(e):
                act.wait_ge(pe_xeT, e + 1)
                if e >= 2:
                    act.wait_ge(pe_hid, 4 * (e - 1))
                act.activation(xeT_hi[e % 2][:, :, :], bank[6 + e % 2][:, 0:KD * CAP],
                               ACT.Copy).then_inc(xe_hi, 1)

            def hidden(e):
                for f in range(KF):
                    act.wait_ge(pe_hid, 4 * e + f // 2 + 1)
                    if e >= 1:
                        act.wait_ge(hid_lo_ready, 2 * (e - 1) + f // 4 + 1)
                    act.activation(hid[:, f, :], bank[f // 2][:, (f % 2) * CAP:(f % 2 + 1) * CAP],
                                   ACT.Gelu_apprx_tanh,
                                   bias=vec[:, V_B1 + e * KF + f:V_B1 + e * KF + f + 1]).then_inc(hid_ready, 1)
                    if f % 4 == 3:
                        act.wait_ge(hid_ready, KF * e + f + 1)
                        if e >= 2:
                            act.wait_ge(pe_y, 2 * (e - 1))
                        act.activation(hid_hi[e % 2][:, f - 3:f + 1, :], hid[:, f - 3:f + 1, :],
                                       ACT.Copy).then_inc(hid_hi_ready, 1)

            xe_high(0)
            hidden(0)
            xe_high(1)
            w_high(3)
            w_high(4)
            xe_high(2)
            hidden(1)
            for e in range(1, E):
                if e + 2 < E:
                    xe_high(e + 2)
                if e + 1 < E:
                    w_high(2 * (e + 1) + 1)
                if e + 2 < E:
                    w_high(2 * (e + 2))
                if e + 1 < E:
                    hidden(e + 1)

        @block.tensor
        def _(pe):
            def keep_clock(n, at):
                for _ in range(n):
                    pe.matmul(bank[at][:, 0:P], busy[:, :], busy[:, :], start=True, stop=True)

            def turn(n, banks):
                g = n % 2
                for b in range(GB):
                    if n == 0:
                        keep_clock(KW_TURN[b], 6)
                    pe.wait_ge(xn_ready, B * (n // 2) + g * GB + b + 1)
                    for k in range(KD):
                        mm = pe.transpose(banks[k][:, row_tok(b)], xn_sb[:, g * GB + b, k * P:(k + 1) * P],
                                          ident[0:S, 0:S])
                        if b == GB - 1:
                            mm.then_inc(pe_turn, 1)

            def split_mm(dst, a, b, first, last, **kw):
                pe.matmul(dst, a[0], b[0], start=first, stop=False, **kw)
                pe.matmul(dst, a[0], b[1], start=False, stop=False, **kw)
                return pe.matmul(dst, a[1], b[0], start=False, stop=last, **kw)

            pe.wait_ge(busy_ready, 1)
            keep_clock(KW_START, 6)
            pe.wait_ge(ld_ident, 16)
            turn(0, bank[0:2])
            pe.wait_ge(ld_rows, 16)
            for m in range(2):
                pe.matmul(bank[7][:, m * S:(m + 1) * S], rows_sb[0:PE_DIM + 1, R_WX + m * P:R_WX + (m + 1) * P],
                          rows_sb[0:PE_DIM + 1, R_PE:R_PE + S], start=True, stop=True)
            pe.matmul(bank[7][0:S, D:2 * D], rows_sb[:, R_PE:R_PE + S], rows_sb[:, R_WDX:R_WDX + D],
                      start=True, stop=True).then_inc(pe_tabs, 1)

            def xh_products(g, m):
                dst, ms = bank[2 + 2 * g + m][:, 0:GT], slice(m * P, (m + 1) * P)
                pe.wait_ge(wx_hi_ready, 1)
                for k in range(KD):
                    pe.wait_ge(turn_hi, 2 * g + k + 1)
                    pe.matmul(dst, wx_hi[:, k, ms], xnT_hi[:, k, tok(g)], start=k == 0, stop=False)
                pe.wait_ge(wx_lo_ready, 1)
                for k in range(KD):
                    pe.matmul(dst, wx_lo[:, k, ms], xnT_hi[:, k, tok(g)], start=False, stop=False)
                for k in range(KD):
                    pe.wait_ge(turn_lo, 2 * g + k + 1)
                    mm = pe.matmul(dst, wx_hi[:, k, ms], xnT_lo[:, k, tok(g)], start=False, stop=k == KD - 1)
                mm.then_inc(pe_xh, 1)

            xh_products(0, 0)
            turn(1, bank[0:2])
            xh_products(0, 1)
            xh_products(1, 0)
            xh_products(1, 1)

            def gate_products(w, g):
                pe.wait_ge(xh_lo_ready, 2 * g + 2)
                pe.wait_ge(wgate_lo, 1 if w == L_GA else 2)
                for m in range(2):
                    n = 2 * g + m
                    if w == L_GX:
                        pe.wait_ge(gate_ready, n + 1)
                    for k in range(KD):
                        ms = slice(m * P, (m + 1) * P)
                        mm = split_mm(bank[n][:, 0:GT], (wl_hi[:, w - 1, k, ms], wl_lo[:, w - 1, k, ms]),
                                      (xh_hi[:, k, tok(g)], xh_lo[:, k, tok(g)]), k == 0, k == KD - 1)
                    mm.then_inc(pe_gate, 1)

            def dx_products(pair):
                pe.wait_ge(dx_split, 2)
                if pair >= 2:
                    pe.wait_ge(setup_ready, 5)
                    pe.wait_ge(m_lo_ready, 1)
                for i in range(2):
                    for k in range(KD):
                        t = row_tok(2 * pair + i)
                        split_mm(bank[4 + pair][0:S, i * D:(i + 1) * D], (xnT_hi[:, k, t], xnT_lo[:, k, t]),
                                 (wl_hi[:, L_DX - 1, k, :], wl_lo[:, L_DX - 1, k, :]), i == 0 and k == 0, False,
                                 skip_group_check=True)

            def h_products(pair):
                pe.wait_ge(h_lo_ready, 2 * (pair // 2) + 2)
                for i in range(2):
                    for k in range(KD):
                        t = row_tok(2 * pair + i)
                        mm = split_mm(bank[4 + pair][0:S, i * D:(i + 1) * D], (xh_hi[:, k, t], xh_lo[:, k, t]),
                                      (wl_hi[:, L_O - 1, k, :], wl_lo[:, L_O - 1, k, :]), False,
                                      i == 1 and k == KD - 1, skip_group_check=True)
                mm.then_inc(pe_x2, 1)

            for w in (L_GA, L_GX):
                for g in range(NG):
                    gate_products(w, g)

            pe.wait_ge(ld_att, 16)
            for m in range(KD):
                for k in range(KD):
                    pe.matmul(bank[6][:, m * DA:(m + 1) * DA], wa[:, k, A_WQ + m * P:A_WQ + (m + 1) * P],
                              wa[:, k, A_WK:A_WK + DA], start=k == 0, stop=k == KD - 1)
            for m, n in ((0, P), (1, DB)):
                for k in range(KD):
                    mm = pe.matmul(bank[6][0:n, 400 + m:401 + m], wa[:, k, A_WK + m * P:A_WK + m * P + n],
                                   vec[:, V_BQ + k:V_BQ + k + 1], start=k == 0, stop=k == KD - 1)
            mm.then_inc(pe_setup, 1)
            pe.wait_ge(tabs_ready, 3)
            for m, n in ((0, P), (1, DC - P)):
                for k in range(KD):
                    mm = pe.matmul(bank[7][0:n, m * D:(m + 1) * D], wa[:, k, A_WV + m * P:A_WV + m * P + n],
                                   wa[:, k, A_WO:A_WO + D], start=k == 0, stop=k == KD - 1)
            mm.then_inc(pe_setup, 1)
            pe.wait_ge(bvb_ready, 1)
            pe.wait_ge(gate_ready, 5)
            for k in range(KD):
                pe.matmul(bank[0][0:S, 0:D], bvb[:, k, :], wa[:, k, A_WO:A_WO + D], start=k == 0, stop=False)
            pe.wait_ge(ld_cst, 16)
            pe.matmul(bank[0][0:S, 0:D], ones[0:1, 0:S], rows_sb[0:1, R_BO:R_BO + D],
                      start=False, stop=True).then_inc(pe_setup, 1)

            dx_products(0)
            dx_products(1)
            h_products(0)
            h_products(1)
            dx_products(2)
            dx_products(3)
            h_products(2)
            pe.wait_ge(gate_ready, 8)
            turn(2, bank[0:2])
            h_products(3)

            def q_products(g):
                n = 2 + g
                if g == 1:
                    pe.wait_ge(q0_ready, 1)
                    pe.wait_ge(q1_ready, 1)
                pe.wait_ge(m_lo_ready, 1)
                for m, c in ((0, P), (1, DB)):
                    dst, ms, t = bank[2 + m][0:c, 0:GT], slice(m * P, m * P + c), tok(g)
                    for k in range(KD):
                        pe.wait_ge(turn_hi, 2 * n + k + 1)
                        pe.matmul(dst, m_hi[:, k, ms], qn_hi[:, k, t], start=k == 0, stop=False)
                    for k in range(KD):
                        pe.matmul(dst, m_lo[:, k, ms], qn_hi[:, k, t], start=False, stop=False)
                    for k in range(KD):
                        pe.wait_ge(turn_lo, 2 * n + k + 1)
                        mm = pe.matmul(dst, m_hi[:, k, ms], qn_lo[:, k, t], start=False, stop=k == KD - 1)
                    mm.then_inc(pe_q, 1)

            def scores(b):
                if b >= 2:
                    pe.wait_ge(probs_ready, b - 1)
                else:
                    pe.wait_ge(x2_ready, 4)
                pe.wait_ge(q0_ready, b // GB + 1)
                pe.wait_ge(q1_ready, b // GB + 1)
                for m, n in ((0, P), (1, DB)):
                    mm = pe.matmul(bank[4 + b % 2][0:S, 0:CE], qT[0:n, m, row_tok(b)],
                                   yT[0:n, m, b * CE:(b + 1) * CE], start=m == 0, stop=m == 1)
                mm.then_inc(pe_score, 1)

            def turn_probs(b):
                pe.wait_ge(probs_ready, b + 1)
                if b >= 1:
                    pe.wait_ge(pT_ready, b)
                for c in range(NC):
                    mm = pe.transpose(bank[6][0:CR, c * S:(c + 1) * S], probs[:, b % 2, c * CR:(c + 1) * CR],
                                      ident[0:S, 0:S])
                mm.then_inc(pe_pT, 1)

            def mix(b):
                pe.wait_ge(pT_ready, b + 1)
                if b >= 1:
                    pe.wait_ge(z_ready, b)
                for m, n in ((0, P), (1, DC - P)):
                    for c in range(NC):
                        mm = pe.matmul(bank[7][0:n, m * S:(m + 1) * S], yr[:, b * NC + c, m * P:m * P + n],
                                       pT[:, b % 2, c * S:(c + 1) * S], start=c == 0, stop=c == NC - 1)
                mm.then_inc(pe_z, 1)

            def project(b):
                pe.wait_ge(z_ready, b + 1)
                if b >= 2:
                    pe.wait_ge(x3_ready, b - 1)
                for m, n in ((0, P), (1, DC - P)):
                    mm = pe.matmul(bank[b % 2][0:S, 0:D], zT[0:n, b % 2, m, :], wvo[0:n, m, :],
                                   start=m == 0, stop=m == 1)
                mm.then_inc(pe_x3, 1)

            def turn3(b):
                if b < 2:
                    pe.wait_ge(q0_ready, 2)
                    pe.wait_ge(q1_ready, 2)
                else:
                    pe.wait_ge(lg_ready, b - 1)
                pe.wait_ge(xn_ready, 2 * B + b + 1)
                for k in range(KD):
                    mm = pe.transpose(bank[2 + b % 2][:, k * S:(k + 1) * S], xn_sb[:, b, k * P:(k + 1) * P],
                                      ident[0:S, 0:S])
                mm.then_inc(pe_turn3, 1)

            def logits(b):
                pe.wait_ge(ld_moe, 48)
                pe.wait_ge(turn3_ready, b + 1)
                c = KD * S
                for k in range(KD):
                    mm = pe.matmul(bank[2 + b % 2][0:S, c:c + E], xnT[:, k, row_tok(b)], wg_sb[:, k, :],
                                   start=k == 0, stop=k == KD - 1)
                mm.then_inc(pe_logits, 1)

            q_products(0)
            pe.wait_ge(ld_yT, 16)
            scores(0)
            scores(1)
            turn(3, bank[0:2])
            pe.wait_ge(ld_yr, 16)
            for b in range(B):
                turn_probs(b)
                if b + 2 < B:
                    scores(b + 2)
                if b >= 3:
                    logits(b - 3)
                if b >= 1:
                    project(b - 1)
                mix(b)
                if b == 0:
                    q_products(1)
                if b >= 2:
                    turn3(b - 2)
            project(B - 1)
            logits(B - 3)
            keep_clock(KW_TAIL[0], 4)
            turn3(B - 2)
            keep_clock(KW_TAIL[1], 4)
            logits(B - 2)
            keep_clock(KW_TAIL[2], 4)
            turn3(B - 1)
            keep_clock(KW_TAIL[3], 4)
            logits(B - 1)
            keep_clock(KW_TAIL[4], 4)
            pe.wait_ge(hot_ready, 1)
            hots = hot[:, :, :].rearrange("p e k -> p (e k)")
            pe.matmul(bank[5][0:S, 0:P], lm_b[:, :], hots, start=True, stop=True)
            pe.matmul(bank[5][0:S, P:2 * P], one_b[:, :], hots, start=True, stop=True).then_inc(pe_count, 1)
            keep_clock(KW_TAIL[5], 4)
            for b in range(B):
                pe.wait_ge(xn_split, b + 1)
                pe.wait_ge(hot0_ready, b + 1)
                for part, src in ((6, xn_hi), (7, xn_lo)):
                    for k in range(KD):
                        mm = pe.matmul(bank[part][:, k * CAP:(k + 1) * CAP], src[:, b, k * P:(k + 1) * P],
                                       hot0[0:S, b, :], start=b == 0 and k == 0, stop=b == B - 1,
                                       skip_group_check=True)
            mm.then_inc(pe_xeT, 1)
            keep_clock(KW_TAIL[6], 4)

            def map_rows():
                pe.wait_ge(map_ready, 2)
                for n in range(KB):
                    mm = pe.matmul(bank[4][0:HR, 0:NQ * NH], hotl[:, :, n],
                                   rhs[:, :, :, n].rearrange("p q h -> p (q h)"), start=n == 0, stop=n == KB - 1)
                mm.then_inc(pe_map, 1)

            def turn_rows(e):
                pe.wait_ge(got[e % 2], 32 * ((e + 1) // 2))
                if e == 1:
                    pe.wait_ge(xe_lo, 1)
                else:
                    pe.wait_ge(xe_lo, e - 1)
                for k in range(KD):
                    for j in range(2):
                        mm = pe.transpose(bank[6 + e % 2][:, k * CAP + j * HR:k * CAP + (j + 1) * HR],
                                          xe[:, e % 2, j, k * P:(k + 1) * P], ident[0:HR, 0:HR])
                mm.then_inc(pe_xeT, 1)

            def up(e):
                pe.wait_ge(xe_hi, e + 1)
                pe.wait_ge(xe_lo, e + 1)
                pe.wait_ge(w_lo, 2 * e + 1)
                s = e % 2
                for f in range(KF):
                    if e == 0 and f == 4:
                        map_rows()
                    if e >= 1 and f % 2 == 0:
                        pe.wait_ge(hid_ready, KF * (e - 1) + f + 2)
                    for k in range(KD):
                        fs = slice(f * P, (f + 1) * P)
                        mm = split_mm(bank[f // 2][:, (f % 2) * CAP:(f % 2 + 1) * CAP],
                                      (w1_hi[s][:, k, fs], w1_lo[s][:, k, fs]),
                                      (xeT_hi[s][:, k, :], xeT_lo[s][:, k, :]), k == 0, k == KD - 1)
                    if f % 2 == 1:
                        mm.then_inc(pe_hid, 1)

            def down(e, j, f0, f1):
                if f0 == 0 and e >= 1:
                    pe.wait_ge(y_ready, 2 * (e - 1) + j + 1)
                hs = slice(j * HR, (j + 1) * HR)
                for f in range(f0, f1):
                    if j == 0 and f % 4 == 0:
                        pe.wait_ge(hid_lo_ready, 2 * e + f // 4 + 1)
                    mm = split_mm(bank[4 + j][0:HR, 0:D], (hid_hi[e % 2][:, f, hs], hid_lo[e % 2][:, f, hs]),
                                  (w2_hi[e % 2][:, f, :], w2_lo[e % 2][:, f, :]), f == 0, f == KF - 1)
                if f1 == KF:
                    mm.then_inc(pe_y, 1)

            up(0)
            pe.wait_ge(w_lo, 2)
            pe.wait_ge(map_read, 1)
            down(0, 0, 0, KF // 2)
            down(0, 1, 0, KF // 2)
            turn_rows(1)
            down(0, 0, KF // 2, KF)
            down(0, 1, KF // 2, KF)
            turn_rows(2)
            up(1)
            for e in range(1, E):
                if e + 2 < E:
                    turn_rows(e + 2)
                if e + 1 < E:
                    up(e + 1)
                pe.wait_ge(w_lo, 2 * e + 2)
                down(e, 0, 0, KF)
                down(e, 1, 0, KF)

        @block.vector
        def _(dve):
            links = [0]

            def link(ins):
                links[0] += 1
                ins.then_inc(v_chain, 1)
                dve.wait_ge(v_chain, links[0])

            def ln_stats(layer, b):
                link(dve.bn_stats(stats[:, b, :], x_sb[:, b, :]))
                dve.bn_aggr(mv[:, b, :], stats[:, b, :]).then_inc(var_ready, 1)

            def ln_scale(layer, b):
                dve.wait_ge(rstd_ready, B * layer + b + 1)
                dve.tensor_scalar(xn_sb[:, b, :], x_sb[:, b, :], mv[:, b, 0:1], rstd[:, b:b + 1],
                                  ALU.subtract, ALU.mult).then_inc(xn_ready, 1)

            def w_low(u, parts=1, part=0):
                n = KF * D // parts
                cols = slice(part * n, (part + 1) * n)
                dve.wait_ge(w_hi, u + 1)
                hi, lo = split_of(u)
                ins = dve.tensor_tensor(lo[:, cols], raw[u % RAW][:, cols], hi[:, cols].bitcast(F32), ALU.subtract)
                if part == parts - 1:
                    ins.then_inc(w_lo, 1)

            def turn_low(n):
                hi, lo = (xnT_hi, xnT_lo) if n < 2 else (qn_hi, qn_lo)
                for k in range(KD):
                    dve.wait_ge(turn_hi, 2 * n + k + 1)
                    dve.tensor_tensor(lo[:, k, tok(n % 2)], bank[k][:, 0:GT], hi[:, k, tok(n % 2)].bitcast(F32),
                                      ALU.subtract).then_inc(turn_lo, 1)

            def stats_pair(p):
                if p < 3:
                    dve.wait_ge(ld_x[p], 16)
                dve.bn_stats(stats[:, 2 * p, :], x_sb[:, 2 * p, :])
                link(dve.bn_stats(stats[:, 2 * p + 1, :], x_sb[:, 2 * p + 1, :]))
                for b in (2 * p, 2 * p + 1):
                    dve.bn_aggr(mv[:, b, :], stats[:, b, :]).then_inc(var_ready, 1)

            def bias_pair(p):
                dve.wait_ge(rstd_ready, 2 * p + 2)
                pr = slice(2 * p, 2 * p + 2)
                dve.scalar_tensor_tensor(nmr[:, pr], mv[:, pr, 0], -1.0, rstd[:, pr],
                                         ALU.mult, ALU.mult).then_inc(nmr_ready, 1)

            stats_pair(0)
            stats_pair(1)
            bias_pair(0)
            stats_pair(2)
            bias_pair(1)
            stats_pair(3)
            bias_pair(2)
            dve.wait_ge(elog_ready, 1)
            link(dve.tensor_scalar(nlog[:, :], nlog[:, :], 1.0, None, ALU.add))
            dve.reciprocal(ae[:, :], nlog[:, :]).then_inc(ae_ready, 1)
            dve.wait_ge(wx_hi_ready, 1)
            dve.tensor_tensor(wx_lo[:, :, :], wl[:, L_X, :, :], wx_hi[:, :, :].bitcast(F32),
                              ALU.subtract).then_inc(wx_lo_ready, 1)
            bias_pair(3)
            turn_low(0)
            dve.wait_ge(pe_tabs, 1)
            dve.wait_ge(sin_ready, 1)
            for m in range(2):
                dve.tensor_scalar(xtab[:, m, :], bank[7][:, m * S:(m + 1) * S], s_in[:, m:m + 1], None,
                                  ALU.mult).then_inc(tabs_ready, 1)
            def xh_low(n):
                dve.wait_ge(xh_hi_ready, n + 1)
                h = (slice(None), n % 2, tok(n // 2))
                dve.tensor_tensor(xh_lo[h], xh[h], xh_hi[h].bitcast(F32), ALU.subtract).then_inc(xh_lo_ready, 1)

            def xh_evac(n):
                m, t = n % 2, tok(n // 2)
                dve.wait_ge(pe_xh, n + 1)
                dve.scalar_tensor_tensor(
                    xh[:, m, t].rearrange("p (b t) -> p b t", t=S),
                    bank[2 + n][:, 0:GT].rearrange("p (b t) -> p b t", t=S),
                    s_in[:, m:m + 1], xtab[:, m, :].unsqueeze(1).to_broadcast([P, GB, S]),
                    ALU.mult, ALU.add).then_inc(xh_ready, 1)

            dve.wait_ge(tabs_ready, 2)
            xh_evac(0)
            turn_low(1)
            xh_evac(1)
            xh_low(0)
            xh_low(1)
            xh_evac(2)
            xh_evac(3)
            xh_low(2)
            xh_low(3)
            dve.tensor_scalar(dxtab[:, :], bank[7][0:S, D:2 * D], 0.5, None, ALU.mult).then_inc(tabs_ready, 1)
            for k in range(KD):
                ins = dve.tensor_copy(bvb[:, k, :], vec[:, V_BV + k:V_BV + k + 1].to_broadcast([P, S]))
            ins.then_inc(bvb_ready, 1)
            dve.wait_ge(ld_dx, 32)
            for w in (L_DX, L_O):
                link(dve.tensor_copy(wl_hi[:, w - 1], wl[:, w]))
                dve.tensor_tensor(wl_lo[:, w - 1], wl[:, w], wl_hi[:, w - 1].bitcast(F32),
                                  ALU.subtract).then_inc(dx_split, 1)
            for n in range(2 * NG):
                m, t = n % 2, tok(n // 2)
                dve.wait_ge(sq_ready, n + 1)
                link(dve.tensor_scalar(ga[:, m, t], ga[:, m, t], ae[:, m:m + 1], None, ALU.mult))
                dve.memset(ga[:, m, t][:, 0:GT:S], 0.0)
            for n in range(2 * NG):
                m, t = n % 2, tok(n // 2)
                dve.wait_ge(rt_ready, n + 1)
                link(dve.tensor_tensor(rt[:, m, t], rt[:, m, t], xh[:, m, t], ALU.mult))

            def h_low(n):
                h = (slice(None), n % 2, tok(n // 2))
                dve.wait_ge(h_hi_ready, n + 1)
                dve.tensor_tensor(xh_lo[h], xh[h], xh_hi[h].bitcast(F32), ALU.subtract).then_inc(h_lo_ready, 1)

            for n in range(2 * NG):
                m, t = n % 2, tok(n // 2)
                dve.wait_ge(gate_ready, 2 * NG + n + 1)
                link(dve.tensor_tensor(gx[:, m, t], gx[:, m, t], rt[:, m, t], ALU.mult))
                dve.tensor_tensor_scan(xh[:, m, t], ga[:, m, t], gx[:, m, t], 0.0,
                                       ALU.mult, ALU.add).then_inc(h_ready, 1)
                if n >= 1:
                    h_low(n - 1)
            h_low(2 * NG - 1)

            def x2_evac(pair):
                dve.wait_ge(pe_x2, pair + 1)
                dve.wait_ge(xt_ready, pair // 2 + 1)
                xp = x_sb[:, 2 * pair:2 * pair + 2, :].rearrange("p b d -> p (b d)")
                dve.scalar_tensor_tensor(xp, bank[4 + pair][0:S, :], 0.5, xp,
                                         ALU.mult, ALU.add).then_inc(x2_ready, 1)
                dve.wait_ge(x2_ready, pair + 1)

            def q_evac(g):
                dve.wait_ge(pe_q, 2 * g + 1)
                dve.wait_ge(setup_ready, 1)
                dve.tensor_scalar(qT[:, 0, tok(g)], bank[2][:, 0:GT], qb[:, 0:1], SCALE,
                                  ALU.add, ALU.mult).then_inc(q0_ready, 1)

            def row_max(b):
                dve.wait_ge(pe_score, b + 1)
                dve.tensor_reduce(nmax[:, b:b + 1], bank[4 + b % 2][0:S, 0:C], AX.X, ALU.max,
                                  negate=True).then_inc(nmax_ready, 1)

            def x3_evac(b):
                dve.wait_ge(pe_x3, b + 1)
                dve.wait_ge(xb_ready, b // GB + 1)
                link(dve.reciprocal(rsum[:, b:b + 1], psums[:, b:b + 1]))
                dve.scalar_tensor_tensor(x_sb[:, b, :], bank[b % 2][0:S, 0:D], rsum[:, b:b + 1], x_sb[:, b, :],
                                         ALU.mult, ALU.add).then_inc(x3_ready, 1)
                dve.wait_ge(x3_ready, b + 1)
                ln_stats(2, b)

            def logits_out(b):
                dve.wait_ge(pe_logits, b + 1)
                c = KD * S
                dve.tensor_tensor(lg[:, b, :], bank[2 + b % 2][0:S, c:c + E], bg_sb[:, :],
                                  ALU.add).then_inc(lg_ready, 1)

            def best(b):
                dve.wait_ge(lg_ready, b + 1)
                link(dve.max(top[:, b, :], lg[:, b, :]))
                dve.max_index(topi[:, b, :], top[:, b, :], lg[:, b, :])

            dve.wait_ge(m_hi_ready, 1)
            dve.tensor_tensor(m_lo[:, :, :].rearrange("p k c -> p (k c)"), bank[6][:, 0:KD * DA],
                              m_hi[:, :, :].rearrange("p k c -> p (k c)").bitcast(F32),
                              ALU.subtract).then_inc(m_lo_ready, 1)
            x2_evac(0)
            ln_stats(1, 0)
            ln_stats(1, 1)
            x2_evac(1)
            ln_scale(1, 0)
            ln_stats(1, 2)
            ln_scale(1, 1)
            ln_stats(1, 3)
            ln_scale(1, 2)
            ln_scale(1, 3)
            x2_evac(2)
            turn_low(2)
            ln_stats(1, 4)
            ln_stats(1, 5)
            q_evac(0)
            x2_evac(3)
            ln_scale(1, 4)
            ln_stats(1, 6)
            ln_scale(1, 5)
            ln_stats(1, 7)
            row_max(0)
            ln_scale(1, 6)
            ln_scale(1, 7)
            row_max(1)
            turn_low(3)
            for b in range(B):
                if b == 1:
                    q_evac(1)
                if b + 2 < B:
                    row_max(b + 2)
                if b >= 1:
                    w_low((b - 1) // 4, 4, (b - 1) % 4)
                if b >= 2:
                    ln_scale(2, b - 2)
                if b >= 4:
                    logits_out(b - 4)
                    best(b - 4)
                if b >= 1:
                    x3_evac(b - 1)
            ln_scale(2, B - 2)
            logits_out(B - 4)
            x3_evac(B - 1)
            best(B - 4)
            logits_out(B - 3)
            ln_scale(2, B - 1)
            best(B - 3)
            dve.wait_ge(ld_cst, 16)
            dve.tensor_copy(lm_b[:, :], cst[0:S, C_LM:C_LM + S])
            dve.tensor_copy(one_b[:, :], cst[0:S, C_ONE:C_ONE + S])
            logits_out(B - 2)
            best(B - 2)
            dve.tensor_copy(tokq[:, 0, :], cst[0:S, C_TOKH:C_TOKH + KB])
            logits_out(B - 1)
            best(B - 1)

            def xe_low(e):
                if e == 0:
                    dve.wait_ge(pe_xeT, 1)
                    dve.tensor_copy(xeT_lo[0][:, :, :], bank[7][:, 0:KD * CAP].rearrange(
                        "p (k r) -> p k r", k=KD)).then_inc(xe_lo, 1)
                    return
                dve.wait_ge(xe_hi, e + 1)
                dve.tensor_tensor(xeT_lo[e % 2][:, :, :], bank[6 + e % 2][:, 0:KD * CAP].rearrange(
                    "p (k r) -> p k r", k=KD), xeT_hi[e % 2][:, :, :].bitcast(F32), ALU.subtract).then_inc(xe_lo, 1)

            dve.tensor_tensor(dlog[:, :], top[:, :, 1], top[:, :, 0], ALU.subtract).then_inc(dlog_ready, 1)
            dve.wait_ge(dlog_ready, 1)
            link(dve.tensor_copy(chosen[:, :].rearrange("p (k b) -> p k b", k=TOPK),
                                 topi[:, :, 0:TOPK].rearrange("p b k -> p k b")))
            dve.tensor_tensor(hot[:, :, :], chosen[:, :].unsqueeze(1).to_broadcast([S, E, KB]),
                              cst[0:S, C_EXP:C_EXP + E * KB].rearrange("p (e k) -> p e k", e=E),
                              ALU.is_equal).then_inc(hot_ready, 1)
            dve.wait_ge(e2_ready, 1)
            link(dve.tensor_scalar(den[:, :], e2[:, :], 1.0, None, ALU.add))
            dve.reciprocal(gate[:, 0:B], den[:, :]).then_inc(gate0_ready, 1)
            def rows_of(e0, e1):
                ks = slice(e0 * KB, e1 * KB)
                link(dve.tensor_tensor_scan(cum[:, ks], cst[0:S, C_MASK + e0 * KB:C_MASK + e1 * KB],
                                            bank[5][0:S, P + e0 * KB:P + e1 * KB], 0.0, ALU.mult, ALU.add))
                link(dve.tensor_tensor(pos[:, ks], bank[5][0:S, ks], cum[:, ks], ALU.add))
                return dve.scalar_tensor_tensor(kept[:, e0:e1, :].rearrange(flat), pos[:, ks], float(CAP),
                                                hot[:, e0:e1, :].rearrange(flat), ALU.is_lt, ALU.mult)

            flat = "p e k -> p (e k)"
            dve.wait_ge(pe_count, 1)
            link(rows_of(0, 1))
            link(dve.scalar_tensor_tensor(own1[:, :], pos[:, 0:KB], 1.0, kept[:, 0, :], ALU.add, ALU.mult))
            link(dve.scalar_tensor_tensor(row0[:, :], own1[:, 0:B], -1.0, own1[:, B:2 * B], ALU.add, ALU.add))
            for b in range(B):
                dve.tensor_scalar(hot0[0:S, b, :], cst[0:S, C_ROW:C_ROW + CAP], row0[:, b:b + 1], None,
                                  ALU.is_equal).then_inc(hot0_ready, 1)
            rows_of(1, E)
            link(dve.tensor_tensor(posk[:, :, :].rearrange(flat), pos[:, :], hot[:, :, :].rearrange(flat), ALU.mult))
            link(dve.tensor_reduce(own[:, :], posk[:, :, :].rearrange("p e k -> p k e"), AX.X, ALU.add))
            dve.tensor_tensor(tokq[:, 1, :], cst[0:S, C_TOKL:C_TOKL + KB], own[:, :], ALU.subtract)
            link(dve.tensor_scalar(ishi[:, :], own[:, :], float(HR), None, ALU.is_ge))
            link(dve.scalar_tensor_tensor(low[:, :], ishi[:, :], -float(HR), own[:, :], ALU.mult, ALU.add))
            link(dve.tensor_tensor(hoth[:, :, 1, :], kept[:, :, :], ishi[:, :].unsqueeze(1).to_broadcast([S, E, KB]),
                                   ALU.mult))
            dve.tensor_tensor(hoth[:, :, 0, :], kept[:, :, :], hoth[:, :, 1, :],
                              ALU.subtract).then_inc(hoth_ready, 1)
            xe_low(0)
            dve.wait_ge(hoth_ready, 1)
            dve.wait_ge(rows_b_ready, 1)
            dve.tensor_tensor(hotl[:, :, :], low[:, :].unsqueeze(1).to_broadcast([S, HR, KB]), rows_b[:, :, :],
                              ALU.is_equal)
            dve.wait_ge(gate_parts, 1)
            map_rhs(dve, 0, NQ - GQ).then_inc(map_ready, 1)
            def hidden_low(e, n):
                fs = slice(4 * n, 4 * n + 4)
                dve.wait_ge(hid_hi_ready, 2 * e + n + 1)
                dve.tensor_tensor(hid_lo[e % 2][:, fs, :], hid[:, fs, :], hid_hi[e % 2][:, fs, :].bitcast(F32),
                                  ALU.subtract).then_inc(hid_lo_ready, 1)

            def y_rows_out(e):
                if e >= 2:
                    dve.wait_ge(put, 32 * (e - 1))
                for j in range(2):
                    h = 2 * e + j
                    yo, g = y_sb[:, e % 2, j, :], slot_gate[:, h:h + 1]
                    link(dve.tensor_scalar(yo, b2_sb[:, e, :], g, None, ALU.mult))
                    dve.wait_ge(pe_y, h + 1)
                    dve.scalar_tensor_tensor(yo, bank[4 + j][0:HR, 0:D], g, yo,
                                             ALU.mult, ALU.add).then_inc(y_ready, 1)

            w_low(1, 4, 3)
            dve.wait_ge(pe_map, 1)
            qcol = [bank[4][0:HR, q * NH:(q + 1) * NH] for q in range(NQ)]
            link(dve.tensor_tensor(slot_tok[:, :], qcol[0], cst[0:HR, C_SPARE:C_SPARE + NH], ALU.add))
            link(dve.tensor_tensor(slot_tok[:, :], qcol[1], slot_tok[:, :], ALU.add))
            dve.tensor_scalar(get_idx[:, :], slot_tok[:, :], float(T - 1), None, ALU.min).then_inc(idx_ready, 1)
            dve.tensor_copy(put_idx[:, :], slot_tok[:, :]).then_inc(idx_ready, 1)
            link(dve.tensor_copy(slot_gate[:, :], qcol[2]))
            link(dve.tensor_tensor(slot_gate[:, :], qcol[3], slot_gate[:, :], ALU.add))
            dve.tensor_tensor(slot_gate[:, :], qcol[4], slot_gate[:, :], ALU.add).then_inc(map_read, 1)
            dve.wait_ge(map_read, 1)
            hidden_low(0, 0)
            w_low(2)
            hidden_low(0, 1)
            xe_low(1)
            w_low(3)
            w_low(4)
            xe_low(2)
            y_rows_out(0)
            hidden_low(1, 0)
            hidden_low(1, 1)
            for e in range(1, E):
                if e + 2 < E:
                    xe_low(e + 2)
                if e + 1 < E:
                    w_low(2 * (e + 1) + 1)
                if e + 2 < E:
                    w_low(2 * (e + 2))
                if e + 1 < E:
                    hidden_low(e + 1, 0)
                    hidden_low(e + 1, 1)
                y_rows_out(e)


def position_features():
    at = np.arange(S, dtype=np.float32)[:, None]
    div = np.exp(np.arange(0, PE_DIM, 2, dtype=np.float32) * np.float32(-np.log(10000.0) / PE_DIM))
    pe = np.zeros((S, PE_DIM), np.float32)
    pe[:, 0::2] = np.sin(at * div)
    pe[:, 1::2] = np.cos(at * div)
    return (pe / np.float32(10) / np.float32(10)).T


def constants():
    c = np.zeros((P, C_ALL), np.float32)
    row = np.arange(P)
    c[:, C_ID:C_ID + P] = np.eye(P)
    c[:, C_LM:C_LM + S] = (row[:, None] < np.arange(S)[None]) - 1.0
    c[:, C_ONE:C_ONE + P] = 1.0
    c[:, C_MASK:C_MASK + P] = np.arange(P) % KB != 0
    c[:, C_EXP:C_EXP + P] = np.arange(P) // KB
    token = (np.arange(KB) % B)[None] * S + row[:, None] - T
    c[:, C_TOKH:C_TOKH + KB] = token // 4 * 4
    c[:, C_TOKL:C_TOKL + KB] = token % 4
    c[:, C_ROW:C_ROW + CAP] = np.arange(CAP)
    c[:, C_SPARE:C_SPARE + NH] = T + row[:, None] + HR * (np.arange(NH) % 2)[None]
    return c


def kernel(**inputs):
    import numpy as _np
    import concourse.bacc as _bacc
    from concourse import mybir as _mybir
    from concourse.bass_utils import run_bass_kernel_spmd as _run

    v = {k: _np.asarray(a) for k, a in inputs.items()}

    def blocks(w):
        return w.reshape(-1, P, w.shape[-1]).transpose(1, 0, 2)

    def cols(w):
        return w.reshape(-1, P).T

    cat, f32 = _np.concatenate, _np.float32
    w_x, w_dx = v["L0_attn_W_x"], v["L0_attn_W_dx"]
    ctx = v["ctx_768"]
    rows = _np.zeros((PE_DIM + 2, R_ALL), f32)
    rows[:, R_PE:R_PE + S] = cat([position_features(), _np.ones((2, S), f32)])
    rows[:PE_DIM, R_WX:R_WX + D] = w_x[D:]
    rows[PE_DIM, R_WX:R_WX + D] = v["L0_attn_b_x"]
    rows[:PE_DIM, R_WDX:R_WDX + D] = w_dx[D:]
    rows[PE_DIM, R_WDX:R_WDX + D] = v["L0_attn_b_dx"]
    rows[PE_DIM + 1, R_WDX:R_WDX + D] = v["L0_attn_b_o"]
    rows[0, R_BO:R_BO + D] = v["L0_xattn_bo"]
    y_turned = _np.zeros((2 * P, B, CE), f32)
    y_turned[:DC, :, :C] = ctx.transpose(2, 0, 1)
    y_turned[DC] = 1.0
    y_rows = _np.zeros((B, CP, DC), f32)
    y_rows[:, :C] = ctx
    arrays = {
        "x": v["x"].transpose(1, 0, 2),
        "consts": constants(),
        "vectors": cat([cols(v[n]) for n in ("L0_attn_a_logit", "L0_attn_b_gx", "L0_attn_b_ga", "L0_xattn_bq",
                                             "L0_xattn_bv", "L0_ffn_b1")], 1),
        "rows": rows,
        "w_lru": _np.stack([blocks(w) for w in (w_x[:D], w_dx[:D], v["L0_attn_W_gx"], v["L0_attn_W_ga"],
                                                v["L0_attn_W_o"])], 1),
        "w_att": cat([blocks(v["L0_xattn_Wq"].T), blocks(v["L0_xattn_Wk"].T), blocks(v["L0_xattn_bk"][:, None]),
                      blocks(v["L0_xattn_Wv"].T), blocks(v["L0_xattn_Wo"])], 2),
        "y_turned": y_turned.reshape(2, P, B * CE).transpose(1, 0, 2),
        "y_rows": y_rows.reshape(B * NC, CR, DC).transpose(1, 0, 2),
        "wg": blocks(v["L0_ffn_Wg"]),
        "bg": v["L0_ffn_bg"][None],
        "w1": v["L0_ffn_W1"].reshape(E, KD, P, F).transpose(0, 2, 1, 3).reshape(E, P, KD * F),
        "w2": v["L0_ffn_W2"].reshape(E, KF, P, D).transpose(0, 2, 1, 3).reshape(E, P, KF * D),
        "b2": v["L0_ffn_b2"],
    }
    arrays = {f"in_{k}_dram": _np.ascontiguousarray(a) for k, a in arrays.items()}
    nc = _bacc.Bacc("TRN2", target_bir_lowering=False, num_devices=1)
    args = [nc.dram_tensor(n, a.shape, _mybir.dt.from_np(a.dtype), kind="ExternalInput").ap()
            for n, a in arrays.items()]
    xn_dram = nc.dram_tensor("xn_dram", (T, D), _mybir.dt.float32, kind="Internal").ap()
    out = nc.dram_tensor("out_0_dram", (OUT_ROWS, D), _mybir.dt.float32, kind="ExternalOutput").ap()
    layer_kernel(nc, *args, xn_dram, out)
    r = _run(nc, [arrays], core_ids=[0])
    return r.results[0]["out_0_dram"][:T].reshape(B, S, D)
```
